# Optimizing a Trainium2 kernel written in Bass

```python
import numpy as np
import jax
import jax.numpy as jnp

def _softmax(x, axis=-1):
    return jax.nn.softmax(x, axis=axis)

def _gelu(x):
    return jax.nn.gelu(x, approximate=True)

def _silu(x):
    return jax.nn.silu(x)

def _sigmoid(x):
    return jax.nn.sigmoid(x)

def _layernorm(x, axis=-1, eps=1e-05):
    m = jnp.mean(x, axis=axis, keepdims=True)
    v = jnp.var(x, axis=axis, keepdims=True)
    return (x - m) / jnp.sqrt(v + eps)

def _scatter_add(tgt, idx, src, axis=0):
    return tgt.at[idx].add(src)

def _segment_sum(src, seg, n):
    return jax.ops.segment_sum(src, seg, n)
kernel_name = 'mk_gnn_preln_d2_gnn_r64_19785d'

def setup_inputs(seed: int=0):
    np.random.seed(seed)
    _w = jnp.asarray

    def _rec_inputs():
        import jax
        import jax.numpy as jnp
        _gk = jax.random.key(seed)
        x = -0.0002117 + 1 * jax.random.normal(jax.random.fold_in(_gk, 1), (50000, 256), jnp.float32)
        src = jax.random.randint(jax.random.fold_in(_gk, 2), (12500,), 0, 50000, jnp.int32)
        dst = jnp.minimum((50000 * jax.random.uniform(jax.random.fold_in(_gk, 3), (12500,)) ** 2.0).astype(jnp.int32), 49999)
        _o = jnp.argsort(dst, stable=True)
        src = src[_o]
        dst = dst[_o]
        edge_attr_256 = -5.16925e-05 + 1.00005 * jax.random.normal(jax.random.fold_in(_gk, 13), (12500, 256), jnp.float32)
        return (x, src, dst, edge_attr_256)
    x, src, dst, edge_attr_256 = _rec_inputs()

    def _L0_gnn_setup():
        import jax, jax.numpy as jnp
        import numpy as np
        N_NODES = 100000
        N_EDGES = 6250
        C = 256
        NUM_GRAPHS = 64
        EPS = 1e-05
        key = jax.random.key(seed)
        ks = jax.random.split(key, 12)
        x = jax.random.normal(ks[0], (N_NODES, C), dtype=jnp.float32)
        edge_index = jax.random.randint(ks[1], (2, N_EDGES), 0, N_NODES, dtype=jnp.int32)
        edge_attr = jax.random.normal(ks[2], (N_EDGES, C), dtype=jnp.float32)
        batch = jnp.sort(jax.random.randint(ks[3], (N_NODES,), 0, NUM_GRAPHS, dtype=jnp.int32))
        s1 = 1.0 / np.sqrt(C)
        s2 = 1.0 / np.sqrt(2 * C)
        W1 = jax.random.normal(ks[4], (C, 2 * C), dtype=jnp.float32) * s1
        b1 = jnp.zeros((2 * C,), dtype=jnp.float32)
        bn_gamma = jnp.ones((2 * C,), dtype=jnp.float32)
        bn_beta = jnp.zeros((2 * C,), dtype=jnp.float32)
        W2 = jax.random.normal(ks[5], (2 * C, C), dtype=jnp.float32) * s2
        b2 = jnp.zeros((C,), dtype=jnp.float32)
        ln_w = jnp.ones((C,), dtype=jnp.float32)
        ln_b = jnp.zeros((C,), dtype=jnp.float32)
        gn_w = jnp.ones((C,), dtype=jnp.float32)
        gn_b = jnp.zeros((C,), dtype=jnp.float32)
        gn_ms = jnp.ones((C,), dtype=jnp.float32)
        return dict(x=x, edge_index=edge_index, edge_attr=edge_attr, batch=batch, W1=W1, b1=b1, bn_gamma=bn_gamma, bn_beta=bn_beta, W2=W2, b2=b2, ln_w=ln_w, ln_b=ln_b, gn_w=gn_w, gn_b=gn_b, gn_ms=gn_ms)
    _L0_gnn_all = _L0_gnn_setup()
    _L0_gnn_in = {k: v for k, v in _L0_gnn_all.items() if k in ('W1', 'b1', 'bn_gamma', 'bn_beta', 'W2', 'b2', 'ln_w', 'ln_b', 'gn_w', 'gn_b', 'gn_ms')}
    del _L0_gnn_all

    def _L1_gnn_setup():
        import jax, jax.numpy as jnp
        import numpy as np
        N_NODES = 10000
        N_EDGES = 5000
        D = 256
        key = jax.random.key(seed)
        k_x, k_w, k_m, k_s, k_d = jax.random.split(key, 5)
        x = jax.random.normal(k_x, (N_NODES, D), dtype=jnp.float32)
        W = jax.random.normal(k_w, (D, D), dtype=jnp.float32)
        M = jax.random.normal(k_m, (D, D), dtype=jnp.float32)
        edge_src = jax.random.randint(k_s, (N_EDGES,), 0, N_NODES, dtype=jnp.int64)
        edge_dst = jax.random.randint(k_d, (N_EDGES,), 0, N_NODES, dtype=jnp.int64)
        return {'x': x, 'W': W, 'M': M, 'edge_src': edge_src, 'edge_dst': edge_dst}
    _L1_gnn_all = _L1_gnn_setup()
    _L1_gnn_in = {k: v for k, v in _L1_gnn_all.items() if k in ('W', 'M')}
    del _L1_gnn_all
    return {'x': x, 'src': src, 'dst': dst, 'edge_attr_256': edge_attr_256, 'L0_gnn_W1': _L0_gnn_in['W1'], 'L0_gnn_b1': _L0_gnn_in['b1'], 'L0_gnn_bn_gamma': _L0_gnn_in['bn_gamma'], 'L0_gnn_bn_beta': _L0_gnn_in['bn_beta'], 'L0_gnn_W2': _L0_gnn_in['W2'], 'L0_gnn_b2': _L0_gnn_in['b2'], 'L0_gnn_ln_w': _L0_gnn_in['ln_w'], 'L0_gnn_ln_b': _L0_gnn_in['ln_b'], 'L0_gnn_gn_w': _L0_gnn_in['gn_w'], 'L0_gnn_gn_b': _L0_gnn_in['gn_b'], 'L0_gnn_gn_ms': _L0_gnn_in['gn_ms'], 'L1_gnn_W': _L1_gnn_in['W'], 'L1_gnn_M': _L1_gnn_in['M']}

def reference(x, src, dst, edge_attr_256, L0_gnn_W1, L0_gnn_b1, L0_gnn_bn_gamma, L0_gnn_bn_beta, L0_gnn_W2, L0_gnn_b2, L0_gnn_ln_w, L0_gnn_ln_b, L0_gnn_gn_w, L0_gnn_gn_b, L0_gnn_gn_ms, L1_gnn_W, L1_gnn_M):
    import jax
    import jax.numpy as jnp

    def _L0_gnn_ref(x, edge_index, edge_attr, batch, W1, b1, bn_gamma, bn_beta, W2, b2, ln_w, ln_b, gn_w, gn_b, gn_ms):
        import jax, jax.numpy as jnp
        import numpy as np
        N_NODES = 100000
        N_EDGES = 6250
        C = 256
        NUM_GRAPHS = 64
        EPS = 1e-05
        src, dst = (edge_index[0], edge_index[1])
        msg = jax.nn.relu(x[src] + edge_attr)
        agg = jnp.zeros_like(x).at[dst].add(msg)
        h = x + agg
        h = h @ W1 + b1
        mu = jnp.mean(h, axis=0)
        var = jnp.mean((h - mu) ** 2, axis=0)
        h = (h - mu) / jnp.sqrt(var + EPS) * bn_gamma + bn_beta
        h = jax.nn.relu(h) @ W2 + b2
        cnt = jax.ops.segment_sum(jnp.ones((h.shape[0],), h.dtype), batch, NUM_GRAPHS)
        denom = jnp.maximum(cnt, 1.0) * C
        mean_g = jax.ops.segment_sum(h.sum(axis=1), batch, NUM_GRAPHS) / denom
        h = h - mean_g[batch][:, None]
        var_g = jax.ops.segment_sum((h * h).sum(axis=1), batch, NUM_GRAPHS) / denom
        h = h * jax.lax.rsqrt(var_g + EPS)[batch][:, None] * ln_w + ln_b
        cnt_c = jnp.maximum(cnt, 1.0)[:, None]
        mean = jax.ops.segment_sum(h, batch, NUM_GRAPHS) / cnt_c
        out = h - mean[batch] * gn_ms
        var2 = jax.ops.segment_sum(out * out, batch, NUM_GRAPHS) / cnt_c
        out = out * jax.lax.rsqrt(var2 + EPS)[batch] * gn_w + gn_b
        out = jax.nn.relu(out)
        return x + out

    def _L1_gnn_ref(x, W, M, edge_src, edge_dst):
        import jax, jax.numpy as jnp
        import numpy as np
        N_NODES = 10000
        N_EDGES = 5000
        D = 256
        self_term = x @ W
        msg = x @ M
        agg = jax.ops.segment_sum(msg[edge_src], edge_dst, num_segments=x.shape[0])
        return jax.nn.relu(self_term + agg)
    edge_index = jnp.stack([src, dst])
    batch0 = jnp.zeros((50000,), jnp.int32)
    h = jnp.maximum(_layernorm(x, axis=-1), 0.0)
    x = x + _L0_gnn_ref(h, edge_index, edge_attr_256, batch0, L0_gnn_W1, L0_gnn_b1, L0_gnn_bn_gamma, L0_gnn_bn_beta, L0_gnn_W2, L0_gnn_b2, L0_gnn_ln_w, L0_gnn_ln_b, L0_gnn_gn_w, L0_gnn_gn_b, L0_gnn_gn_ms)
    h = jnp.maximum(_layernorm(x, axis=-1), 0.0)
    x = x + _L1_gnn_ref(h, L1_gnn_W, L1_gnn_M, src, dst)
    return x

_drawn_inputs = setup_inputs


def setup_inputs(seed=0):
    import zlib

    import numpy as np

    out = dict(_drawn_inputs(seed))
    spreads = {'L0_gnn_b1': (0.0, 2.0),
     'L0_gnn_bn_gamma': (1.0, 0.2),
     'L0_gnn_bn_beta': (0.0, 0.276),
     'L0_gnn_b2': (0.0, 0.573),
     'L0_gnn_ln_w': (1.0, 0.6),
     'L0_gnn_ln_b': (0.0, 0.767),
     'L0_gnn_gn_w': (1.0, 0.2),
     'L0_gnn_gn_b': (0.0, 0.1),
     'L0_gnn_gn_ms': (1.0, 0.2)}
    factors = {}
    for name, (base, spread) in spreads.items():
        noise = np.random.default_rng([zlib.crc32(name.encode()), seed]).standard_normal(out[name].shape)
        drawn = base * np.exp(spread * noise) if base else spread * noise
        out[name] = jnp.asarray(drawn.astype(out[name].dtype))
    for name, factor in factors.items():
        out[name] = (out[name] * factor).astype(out[name].dtype)
    return out
```

```python
import concourse.bass as bass
from concourse import mybir
from contextlib import ExitStack

FP32 = mybir.dt.float32
I32 = mybir.dt.int32
ALU = mybir.AluOpType
ACT = mybir.ActivationFunctionType

NODES, CH, HID, EDGES = 50000, 256, 512, 12500
P = 128
T = 3
TILES = NODES // P
GROUPS = TILES // T
REST = NODES - P * TILES
NG = GROUPS + 1
GC = P * T
KC = CH // P
HC = HID // P
ET = -(-EDGES // P)
EREST = EDGES - P * (ET - 1)
GS, ES = 4, 3
ROUNDS = GROUPS // GS
NO_ROW = 1 << 20
EPS = 1e-5


def is_int(k):
    return isinstance(k, int)


def inside(k, n):
    return not is_int(k) or 0 <= k < n


def after(eng, sem, count):
    if not is_int(count) or count > 0:
        eng.wait_ge(sem, count)


def group_shape(k):
    return (REST, 1) if is_int(k) and k == GROUPS else (P, T)


def group_rows(table, k):
    if is_int(k) and k == GROUPS:
        return table[P * TILES:NODES, :].rearrange("(p t) c -> p t c", t=1)
    return table[0:P * TILES, :].rearrange("(p t) c -> p t c", t=TILES)[:, bass.ds(k * T, T), :]


def back(at, lag, ring):
    k, s, r = at
    return k - lag, (s - lag) % ring, r + (s - lag) // ring


def group_rounds(eng, step, flush):
    def one_round(i):
        for u in range(GS):
            step((i * GS + u, u, i))

    one_round(0)
    with eng.Fori(1, ROUNDS) as i:
        one_round(i)
    for k in range(ROUNDS * GS, NG + flush):
        step((k, k % GS, k // GS))


def mixed_rounds(eng, group, edge, group_flush, edge_flush):
    def one_round(i):
        for u in range(GS):
            group((i * GS + u, u, i))
            if u < ES:
                edge((i * ES + u, u, i))

    for i in range(2):
        one_round(i)
    with eng.Fori(2, ROUNDS) as i:
        one_round(i)
    for k in range(ROUNDS * GS, NG + group_flush):
        group((k, k % GS, k // GS))
    for t in range(ROUNDS * ES, ET + edge_flush):
        edge((t, t % ES, t // ES))


def edge_rounds(eng, edge, flush):
    def one_round(i):
        for u in range(ES):
            edge((i * ES + u, u, i))

    for i in range(2):
        one_round(i)
    with eng.Fori(2, ET // ES) as i:
        one_round(i)
    for t in range(ET // ES * ES, ET + flush):
        edge((t, t % ES, t // ES))


def gnn_kernel(nc, x, src, dst, edge_attr, W1, b1, bn_gamma, bn_beta, W2, b2, ln_w, ln_b,
               gn_w, gn_b, gn_ms, W, M, out):
    agg = nc.dram_tensor("agg", (NODES, CH), FP32, kind="Internal").ap()
    x1_table = nc.dram_tensor("x1_table", (NODES, CH), FP32, kind="Internal").ap()
    yT_table = nc.dram_tensor("yT_table", (NG, P, KC, GC), FP32, kind="Internal").ap()

    with ExitStack() as ctx:
        def sb(name, shape, dt=FP32):
            return ctx.enter_context(nc.sbuf_tensor(name, shape, dt))

        def sem(name):
            return ctx.enter_context(nc.semaphore(name))

        bank = [ctx.enter_context(nc.psum_tensor(f"bank{i}", [P, 512], FP32)) for i in range(2)]
        pair = [ctx.enter_context(nc.psum_tensor(f"pair{i}", [P, 2, 512], FP32)) for i in range(3)]

        ident = sb("ident", [P, P])
        ones = sb("ones", [P, 1])
        mean_of = sb("mean_of", [P, P])
        eps = sb("eps", [P, 1])
        zeros = sb("zeros", [P, 10 * CH])
        W1s = sb("W1s", [P, KC, HID])
        W2s = sb("W2s", [P, HC, CH])
        Ws = sb("Ws", [P, KC, CH])
        Ms = sb("Ms", [P, KC, CH])
        vec_rows = sb("vec_rows", [24, P])
        vec = sb("vec", [P, 24])
        src_rows = sb("src_rows", [ET, P], I32)
        dst_rows = sb("dst_rows", [ET, P], I32)
        next_rows = sb("next_rows", [ET, P], I32)
        rows_f = sb("rows_f", [ET, 3, P])
        src_f = sb("src_f", [P, ET])
        dst_f = sb("dst_f", [P, ET])
        next_f = sb("next_f", [P, ET])
        last_of = sb("last_of", [P, ET])
        carry_key = sb("carry_key", [P, ET])
        key_tmp = sb("key_tmp", [P, ET])
        real_edge = sb("real_edge", [P, ET])
        get_i = sb("get_i", [P, ET, 2], I32)
        get_ring = sb("get_ring", [P, ES, 2], I32)
        put_ring = sb("put_ring", [P, ES, 1], I32)
        put_i = sb("put_i", [P, ET], I32)
        dst_bc = sb("dst_bc", [P, ET * P], I32)
        rstd = sb("rstd", [P, NG * T])
        nmr = sb("nmr", [P, NG * T])
        bufA = sb("bufA", [P, GS, T, CH])
        bufB = sb("bufB", [P, GS, T, CH])
        bufC = sb("bufC", [P, GS, T, CH + 1])
        bufD = sb("bufD", [P, 2, KC, GC])
        bufE = sb("bufE", [P, 4, GC])
        bufF = sb("bufF", [P, 2, KC, GC])
        st6 = sb("st6", [P, GS, T, 6])
        mv = sb("mv", [P, GS, T, 2])
        sd = sb("sd", [P, GS, T])
        e_s = sb("e_s", [P, ES, CH])
        e_d = sb("e_d", [P, ES, CH])
        e_hs = sb("e_hs", [P, ES, CH])
        e_hd = sb("e_hd", [P, ES, CH])
        e_ea = sb("e_ea", [P, ES, CH])
        e_tot = sb("e_tot", [P, ES, CH])
        e_twice = sb("e_twice", [P, ES, CH])
        e_q = sb("e_q", [P, ES, CH])
        e_sel = sb("e_sel", [P, ES, P])
        e_car = sb("e_car", [P, ES, P])
        est6 = sb("est6", [P, ES, 2, 6])
        emv = sb("emv", [P, ES, 2, 2])
        esd = sb("esd", [P, ES, 2])
        er = sb("er", [P, ES, 2])
        enb = sb("enb", [P, ES, 2])
        Dm = sb("Dm", [P, 512])
        sums = sb("sums", [P, 4])
        mh = sb("mh", [P, 2])
        WT = sb("WT", [P, KC, HID])
        small = sb("small", [P, 16, 4])
        bnA = sb("bnA", [P, HC])
        bnC = sb("bnC", [P, HC])
        yst = sb("yst", [P, KC, NG, 6])
        ymv = sb("ymv", [P, KC, 2])
        gnP = sb("gnP", [P, KC])
        gnQ = sb("gnQ", [P, KC])

        b1v, gammav, betav = vec[:, 0:4], vec[:, 4:8], vec[:, 8:12]
        b2v, lnwv, lnbv, gnwv, gnbv, gnmsv = (vec[:, 12 + 2 * i:14 + 2 * i] for i in range(6))

        loaded = sem("loaded")
        consts = sem("consts")
        ident_zero = sem("ident_zero")
        ident_made = sem("ident_made")
        pads = sem("pads")
        rows_float = sem("rows_float")
        turned = sem("turned")
        idx_f = sem("idx_f")
        idx_chain = sem("idx_chain")
        idx_loaded = sem("idx_loaded")
        zeroed = sem("zeroed")

        with nc.Block() as block:
            @block.sync
            def _(sp):
                sp.wait_ge(pads, 1)
                full = P * (ET - 1)
                for tile, table, shift in ((src_rows, src, 0), (dst_rows, dst, 0), (next_rows, dst, 1)):
                    sp.dma_start(tile[0:ET - 1, :],
                                 table[shift:shift + full].rearrange("(t p) -> t p", p=P)).then_inc(idx_loaded, 16)
                    sp.dma_start(tile[ET - 1:ET, 0:EREST - shift],
                                 table[full + shift:EDGES].rearrange("(a p) -> a p", a=1)).then_inc(idx_loaded, 16)
                sp.dma_start(dst_bc[:, 0:EDGES],
                             dst.rearrange("(a n) -> a n", a=1).broadcast_to([P, EDGES])).then_inc(loaded, 16)
                row = 0
                for v, n in ((b1, 4), (bn_gamma, 4), (bn_beta, 4), (b2, 2), (ln_w, 2), (ln_b, 2),
                             (gn_w, 2), (gn_b, 2), (gn_ms, 2)):
                    sp.dma_start(vec_rows[row:row + n, :], v.rearrange("(t p) -> t p", p=P)).then_inc(idx_loaded, 16)
                    row += n
                sp.dma_start(W1s[:], W1.rearrange("(k p) n -> p k n", p=P)).then_inc(loaded, 16)
                sp.dma_start(W2s[:], W2.rearrange("(k p) n -> p k n", p=P)).then_inc(loaded, 16)
                sp.dma_start(Ws[:], W.rearrange("(k p) n -> p k n", p=P)).then_inc(loaded, 16)
                sp.dma_start(Ms[:], M.rearrange("(k p) n -> p k n", p=P)).then_inc(loaded, 16)
                sp.wait_ge(loaded, 16 * 5)

            @block.gpsimd
            def _(pool):
                pool.memset(ident[:], 0.0).then_inc(ident_zero, 1)
                pool.wait_ge(ident_zero, 1)
                pool.affine_select(out=ident[:], in_=ident[:], compare_op=ALU.not_equal, fill=1.0, base=0,
                                   pattern=[[-1, P]], channel_multiplier=1).then_inc(ident_made, 1)

            @block.vector
            def _(dve):
                dve.memset(src_rows[:], 0)
                dve.memset(dst_rows[:], NO_ROW)
                dve.memset(next_rows[:], NO_ROW + 1)
                dve.memset(dst_bc[:, EDGES:], NO_ROW).then_inc(pads, 1)
                dve.memset(ones[:], 1.0)
                dve.memset(mean_of[:], 1.0 / CH)
                dve.memset(eps[:], EPS)
                for s in range(ES):
                    dve.memset(e_ea[:, s, :], 0.0)
                dve.memset(bufC[:, :, :, CH:CH + 1], 1.0)
                dve.memset(zeros[:], 0.0).then_inc(consts, 1)
                dve.wait_ge(idx_loaded, 16 * 15)
                dve.tensor_copy(rows_f[:, 0, :], src_rows[:])
                dve.tensor_copy(rows_f[:, 1, :], dst_rows[:])
                dve.tensor_copy(rows_f[:, 2, :], next_rows[:]).then_inc(rows_float, 1)
                dve.wait_ge(turned, 1)
                dve.tensor_copy(src_f[:], bank[0][:, 0:ET])
                dve.tensor_copy(dst_f[:], bank[0][:, P:P + ET])
                dve.tensor_copy(next_f[:], bank[0][:, 2 * P:2 * P + ET])
                dve.tensor_copy(vec[:], bank[0][:, 3 * P:3 * P + 24]).then_inc(idx_chain, 1)
                dve.wait_ge(idx_chain, 1)
                dve.tensor_copy(get_i[:, :, 0], src_f[:])
                dve.tensor_copy(get_i[:, :, 1], dst_f[:])
                dve.tensor_tensor(last_of[:], dst_f[:], next_f[:], ALU.not_equal).then_inc(idx_chain, 1)
                dve.wait_ge(ident_made, 1)
                dve.memset(carry_key[:, 0:1], -1.0)
                dve.tensor_scalar(carry_key[:, 1:ET], dst_f[:, 0:ET - 1], 1.0, ident[:, P - 1:P],
                                  ALU.add, ALU.mult).then_inc(idx_chain, 1)
                dve.wait_ge(idx_chain, 3)
                dve.tensor_scalar(carry_key[:, 1:ET], carry_key[:, 1:ET], 1.0, None, ALU.subtract)
                dve.tensor_scalar(key_tmp[:], last_of[:], -float(NO_ROW), float(NO_ROW), ALU.mult,
                                  ALU.add).then_inc(idx_chain, 1)
                dve.wait_ge(idx_chain, 4)
                dve.tensor_tensor(key_tmp[:], key_tmp[:], dst_f[:], ALU.add).then_inc(idx_chain, 1)
                dve.wait_ge(idx_chain, 5)
                dve.tensor_copy(put_i[:], key_tmp[:])
                dve.tensor_scalar(real_edge[:], dst_f[:], float(NODES), None, ALU.is_lt).then_inc(idx_chain, 1)
                dve.wait_ge(idx_chain, 6)
                dve.tensor_tensor(last_of[:], last_of[:], real_edge[:], ALU.mult).then_inc(idx_f, 1)

            @block.tensor
            def _(pe):
                pe.wait_ge(ident_made, 1)
                pe.wait_ge(rows_float, 1)
                for j in range(3):
                    pe.transpose(bank[0][:, j * P:j * P + ET], rows_f[:, j, :], ident[0:ET, 0:ET])
                pe.transpose(bank[0][:, 3 * P:3 * P + 24], vec_rows[:], ident[0:24, 0:24]).then_inc(turned, 1)

        x_in = [sem(f"x_in{s}") for s in range(GS)]
        st_done = sem("st_done")
        var_done = sem("var_done")
        sd_done = sem("sd_done")
        rc_done = sem("rc_done")
        nb_done = sem("nb_done")
        h_done = sem("h_done")
        gram_done = sem("gram_done")
        s_in = [sem(f"s_in{s}") for s in range(ES)]
        d_in = [sem(f"d_in{s}") for s in range(ES)]
        ea_in = [sem(f"ea_in{s}") for s in range(ES)]
        put_out = [sem(f"put_out{s}") for s in range(ES)]
        est_done = sem("est_done")
        got_index = sem("got_index")
        put_index = sem("put_index")
        evar_done = sem("evar_done")
        esd_done = sem("esd_done")
        erc_done = sem("erc_done")
        enb_done = sem("enb_done")
        ehn_done = sem("ehn_done")
        eadd_done = sem("eadd_done")
        msg_done = sem("msg_done")
        tot_made = sem("tot_made")
        tot_kept = sem("tot_kept")
        twice_done = sem("twice_done")
        q_done = sem("q_done")
        corr_done = sem("corr_done")
        opened = sem("opened")

        G, B = bank[0], bank[1]
        tot_ps = pair[0][:, 0, 0:CH]

        ZR = 10

        with nc.Block() as block:
            @block.sync
            def _(sp):
                def group(at):
                    k, s, r = at
                    if not inside(k, NG):
                        return
                    p, n = group_shape(k)
                    after(sp, h_done, k - GS + 1)
                    sp.dma_start(bufA[0:p, s, 0:n, :], group_rows(x, k)).then_inc(x_in[s], 16)

                def edge(at):
                    t, s, r = at
                    if not inside(t, ET):
                        return
                    after(sp, msg_done, t - ES + 1)
                    n = EREST if is_int(t) and t == ET - 1 else P
                    rows = edge_attr[bass.ds(t * P, n), :]
                    sp.dma_start(e_ea[0:n, s, :], rows).then_inc(ea_in[s], 16)

                mixed_rounds(sp, group, edge, 0, 0)

            @block.gpsimd
            def _(pool):
                def edge(at):
                    t, s, r = at
                    if inside(t, ET):
                        after(pool, ehn_done, t - ES + 1)
                        pool.nop(nofuse=True)
                        pool.tensor_copy(get_ring[:, s, :], get_i[:, bass.ds(t, 1), :].rearrange("p a b -> p (a b)")
                                         ).then_inc(got_index, 1)
                        pool.wait_ge(got_index, t + 1)
                        pool.nop(nofuse=True)
                        pool.indirect_dma_start(e_s[:, s, :], None, x[:, :],
                                                bass.IndirectOffsetOnAxis(ap=get_ring[:, s, 0:1], axis=0),
                                                bounds_check=NODES - 1, oob_is_err=False).then_inc(s_in[s], 16)
                        pool.indirect_dma_start(e_d[:, s, :], None, x[:, :],
                                                bass.IndirectOffsetOnAxis(ap=get_ring[:, s, 1:2], axis=0),
                                                bounds_check=NODES - 1, oob_is_err=False).then_inc(d_in[s], 16)
                    c, cs, cr = back(at, 3, ES)
                    if inside(c, ET):
                        if is_int(c) and c == 0:
                            pool.wait_ge(zeroed, 16 * (TILES // ZR + 1))
                            pool.nop(nofuse=True)
                        after(pool, put_out[cs], 16 * cr)
                        pool.nop(nofuse=True)
                        pool.tensor_copy(put_ring[:, cs, :], put_i[:, bass.ds(c, 1)]).then_inc(put_index, 1)
                        pool.wait_ge(put_index, c + 1)
                        pool.nop(nofuse=True)
                        pool.wait_ge(tot_kept, c + 1)
                        pool.nop(nofuse=True)
                        pool.indirect_dma_start(agg[:, :],
                                                bass.IndirectOffsetOnAxis(ap=put_ring[:, cs, :], axis=0),
                                                e_tot[:, cs, :], None,
                                                bounds_check=NODES - 1, oob_is_err=False
                                                ).then_inc(put_out[cs], 16)

                edge_rounds(pool, edge, 3)
                for s in range(ES):
                    pool.wait_ge(put_out[s], 16 * (-(-(ET - s) // ES)))
                    pool.nop(nofuse=True)

            @block.scalar
            def _(act):
                for z in range(TILES // ZR):
                    act.dma_start(agg[0:P * TILES, :].rearrange("(p t) c -> p (t c)", t=TILES)
                                  [:, z * ZR * CH:(z + 1) * ZR * CH], zeros[:]).then_inc(zeroed, 16)
                act.dma_start(agg[P * TILES:NODES, :], zeros[0:REST, 0:CH]).then_inc(zeroed, 16)

                def group(at):
                    k, s, r = at
                    if inside(k, NG):
                        p, n = group_shape(k)
                        act.wait_ge(var_done, k + 1)
                        act.activation(sd[0:p, s, 0:n], mv[0:p, s, 0:n, 1], ACT.Sqrt,
                                       bias=eps[0:p, :]).then_inc(sd_done, 1)
                    k, s, r = back(at, 1, GS)
                    if inside(k, NG):
                        p, n = group_shape(k)
                        act.wait_ge(nb_done, k + 1)
                        after(act, gram_done, k - GS + 1)
                        for j in range(n):
                            last = act.activation(bufC[0:p, s, j, 0:CH], bufA[0:p, s, j, :], ACT.Relu,
                                                  bias=nmr[0:p, bass.ds(k * T + j, 1)],
                                                  scale=rstd[0:p, bass.ds(k * T + j, 1)])
                        last.then_inc(h_done, 1)

                def edge(at):
                    t, s, r = at
                    if inside(t, ET):
                        act.wait_ge(evar_done, t + 1)
                        act.activation(esd[:, s, :], emv[:, s, :, 1], ACT.Sqrt,
                                       bias=eps[:]).then_inc(esd_done, 1)
                    c, cs, cr = back(at, 1, ES)
                    if inside(c, ET):
                        act.wait_ge(enb_done, c + 1)
                        after(act, q_done, c - ES + 1)
                        act.activation(e_hs[:, cs, :], e_s[:, cs, :], ACT.Relu,
                                       bias=enb[:, cs, 0:1], scale=er[:, cs, 0:1])
                        act.activation(e_hd[:, cs, :], e_d[:, cs, :], ACT.Relu,
                                       bias=enb[:, cs, 1:2], scale=er[:, cs, 1:2]).then_inc(ehn_done, 1)
                    c, cs, cr = back(at, 3, ES)
                    if inside(c, ET):
                        act.wait_ge(tot_made, c + 1)
                        after(act, q_done, c - ES + 1)
                        if not is_int(c) or c >= ES:
                            act.wait_ge(put_out[cs], 16 * cr)
                        act.activation(e_tot[:, cs, :], tot_ps, ACT.Copy).then_inc(tot_kept, 1)

                mixed_rounds(act, group, edge, 1, 3)

            @block.vector
            def _(dve):
                def group(at):
                    k, s, r = at
                    if inside(k, NG):
                        p, n = group_shape(k)
                        dve.wait_ge(x_in[s], 16 * (r + 1))
                        after(dve, sd_done, k - GS + 1)
                        for j in range(n):
                            last = dve.bn_stats(st6[0:p, s, j, :], bufA[0:p, s, j, :])
                        last.then_inc(st_done, 1)
                        dve.wait_ge(st_done, k + 1)
                        dve.nop(nofuse=True)
                        for j in range(n):
                            last = dve.bn_aggr(mv[0:p, s, j, :], st6[0:p, s, j, :])
                        last.then_inc(var_done, 1)
                    k, s, r = back(at, 1, GS)
                    if inside(k, NG):
                        p, n = group_shape(k)
                        dve.wait_ge(sd_done, k + 1)
                        dve.reciprocal(rstd[0:p, bass.ds(k * T, n)], sd[0:p, s, 0:n]).then_inc(rc_done, 1)
                        dve.wait_ge(rc_done, k + 1)
                        dve.scalar_tensor_tensor(out=nmr[0:p, bass.ds(k * T, n)], in0=mv[0:p, s, 0:n, 0],
                                                 scalar=-1.0, in1=rstd[0:p, bass.ds(k * T, n)],
                                                 op0=ALU.mult, op1=ALU.mult).then_inc(nb_done, 1)

                def edge(at):
                    t, s, r = at
                    if inside(t, ET):
                        dve.wait_ge(s_in[s], 16 * (r + 1))
                        dve.wait_ge(d_in[s], 16 * (r + 1))
                        dve.bn_stats(est6[:, s, 0, :], e_s[:, s, :])
                        dve.bn_stats(est6[:, s, 1, :], e_d[:, s, :]).then_inc(est_done, 1)
                        dve.wait_ge(est_done, t + 1)
                        dve.nop(nofuse=True)
                        dve.bn_aggr(emv[:, s, 0, :], est6[:, s, 0, :])
                        dve.bn_aggr(emv[:, s, 1, :], est6[:, s, 1, :]).then_inc(evar_done, 1)
                    c, cs, cr = back(at, 1, ES)
                    if inside(c, ET):
                        dve.wait_ge(esd_done, c + 1)
                        dve.reciprocal(er[:, cs, :], esd[:, cs, :]).then_inc(erc_done, 1)
                        dve.wait_ge(erc_done, c + 1)
                        dve.scalar_tensor_tensor(out=enb[:, cs, :], in0=emv[:, cs, :, 0], scalar=-1.0,
                                                 in1=er[:, cs, :], op0=ALU.mult,
                                                 op1=ALU.mult).then_inc(enb_done, 1)
                    c, cs, cr = back(at, 2, ES)
                    if inside(c, ET):
                        dve.wait_ge(ehn_done, c + 1)
                        dve.wait_ge(ea_in[cs], 16 * (cr + 1))
                        dve.tensor_tensor(e_hs[:, cs, :], e_hs[:, cs, :], e_ea[:, cs, :],
                                          ALU.add).then_inc(eadd_done, 1)
                        after(dve, tot_made, c - ES + 1)
                        cols = dst_bc[:, bass.ds(c * P, P)]
                        dve.tensor_scalar(e_sel[:, cs, :], cols, dst_f[:, bass.ds(c, 1)], None, ALU.is_equal)
                        dve.tensor_scalar(e_car[:, cs, :], cols, carry_key[:, bass.ds(c, 1)], None, ALU.is_equal)
                        dve.wait_ge(eadd_done, c + 1)
                        dve.tensor_scalar(e_hs[:, cs, :], e_hs[:, cs, :], 0.0, None,
                                          ALU.max).then_inc(msg_done, 1)
                    c, cs, cr = back(at, 3, ES)
                    if inside(c, ET):
                        dve.wait_ge(tot_kept, c + 1)
                        after(dve, corr_done, c - ES + 1)
                        dve.tensor_scalar(e_twice[:, cs, :], e_tot[:, cs, :], last_of[:, bass.ds(c, 1)], 2.0,
                                          ALU.mult, ALU.mult).then_inc(twice_done, 1)
                        dve.wait_ge(twice_done, c + 1)
                        dve.scalar_tensor_tensor(out=e_q[:, cs, :], in0=e_twice[:, cs, :], scalar=0.25,
                                                 in1=e_hd[:, cs, :], op0=ALU.mult,
                                                 op1=ALU.add).then_inc(q_done, 1)

                mixed_rounds(dve, group, edge, 1, 3)

            @block.tensor
            def _(pe):
                pe.matmul(G[:, :], zeros[:, 0:P], zeros[:, 0:512], start=True, stop=False, skip_group_check=True)
                pe.matmul(B[:, :], zeros[:, 0:P], zeros[:, 0:512], start=True, stop=False, skip_group_check=True)

                def add(o, a, b):
                    return pe.matmul(o, a, b, start=False, stop=False, skip_group_check=True)

                def group(at):
                    k, s, r = at
                    if not inside(k, NG):
                        return
                    p, n = group_shape(k)
                    pe.wait_ge(h_done, k + 1)
                    for j in range(n):
                        h = bufC[0:p, s, j, :]
                        add(G[:, 0:CH + 1], h[:, 0:P], h)
                        last = add(G[:, CH + 1:CH + 2 + P], h[:, P:CH], h[:, P:CH + 1])
                    last.then_inc(gram_done, 1)

                def edge(at):
                    t, s, r = at
                    c, cs, cr = back(at, 2, ES)
                    if inside(c, ET):
                        pe.wait_ge(msg_done, c + 1)
                        after(pe, tot_kept, c)
                        first = is_int(c) and c == 0
                        if first:
                            pe.matmul(tot_ps, e_sel[:, cs, :], e_hs[:, cs, :], start=True,
                                      stop=True).then_inc(tot_made, 1)
                        else:
                            pe.matmul(tot_ps, e_sel[:, cs, :], e_hs[:, cs, :], start=True, stop=False)
                            pe.matmul(tot_ps, e_car[96:P, cs, :], e_tot[96:P, (cs - 1) % ES, :],
                                      start=False, stop=True).then_inc(tot_made, 1)
                    c, cs, cr = back(at, 3, ES)
                    if inside(c, ET):
                        pe.wait_ge(q_done, c + 1)
                        a = e_twice[:, cs, :]
                        add(B[:, 0:CH], e_q[:, cs, 0:P], a)
                        add(B[:, CH:2 * CH], e_q[:, cs, P:CH], a)
                        add(G[:, CH + 2 + P:CH + 3 + P], a[:, 0:P], ones[:])
                        add(G[:, CH + 3 + P:CH + 4 + P], a[:, P:CH], ones[:]).then_inc(corr_done, 1)

                mixed_rounds(pe, group, edge, 0, 3)
                pe.matmul(G[:, :], zeros[:, 0:P], zeros[:, 0:512], start=False, stop=True, skip_group_check=True)
                pe.matmul(B[:, :], zeros[:, 0:P], zeros[:, 0:512], start=False, stop=True, skip_group_check=True)

        c0 = sem("c0")
        d_copied = sem("d_copied")
        d_made = sem("d_made")
        t_made = sem("t_made")
        wt_made = sem("wt_made")
        q_made = sem("q_made")
        var_made = sem("var_made")
        sdev_made = sem("sdev_made")
        N = float(NODES)
        with nc.Block() as block:
            @block.scalar
            def _(act):
                act.activation(Dm[:], B[:, :], ACT.Copy, scale=1.0 / N)
                act.activation(sums[:, 0:1], G[:, CH:CH + 1], ACT.Copy, scale=1.0 / N)
                act.activation(sums[:, 1:4], G[:, CH + 1 + P:CH + 4 + P], ACT.Copy,
                               scale=1.0 / N).then_inc(d_copied, 1)
                act.wait_ge(var_made, 1)
                act.activation(small[:, 4, :], small[:, 3, :], ACT.Sqrt, bias=eps[:]).then_inc(sdev_made, 1)

            @block.vector
            def _(dve):
                count = [0]

                def link(ins):
                    count[0] += 1
                    ins.then_inc(c0, 1)
                    dve.wait_ge(c0, count[0])

                dve.wait_ge(d_copied, 1)
                for o, g, f in ((0, 0, 1.0), (P, P, 2.0), (3 * P, CH + 1, 1.0)):
                    dve.scalar_tensor_tensor(out=Dm[:, o:o + P], in0=G[:, g:g + P], scalar=f / N,
                                             in1=Dm[:, o:o + P], op0=ALU.mult, op1=ALU.add)
                for j in range(2):
                    last = dve.scalar_tensor_tensor(out=mh[:, j:j + 1], in0=sums[:, 2 + j:3 + j], scalar=0.5,
                                                    in1=sums[:, j:j + 1], op0=ALU.mult, op1=ALU.add)
                last.then_inc(d_made, 1)
                dve.wait_ge(t_made, 1)
                for j in range(KC):
                    last = dve.tensor_tensor(WT[:, j, :], W1s[:, j, :], pair[0][:, j, :], ALU.mult)
                last.then_inc(wt_made, 1)
                dve.wait_ge(q_made, 1)
                link(dve.tensor_copy(small[:, 0:2, :], pair[1][:, 0, 0:8].rearrange("p (a b) -> p a b", a=2)))
                zq, zm = small[:, 0, :], small[:, 1, :]
                link(dve.tensor_tensor(small[:, 2, :], zm, zm, ALU.mult))
                link(dve.tensor_tensor(small[:, 2, :], zq, small[:, 2, :], ALU.subtract))
                dve.tensor_scalar(small[:, 3, :], small[:, 2, :], 0.0, None, ALU.max).then_inc(var_made, 1)
                link(dve.tensor_tensor(small[:, 5, :], zm, b1v, ALU.add))
                link(dve.tensor_tensor(small[:, 5, :], b1v, small[:, 5, :], ALU.subtract))
                dve.wait_ge(sdev_made, 1)
                link(dve.reciprocal(small[:, 6, :], small[:, 4, :]))
                link(dve.tensor_tensor(bnA[:], small[:, 6, :], gammav, ALU.mult))
                link(dve.tensor_tensor(small[:, 7, :], bnA[:], small[:, 5, :], ALU.mult))
                link(dve.tensor_tensor(bnC[:], small[:, 7, :], betav, ALU.add))

            @block.tensor
            def _(pe):
                pe.wait_ge(d_made, 1)
                for o in range(KC):
                    for l in range(KC):
                        last = pe.matmul(pair[0][:, o, :], Dm[:, l * CH + o * P:l * CH + o * P + P],
                                         W1s[:, l, :], start=l == 0, stop=l == KC - 1)
                last.then_inc(t_made, 1)
                pe.wait_ge(wt_made, 1)
                for m in range(HC):
                    for l in range(KC):
                        pe.matmul(pair[1][:, 0, m:m + 1], WT[:, l, m * P:m * P + P], ones[:],
                                  start=l == 0, stop=l == KC - 1)
                for m in range(HC):
                    for l in range(KC):
                        last = pe.matmul(pair[1][:, 0, 4 + m:5 + m], W1s[:, l, m * P:m * P + P], mh[:, l:l + 1],
                                         start=l == 0, stop=l == KC - 1)
                last.then_inc(q_made, 1)

        x2_in = [sem(f"x2_in{s}") for s in range(GS)]
        a2_in = [sem(f"a2_in{s}") for s in range(GS)]
        y_out = [sem(f"y_out{s}") for s in range(2)]
        h2n_done = sem("h2n_done")
        h2_done = sem("h2_done")
        t2_made = sem("t2_made")
        t2_kept = sem("t2_kept")
        z_made = sem("z_made")
        r_kept = sem("r_kept")
        y_made = sem("y_made")
        y_kept = sem("y_kept")
        yst_done = sem("yst_done")
        hT_ps, z_ps, y_ps = pair[0], [pair[1][:, 0, :], pair[1][:, 1, :], pair[2][:, 0, :], pair[2][:, 1, :]], bank

        def cols_of(k):
            p, n = group_shape(k)
            return p * n

        with nc.Block() as block:
            @block.sync
            def _(sp):
                def load(at):
                    k, s, r = at
                    if not inside(k, NG):
                        return
                    p, n = group_shape(k)
                    after(sp, h2n_done, k - GS + 1)
                    sp.dma_start(bufA[0:p, s, 0:n, :], group_rows(x, k)).then_inc(x2_in[s], 16)
                    after(sp, h2_done, k - GS + 1)
                    sp.dma_start(bufB[0:p, s, 0:n, :], group_rows(agg, k)).then_inc(a2_in[s], 16)

                group_rounds(sp, load, 0)

            @block.gpsimd
            def _(pool):
                def store(at):
                    k, s, r = at
                    if not inside(k, NG):
                        return
                    n = cols_of(k)
                    s = s % 2
                    pool.wait_ge(y_kept, k + 1)
                    pool.nop(nofuse=True)
                    where = yT_table[k] if is_int(k) else yT_table[bass.ds(k, 1)].rearrange("a p c n -> (a p) c n")
                    pool.dma_start(where[:, :, 0:n], bufF[:, s, :, 0:n]).then_inc(y_out[s], 16)

                group_rounds(pool, store, 0)
                for s in range(2):
                    pool.wait_ge(y_out[s], 16 * (-(-(NG - s) // 2)))
                    pool.nop(nofuse=True)

            @block.scalar
            def _(act):
                def norm(at):
                    k, s, r = at
                    if not inside(k, NG):
                        return
                    p, n = group_shape(k)
                    act.wait_ge(x2_in[s], 16 * (r + 1))
                    after(act, t2_made, k - GS + 1)
                    for j in range(n):
                        last = act.activation(bufC[0:p, s, j, 0:CH], bufA[0:p, s, j, :], ACT.Relu,
                                              bias=nmr[0:p, bass.ds(k * T + j, 1)],
                                              scale=rstd[0:p, bass.ds(k * T + j, 1)])
                    last.then_inc(h2n_done, 1)

                def hidden(at):
                    k, s, r = at
                    if not inside(k, NG):
                        return
                    n = cols_of(k)
                    after(act, y_made, k)
                    for m in range(HC):
                        act.wait_ge(z_made, k * HC + m + 1)
                        act.activation(bufE[:, m, 0:n], z_ps[m][:, 0:n], ACT.Relu, bias=bnC[:, m:m + 1],
                                       scale=bnA[:, m:m + 1]).then_inc(r_kept, 1)

                def keep_y(at):
                    k, s, r = at
                    if not inside(k, NG):
                        return
                    n = cols_of(k)
                    f = s % 2
                    act.wait_ge(y_made, k + 1)
                    after(act, yst_done, k - 1)
                    after(act, y_out[f], 16 * (GS // 2 * r + s // 2))
                    for c in range(KC):
                        last = act.activation(bufF[:, f, c, 0:n], y_ps[c][:, 0:n], ACT.Identity,
                                              bias=b2v[:, c:c + 1])
                    last.then_inc(y_kept, 1)

                def step(at):
                    k, s, r = at
                    keep_y(back(at, 1, GS))
                    hidden(at)
                    norm(back(at, -2, GS))

                norm((0, 0, 0))
                norm((1, 1, 0))
                group_rounds(act, step, 1)

            @block.vector
            def _(dve):
                def add(at):
                    k, s, r = at
                    if not inside(k, NG):
                        return
                    p, n = group_shape(k)
                    dve.wait_ge(h2n_done, k + 1)
                    dve.wait_ge(a2_in[s], 16 * (r + 1))
                    dve.tensor_tensor(bufC[0:p, s, 0:n, 0:CH], bufC[0:p, s, 0:n, 0:CH], bufB[0:p, s, 0:n, :],
                                      ALU.add).then_inc(h2_done, 1)

                def keep_T(at):
                    k, s, r = at
                    if not inside(k, NG):
                        return
                    n = cols_of(k)
                    dve.wait_ge(t2_made, k + 1)
                    after(dve, z_made, (k - 1) * HC)
                    for c in range(KC):
                        last = dve.tensor_copy(bufD[:, s % 2, c, 0:n], hT_ps[:, c, 0:n])
                    last.then_inc(t2_kept, 1)

                def stats(at):
                    k, s, r = at
                    if not inside(k, NG):
                        return
                    n = cols_of(k)
                    dve.wait_ge(y_kept, k + 1)
                    for c in range(KC):
                        last = dve.bn_stats(yst[:, c, bass.ds(k, 1), :].rearrange("p a b -> p (a b)"),
                                            bufF[:, s % 2, c, 0:n])
                    last.then_inc(yst_done, 1)

                def step(at):
                    k, s, r = at
                    stats(back(at, 1, GS))
                    add(back(at, -2, GS))
                    keep_T(back(at, -1, GS))

                add((0, 0, 0))
                add((1, 1, 0))
                keep_T((0, 0, 0))
                group_rounds(dve, step, 1)

            @block.tensor
            def _(pe):
                def turn(at):
                    k, s, r = at
                    if not inside(k, NG):
                        return
                    p, n = group_shape(k)
                    pe.wait_ge(h2_done, k + 1)
                    after(pe, t2_kept, k)
                    for c in range(KC):
                        for j in range(n):
                            last = pe.transpose(hT_ps[:, c, j * P:j * P + p],
                                                bufC[0:p, s, j, c * P:(c + 1) * P], ident[0:p, 0:p])
                    last.then_inc(t2_made, 1)

                def step(at):
                    k, s, r = at
                    if not inside(k, NG):
                        return
                    n = cols_of(k)
                    pe.wait_ge(t2_kept, k + 1)
                    for m in range(HC):
                        after(pe, r_kept, (k - 1) * HC + m + 1)
                        for c in range(KC):
                            last = pe.matmul(z_ps[m][:, 0:n], W1s[:, c, m * P:(m + 1) * P],
                                             bufD[:, s % 2, c, 0:n], start=c == 0, stop=c == KC - 1)
                        last.then_inc(z_made, 1)
                    turn(back(at, -1, GS))
                    after(pe, y_kept, k)
                    for ms in (range(HC - 1), (HC - 1,)):
                        pe.wait_ge(r_kept, k * HC + ms[-1] + 1)
                        for c in range(KC):
                            for m in ms:
                                last = pe.matmul(y_ps[c][:, 0:n], W2s[:, m, c * P:(c + 1) * P],
                                                 bufE[:, m, 0:n], start=m == 0, stop=m == HC - 1)
                    last.then_inc(y_made, 1)

                turn((0, 0, 0))
                group_rounds(pe, step, 0)

        c1 = sem("c1")
        mu_in = sem("mu_in")
        mu_made = sem("mu_made")
        vg_in = sem("vg_in")
        vg_made = sem("vg_made")
        v1_made = sem("v1_made")
        s1_made = sem("s1_made")
        v2_made = sem("v2_made")
        s2_made = sem("s2_made")
        with nc.Block() as block:
            mu, vg = pair[0][:, 0, 0:1], pair[0][:, 1, 0:1]
            row = [small[:, i, 0:2] for i in range(16)]

            @block.vector
            def _(dve):
                count = [0]

                def link(ins):
                    count[0] += 1
                    ins.then_inc(c1, 1)
                    dve.wait_ge(c1, count[0])

                for c in range(KC):
                    last = dve.bn_aggr(ymv[:, c, :], yst[:, c, :, :].rearrange("p a b -> p (a b)"))
                last.then_inc(mu_in, 1)
                dve.wait_ge(mu_in, 1)
                E, V = ymv[:, :, 0], ymv[:, :, 1]
                dve.wait_ge(mu_made, 1)
                link(dve.tensor_copy(row[15], mu.broadcast_to([P, 2])))
                link(dve.tensor_tensor(row[0], E, row[15], ALU.subtract))
                link(dve.tensor_tensor(row[1], row[0], row[0], ALU.mult))
                dve.tensor_tensor(row[2], row[1], V, ALU.add).then_inc(vg_in, 1)
                dve.wait_ge(vg_made, 1)
                dve.tensor_copy(row[3], vg.broadcast_to([P, 2])).then_inc(v1_made, 1)
                dve.wait_ge(s1_made, 1)
                link(dve.reciprocal(row[5], row[4]))
                link(dve.tensor_tensor(row[5], row[5], lnwv, ALU.mult))
                link(dve.tensor_tensor(row[6], row[0], row[5], ALU.mult))
                link(dve.tensor_tensor(row[6], row[6], lnbv, ALU.add))
                link(dve.tensor_tensor(row[7], row[6], gnmsv, ALU.mult))
                link(dve.tensor_tensor(row[8], row[6], row[7], ALU.subtract))
                link(dve.tensor_tensor(row[8], row[8], row[8], ALU.mult))
                link(dve.tensor_tensor(row[9], row[5], row[5], ALU.mult))
                link(dve.tensor_tensor(row[9], row[9], V, ALU.mult))
                dve.tensor_tensor(row[9], row[9], row[8], ALU.add).then_inc(v2_made, 1)
                link(dve.tensor_tensor(row[11], row[15], row[5], ALU.mult))
                link(dve.tensor_tensor(row[11], lnbv, row[11], ALU.subtract))
                link(dve.tensor_tensor(row[11], row[11], row[7], ALU.subtract))
                dve.wait_ge(s2_made, 1)
                link(dve.reciprocal(row[12], row[10]))
                link(dve.tensor_tensor(row[12], row[12], gnwv, ALU.mult))
                link(dve.tensor_tensor(gnP[:], row[5], row[12], ALU.mult))
                link(dve.tensor_tensor(row[11], row[11], row[12], ALU.mult))
                link(dve.tensor_tensor(gnQ[:], row[11], gnbv, ALU.add))

            @block.scalar
            def _(act):
                act.wait_ge(v1_made, 1)
                act.activation(row[4], row[3], ACT.Sqrt, bias=eps[:]).then_inc(s1_made, 1)
                act.wait_ge(v2_made, 1)
                act.activation(row[10], row[9], ACT.Sqrt, bias=eps[:]).then_inc(s2_made, 1)

            @block.tensor
            def _(pe):
                pe.wait_ge(mu_in, 1)
                for c in range(KC):
                    last = pe.matmul(mu, mean_of[:], ymv[:, c, 0:1], start=c == 0, stop=c == KC - 1)
                last.then_inc(mu_made, 1)
                pe.wait_ge(vg_in, 1)
                for c in range(KC):
                    last = pe.matmul(vg, mean_of[:], row[2][:, c:c + 1], start=c == 0, stop=c == KC - 1)
                last.then_inc(vg_made, 1)

        x3_in = [sem(f"x3_in{s}") for s in range(GS)]
        y3_in = [sem(f"y3_in{s}") for s in range(GS)]
        x1_out = [sem(f"x1_out{s}") for s in range(2)]
        o_out = [sem(f"o_out{s}") for s in range(2)]
        h3_done = sem("h3_done")
        g_done = sem("g_done")
        xh_done = sem("xh_done")
        gt_made = sem("gt_made")
        x1_done = sem("x1_done")
        st3_done = sem("st3_done")
        var3_done = sem("var3_done")
        sd3_done = sem("sd3_done")
        rc3_done = sem("rc3_done")
        nb3_done = sem("nb3_done")
        h1_done = sem("h1_done")
        h1t_made = sem("h1t_made")
        h1t_kept = sem("h1t_kept")
        u_made = sem("u_made")
        o_done = sem("o_done")
        r3 = sb("r3", [P, GS, T])
        n3 = sb("n3", [P, GS, T])
        x1b = sb("x1b", [P, 2, T, CH])
        ob = sb("ob", [P, 2, T, CH])
        h1b = sb("h1b", [P, 2, T, CH])

        def bankpair(i, j):
            return pair[i][:, j // 2, (j % 2) * CH:(j % 2 + 1) * CH]

        def flat(i, p, n):
            return pair[i][:, :, :].rearrange("p a b -> p (a b)")[0:p, 0:n * CH]

        with nc.Block() as block:
            @block.sync
            def _(sp):
                def load(at):
                    k, s, r = at
                    if not inside(k, NG):
                        return
                    p, n = group_shape(k)
                    after(sp, xh_done, k - GS + 1)
                    sp.dma_start(bufA[0:p, s, 0:n, :], group_rows(x, k)).then_inc(x3_in[s], 16)
                    c = cols_of(k)
                    after(sp, g_done, k - GS + 1)
                    where = yT_table[k] if is_int(k) else yT_table[bass.ds(k, 1)].rearrange("a p c n -> (a p) c n")
                    yb = bufB[:, s, :, :].rearrange("p a b -> p (a b)").rearrange("p (c n) -> p c n", c=KC)
                    sp.dma_start(yb[:, :, 0:c], where[:, :, 0:c]).then_inc(y3_in[s], 16)

                group_rounds(sp, load, 0)

            @block.gpsimd
            def _(pool):
                def store(at):
                    k, s, r = at
                    if not inside(k, NG):
                        return
                    p, n = group_shape(k)
                    s = s % 2
                    pool.wait_ge(x1_done, k + 1)
                    pool.nop(nofuse=True)
                    pool.dma_start(group_rows(x1_table, k), x1b[0:p, s, 0:n, :]).then_inc(x1_out[s], 16)
                    pool.wait_ge(o_done, k + 1)
                    pool.nop(nofuse=True)
                    pool.dma_start(group_rows(out, k), ob[0:p, s, 0:n, :]).then_inc(o_out[s], 16)

                group_rounds(pool, store, 0)
                for s in range(2):
                    pool.wait_ge(x1_out[s], 16 * (-(-(NG - s) // 2)))
                    pool.nop(nofuse=True)
                    pool.wait_ge(o_out[s], 16 * (-(-(NG - s) // 2)))
                    pool.nop(nofuse=True)

            @block.scalar
            def _(act):
                def first(at):
                    k, s, r = at
                    if not inside(k, NG):
                        return
                    p, n = group_shape(k)
                    act.wait_ge(x3_in[s], 16 * (r + 1))
                    after(act, xh_done, k - GS + 1)
                    for j in range(n):
                        last = act.activation(bufC[0:p, s, j, 0:CH], bufA[0:p, s, j, :], ACT.Relu,
                                              bias=nmr[0:p, bass.ds(k * T + j, 1)],
                                              scale=rstd[0:p, bass.ds(k * T + j, 1)])
                    last.then_inc(h3_done, 1)
                    m = cols_of(k)
                    act.wait_ge(y3_in[s], 16 * (r + 1))
                    after(act, gt_made, k - 1)
                    yb = bufB[:, s, :, :].rearrange("p a b -> p (a b)").rearrange("p (c n) -> p c n", c=KC)
                    for c in range(KC):
                        last = act.activation(bufF[:, s % 2, c, 0:m], yb[:, c, 0:m], ACT.Relu,
                                              bias=gnQ[:, c:c + 1], scale=gnP[:, c:c + 1])
                    last.then_inc(g_done, 1)

                def root(at):
                    k, s, r = at
                    if not inside(k, NG):
                        return
                    p, n = group_shape(k)
                    act.wait_ge(var3_done, k + 1)
                    act.activation(sd[0:p, s, 0:n], mv[0:p, s, 0:n, 1], ACT.Sqrt,
                                   bias=eps[0:p, :]).then_inc(sd3_done, 1)

                def second(at):
                    k, s, r = at
                    if not inside(k, NG):
                        return
                    p, n = group_shape(k)
                    act.wait_ge(nb3_done, k + 1)
                    after(act, h1t_made, k - 1)
                    for j in range(n):
                        last = act.activation(h1b[0:p, s % 2, j, :], x1b[0:p, s % 2, j, :], ACT.Relu,
                                              bias=n3[0:p, s, j:j + 1], scale=r3[0:p, s, j:j + 1])
                    last.then_inc(h1_done, 1)

                def keep_T(at):
                    k, s, r = at
                    if not inside(k, NG):
                        return
                    n = cols_of(k)
                    act.wait_ge(h1t_made, k + 1)
                    after(act, u_made, k - 1)
                    for c in range(KC):
                        last = act.activation(bufD[:, s % 2, c, 0:n], pair[1][:, c, 0:n], ACT.Copy)
                    last.then_inc(h1t_kept, 1)

                def step(at):
                    k, s, r = at
                    root(at)
                    first(back(at, -1, GS))
                    second(at)
                    keep_T(back(at, 1, GS))

                first((0, 0, 0))
                group_rounds(act, step, 1)

            @block.vector
            def _(dve):
                def begin(at):
                    k, s, r = at
                    if not inside(k, NG):
                        return
                    p, n = group_shape(k)
                    dve.wait_ge(h3_done, k + 1)
                    dve.tensor_tensor(bufC[0:p, s, 0:n, 0:CH], bufC[0:p, s, 0:n, 0:CH], bufA[0:p, s, 0:n, :],
                                      ALU.add).then_inc(xh_done, 1)

                def middle(at):
                    k, s, r = at
                    if not inside(k, NG):
                        return
                    p, n = group_shape(k)
                    dve.wait_ge(xh_done, k + 1)
                    dve.wait_ge(gt_made, k + 1)
                    after(dve, x1_out[s % 2], 16 * (GS // 2 * r + s // 2))
                    after(dve, h1_done, k - 1)
                    after(dve, o_done, k - 1)
                    dve.tensor_tensor(x1b[0:p, s % 2, 0:n, :], bufC[0:p, s, 0:n, 0:CH],
                                      flat(0, p, n).rearrange("p (a b) -> p a b", a=n),
                                      ALU.add).then_inc(x1_done, 1)
                    dve.wait_ge(x1_done, k + 1)
                    for j in range(n):
                        last = dve.bn_stats(st6[0:p, s, j, :], x1b[0:p, s % 2, j, :])
                    last.then_inc(st3_done, 1)
                    dve.wait_ge(st3_done, k + 1)
                    dve.nop(nofuse=True)
                    for j in range(n):
                        last = dve.bn_aggr(mv[0:p, s, j, :], st6[0:p, s, j, :])
                    last.then_inc(var3_done, 1)

                def factors(at):
                    k, s, r = at
                    if not inside(k, NG):
                        return
                    p, n = group_shape(k)
                    dve.wait_ge(sd3_done, k + 1)
                    dve.reciprocal(r3[0:p, s, 0:n], sd[0:p, s, 0:n]).then_inc(rc3_done, 1)
                    dve.wait_ge(rc3_done, k + 1)
                    dve.scalar_tensor_tensor(out=n3[0:p, s, 0:n], in0=mv[0:p, s, 0:n, 0], scalar=-1.0,
                                             in1=r3[0:p, s, 0:n], op0=ALU.mult,
                                             op1=ALU.mult).then_inc(nb3_done, 1)

                def finish(at):
                    k, s, r = at
                    if not inside(k, NG):
                        return
                    p, n = group_shape(k)
                    dve.wait_ge(u_made, k + 1)
                    after(dve, o_out[s % 2], 16 * (GS // 2 * r + s // 2))
                    dve.scalar_tensor_tensor(out=ob[0:p, s % 2, 0:n, :].rearrange("p a b -> p (a b)"),
                                             in0=flat(2, p, n), scalar=0.0,
                                             in1=x1b[0:p, s % 2, 0:n, :].rearrange("p a b -> p (a b)"),
                                             op0=ALU.max, op1=ALU.add).then_inc(o_done, 1)

                def step(at):
                    k, s, r = at
                    middle(at)
                    begin(back(at, -1, GS))
                    factors(at)
                    finish(back(at, 1, GS))

                begin((0, 0, 0))
                group_rounds(dve, step, 1)

            @block.tensor
            def _(pe):
                def turn_g(at):
                    k, s, r = at
                    if not inside(k, NG):
                        return
                    p, n = group_shape(k)
                    pe.wait_ge(g_done, k + 1)
                    after(pe, x1_done, k)
                    for j in range(n):
                        for c in range(KC):
                            last = pe.transpose(bankpair(0, j)[0:p, c * P:(c + 1) * P],
                                                bufF[:, s % 2, c, j * P:j * P + p], ident[:])
                    last.then_inc(gt_made, 1)

                def turn_h(at):
                    k, s, r = at
                    if not inside(k, NG):
                        return
                    p, n = group_shape(k)
                    pe.wait_ge(h1_done, k + 1)
                    after(pe, h1t_kept, k)
                    for c in range(KC):
                        for j in range(n):
                            last = pe.transpose(pair[1][:, c, j * P:j * P + p],
                                                h1b[0:p, s % 2, j, c * P:(c + 1) * P], ident[0:p, 0:p])
                    last.then_inc(h1t_made, 1)

                def product(at):
                    k, s, r = at
                    if not inside(k, NG):
                        return
                    p, n = group_shape(k)
                    pe.wait_ge(h1t_kept, k + 1)
                    after(pe, o_done, k)
                    for j in range(n):
                        for c in range(KC):
                            last = pe.matmul(bankpair(2, j)[0:p, :], bufD[:, s % 2, c, j * P:j * P + p],
                                             Ws[:, c, :], start=c == 0, stop=c == KC - 1)
                    last.then_inc(u_made, 1)

                def step(at):
                    k, s, r = at
                    turn_g(back(at, -1, GS))
                    turn_h(at)
                    product(back(at, 1, GS))

                turn_g((0, 0, 0))
                group_rounds(pe, step, 1)

        s4_in = [sem(f"s4_in{s}") for s in range(ES)]
        d4_in = [sem(f"d4_in{s}") for s in range(ES)]
        o4_out = [sem(f"o4_out{s}") for s in range(ES)]
        st4_done = sem("st4_done")
        got4_index = sem("got4_index")
        put4_index = sem("put4_index")
        var4_done = sem("var4_done")
        sd4_done = sem("sd4_done")
        rc4_done = sem("rc4_done")
        nb4_done = sem("nb4_done")
        hn4_done = sem("hn4_done")
        sel4_done = sem("sel4_done")
        tot4_made = sem("tot4_made")
        tot4_kept = sem("tot4_kept")
        tt4_made = sem("tt4_made")
        tt4_kept = sem("tt4_kept")
        u4_made = sem("u4_made")
        o4_done = sem("o4_done")
        e_hT = bufE
        sum_ps, turn_ps, u_ps = bank[0][:, 0:CH], bank[1], pair[0][:, 0, 0:CH]
        with nc.Block() as block:
            @block.gpsimd
            def _(pool):
                def edge(at):
                    t, s, r = at
                    if inside(t, ET):
                        after(pool, hn4_done, t - ES + 1)
                        pool.nop(nofuse=True)
                        after(pool, o4_done, t - ES + 1)
                        pool.nop(nofuse=True)
                        pool.tensor_copy(get_ring[:, s, :], get_i[:, bass.ds(t, 1), :].rearrange("p a b -> p (a b)")
                                         ).then_inc(got4_index, 1)
                        pool.wait_ge(got4_index, t + 1)
                        pool.nop(nofuse=True)
                        pool.indirect_dma_start(e_s[:, s, :], None, x1_table[:, :],
                                                bass.IndirectOffsetOnAxis(ap=get_ring[:, s, 0:1], axis=0),
                                                bounds_check=NODES - 1, oob_is_err=False).then_inc(s4_in[s], 16)
                        pool.indirect_dma_start(e_d[:, s, :], None, x1_table[:, :],
                                                bass.IndirectOffsetOnAxis(ap=get_ring[:, s, 1:2], axis=0),
                                                bounds_check=NODES - 1, oob_is_err=False).then_inc(d4_in[s], 16)
                    c, cs, cr = back(at, 2, ES)
                    if inside(c, ET):
                        after(pool, o4_out[cs], 16 * cr)
                        pool.nop(nofuse=True)
                        pool.tensor_copy(put_ring[:, cs, :], put_i[:, bass.ds(c, 1)]).then_inc(put4_index, 1)
                        pool.wait_ge(put4_index, c + 1)
                        pool.nop(nofuse=True)
                        pool.wait_ge(o4_done, c + 1)
                        pool.nop(nofuse=True)
                        pool.indirect_dma_start(out[:, :],
                                                bass.IndirectOffsetOnAxis(ap=put_ring[:, cs, :], axis=0),
                                                e_q[:, cs, :], None, bounds_check=NODES - 1,
                                                oob_is_err=False).then_inc(o4_out[cs], 16)

                edge_rounds(pool, edge, 2)
                for s in range(ES):
                    pool.wait_ge(o4_out[s], 16 * (-(-(ET - s) // ES)))
                    pool.nop(nofuse=True)

            @block.scalar
            def _(act):
                def edge(at):
                    t, s, r = at
                    if inside(t, ET):
                        act.wait_ge(var4_done, t + 1)
                        act.activation(esd[:, s, :], emv[:, s, :, 1], ACT.Sqrt, bias=eps[:]).then_inc(sd4_done, 1)
                        act.wait_ge(nb4_done, t + 1)
                        after(act, tt4_made, t - ES + 1)
                        act.activation(e_hs[:, s, :], e_s[:, s, :], ACT.Relu,
                                       bias=enb[:, s, 0:1], scale=er[:, s, 0:1])
                        act.activation(e_hd[:, s, :], e_d[:, s, :], ACT.Relu,
                                       bias=enb[:, s, 1:2], scale=er[:, s, 1:2]).then_inc(hn4_done, 1)
                    c, cs, cr = back(at, 1, ES)
                    if inside(c, ET):
                        act.wait_ge(tot4_made, c + 1)
                        after(act, tt4_made, c - ES + 1)
                        act.activation(e_tot[:, cs, :], sum_ps, ACT.Copy).then_inc(tot4_kept, 1)
                        act.wait_ge(tt4_made, c + 1)
                        after(act, u4_made, c)
                        act.activation(e_hT[:, :, 0:P], turn_ps[:, :].rearrange("p (a b) -> p a b", a=4),
                                       ACT.Copy).then_inc(tt4_kept, 1)

                edge_rounds(act, edge, 1)

            @block.vector
            def _(dve):
                def edge(at):
                    t, s, r = at
                    if inside(t, ET):
                        dve.wait_ge(s4_in[s], 16 * (r + 1))
                        dve.wait_ge(d4_in[s], 16 * (r + 1))
                        dve.bn_stats(est6[:, s, 0, :], e_s[:, s, :])
                        dve.bn_stats(est6[:, s, 1, :], e_d[:, s, :]).then_inc(st4_done, 1)
                        dve.wait_ge(st4_done, t + 1)
                        dve.nop(nofuse=True)
                        dve.bn_aggr(emv[:, s, 0, :], est6[:, s, 0, :])
                        dve.bn_aggr(emv[:, s, 1, :], est6[:, s, 1, :]).then_inc(var4_done, 1)
                        after(dve, tot4_made, t - ES + 1)
                        cols = dst_bc[:, bass.ds(t * P, P)]
                        dve.tensor_scalar(e_sel[:, s, :], cols, dst_f[:, bass.ds(t, 1)], None, ALU.is_equal)
                        dve.tensor_scalar(e_car[:, s, :], cols, carry_key[:, bass.ds(t, 1)], None,
                                          ALU.is_equal).then_inc(sel4_done, 1)
                        dve.wait_ge(sd4_done, t + 1)
                        after(dve, hn4_done, t - ES + 1)
                        dve.reciprocal(er[:, s, :], esd[:, s, :]).then_inc(rc4_done, 1)
                        dve.wait_ge(rc4_done, t + 1)
                        dve.scalar_tensor_tensor(out=enb[:, s, :], in0=emv[:, s, :, 0], scalar=-1.0,
                                                 in1=er[:, s, :], op0=ALU.mult,
                                                 op1=ALU.mult).then_inc(nb4_done, 1)
                    c, cs, cr = back(at, 2, ES)
                    if inside(c, ET):
                        dve.wait_ge(u4_made, c + 1)
                        after(dve, o4_out[cs], 16 * cr)
                        dve.scalar_tensor_tensor(out=e_q[:, cs, :], in0=u_ps, scalar=0.0, in1=e_d[:, cs, :],
                                                 op0=ALU.max, op1=ALU.add).then_inc(o4_done, 1)

                edge_rounds(dve, edge, 2)

            @block.tensor
            def _(pe):
                def edge(at):
                    t, s, r = at
                    if inside(t, ET):
                        pe.wait_ge(hn4_done, t + 1)
                        pe.wait_ge(sel4_done, t + 1)
                        after(pe, tot4_kept, t)
                        first = is_int(t) and t == 0
                        last = pe.matmul(sum_ps, e_sel[:, s, :], e_hs[:, s, :], start=True, stop=first)
                        if not first:
                            last = pe.matmul(sum_ps, e_car[96:P, s, :], e_tot[96:P, (s - 1) % ES, :],
                                             start=False, stop=True)
                        last.then_inc(tot4_made, 1)
                        pe.wait_ge(tot4_kept, t + 1)
                        after(pe, tt4_kept, t)
                        for c in range(KC):
                            pe.transpose(turn_ps[:, c * P:(c + 1) * P], e_hd[:, s, c * P:(c + 1) * P], ident[:])
                        for c in range(KC):
                            last = pe.transpose(turn_ps[:, (2 + c) * P:(3 + c) * P],
                                                e_tot[:, s, c * P:(c + 1) * P], ident[:])
                        last.then_inc(tt4_made, 1)
                    c = t - 1
                    if inside(c, ET):
                        pe.wait_ge(tt4_kept, c + 1)
                        after(pe, o4_done, c)
                        for j, w in enumerate((Ws[:, 0, :], Ws[:, 1, :], Ms[:, 0, :], Ms[:, 1, :])):
                            last = pe.matmul(u_ps, e_hT[:, j, 0:P], w, start=j == 0, stop=j == 3)
                        last.then_inc(u4_made, 1)

                edge_rounds(pe, edge, 1)


_INS = ['x', 'src', 'dst', 'edge_attr_256', 'L0_gnn_W1', 'L0_gnn_b1', 'L0_gnn_bn_gamma', 'L0_gnn_bn_beta',
        'L0_gnn_W2', 'L0_gnn_b2', 'L0_gnn_ln_w', 'L0_gnn_ln_b', 'L0_gnn_gn_w', 'L0_gnn_gn_b', 'L0_gnn_gn_ms',
        'L1_gnn_W', 'L1_gnn_M']


def kernel(**inputs):
    import numpy as _np
    import concourse.bacc as _bacc
    from concourse import mybir as _mybir
    from concourse.bass_utils import run_bass_kernel_spmd as _run

    nc = _bacc.Bacc("TRN2", target_bir_lowering=False, num_devices=1)
    arrays, args = {}, []
    for name in _INS:
        a = _np.ascontiguousarray(inputs[name])
        arrays[f"in_{name}"] = a
        args.append(nc.dram_tensor(f"in_{name}", a.shape, _mybir.dt.from_np(a.dtype), kind="ExternalInput").ap())
    out = nc.dram_tensor("out", (NODES, CH), _mybir.dt.float32, kind="ExternalOutput").ap()
    gnn_kernel(nc, *args, out)
    r = _run(nc, [arrays], core_ids=[0])
    return r.results[0]["out"]
```

```python
import concourse.bass as bass
from concourse import mybir
from contextlib import ExitStack

FP32 = mybir.dt.float32
FP32R = mybir.dt.float32r
I32 = mybir.dt.int32
ALU = mybir.AluOpType
ACT = mybir.ActivationFunctionType

NODES, CH, HID, EDGES = 50000, 256, 512, 12500
P = 128
T = 3
TILES = NODES // P
GROUPS = TILES // T
REST = NODES - P * TILES
NG = GROUPS + 1
GC = P * T
KC = CH // P
HC = HID // P
ET = -(-EDGES // P)
EREST = EDGES - P * (ET - 1)
NO_ROW = 1 << 20
EPS = 1e-5



def back(at, lag):
    k, u, r, n = at
    return k - lag, (u - lag) % n, r + (u - lag) // n, n


def ring(at, size):
    k, u, r, n = at
    assert n % size == 0
    return u % size, r * (n // size) + u // size


def is_int(k):
    return isinstance(k, int)


def inside(at, n):
    return not is_int(at[0]) or 0 <= at[0] < n


def after(eng, sem, count):
    if not is_int(count) or count > 0:
        eng.wait_ge(sem, count)


def group_shape(k):
    return (REST, 1) if is_int(k) and k == GROUPS else (P, T)


def columns(k):
    p, n = group_shape(k)
    return p * n


def group_rows(table, k):
    if is_int(k) and k == GROUPS:
        return table[P * TILES:NODES, :].rearrange("(p t) c -> p t c", t=1)
    return table[0:P * TILES, :].rearrange("(p t) c -> p t c", t=TILES)[:, bass.ds(k * T, T), :]


def group_block(table, k):
    return table[k] if is_int(k) else table[bass.ds(k, 1)].rearrange("a p c n -> (a p) c n")


def rounds(eng, step, steps, unroll, peel, flush):
    def one_round(i):
        for u in range(unroll):
            step((i * unroll + u, u, i, unroll))

    full = steps // unroll
    for i in range(peel):
        one_round(i)
    with eng.Fori(peel, full) as i:
        one_round(i)
    for k in range(full * unroll, steps + flush):
        step((k, k % unroll, k // unroll, unroll))


GU, EU = 8, 6


def mixed_rounds(eng, group, edge, group_flush, edge_flush):
    def one_round(i):
        for u in range(GU):
            group((i * GU + u, u, i, GU))
            if u % 4 < 3:
                e = u // 4 * 3 + u % 4
                edge((i * EU + e, e, i, EU))

    full = NG // GU
    for i in range(2):
        one_round(i)
    with eng.Fori(2, full) as i:
        one_round(i)
    left = [("g", k) for k in range(full * GU, NG + group_flush)]
    tiles = [("e", t) for t in range(full * EU, ET + edge_flush)]
    for j in range(max(len(left), len(tiles))):
        for kind, k in left[j:j + 1] + tiles[j:j + 1]:
            if kind == "g":
                group((k, k % GU, k // GU, GU))
            else:
                edge((k, k % EU, k // EU, EU))


def gnn_kernel(nc, x, src, dst, edge_attr, W1, b1, bn_gamma, bn_beta, W2, b2, ln_w, ln_b,
               gn_w, gn_b, gn_ms, W, M, out):
    sum_table = nc.dram_tensor("sum_table", (ET * P, CH), FP32, kind="Internal").ap()
    id_table = nc.dram_tensor("id_table", (NODES, 1), I32, kind="Internal").ap()
    xh_table = nc.dram_tensor("xh_table", (NODES, CH), FP32, kind="Internal").ap()
    x1_table = nc.dram_tensor("x1_table", (NODES, CH), FP32, kind="Internal").ap()
    yT_table = nc.dram_tensor("yT_table", (NG, P, KC, GC), FP32, kind="Internal").ap()

    with ExitStack() as ctx:
        def sb(name, shape, dt=FP32, scope=ctx):
            return scope.enter_context(nc.sbuf_tensor(name, shape, dt))

        phase = []

        def sem(name):
            phase.append(nc.alloc_semaphore(name))
            return phase[-1]

        def next_phase():
            nc.clear_and_free_semaphores(phase)
            nc.all_engine_barrier()
            phase.clear()

        bank = [ctx.enter_context(nc.psum_tensor(f"bank{i}", [P, 512], FP32)) for i in range(2)]
        pair = [ctx.enter_context(nc.psum_tensor(f"pair{i}", [P, 2, 512], FP32)) for i in range(3)]

        ident = sb("ident", [P, P])
        ones = sb("ones", [P, 1])
        mean_of = sb("mean_of", [P, P])
        eps = sb("eps", [P, 1])
        zeros = sb("zeros", [P, 512])
        no_rows = sb("no_rows", [P, TILES], I32)
        W1s = sb("W1s", [P, KC, HID])
        W2s = sb("W2s", [P, HC, CH])
        W1h = sb("W1h", [P, KC, HID], FP32R)
        W1l = sb("W1l", [P, KC, HID], FP32R)
        W2h = sb("W2h", [P, HC, CH], FP32R)
        W2l = sb("W2l", [P, HC, CH], FP32R)
        Ws = sb("Ws", [P, KC, CH])
        Ms = sb("Ms", [P, KC, CH])
        vec_rows = sb("vec_rows", [24, P])
        vec = sb("vec", [P, 24])
        src_rows = sb("src_rows", [ET, P], I32)
        dst_rows = sb("dst_rows", [ET, P], I32)
        next_rows = sb("next_rows", [ET, P], I32)
        rows_f = sb("rows_f", [ET, 3, P])
        src_f = sb("src_f", [P, ET])
        dst_f = sb("dst_f", [P, ET])
        next_f = sb("next_f", [P, ET])
        last_of = sb("last_of", [P, ET])
        twice_last = sb("twice_last", [P, ET])
        carry_key = sb("carry_key", [P, ET])
        key_tmp = sb("key_tmp", [P, ET])
        real_edge = sb("real_edge", [P, ET])
        prev_last = sb("prev_last", [P, ET])
        edge_id = sb("edge_id", [P, ET], I32)
        index = sb("index", [P, ET, 4], I32)
        rstd = sb("rstd", [P, NG * T])
        nmr = sb("nmr", [P, NG * T])
        Dm = sb("Dm", [P, 512])
        sums = sb("sums", [P, 4])
        mh = sb("mh", [P, 2])
        WT = sb("WT", [P, KC, HID])
        small = sb("small", [P, 16, 4])
        bnA = sb("bnA", [P, HC])
        bnC = sb("bnC", [P, HC])
        yst = sb("yst", [P, KC, NG, 6])
        ymv = sb("ymv", [P, KC, 2])
        gnP = sb("gnP", [P, KC])
        gnQ = sb("gnQ", [P, KC])

        b1v, gammav, betav = vec[:, 0:4], vec[:, 4:8], vec[:, 8:12]
        b2v, lnwv, lnbv, gnwv, gnbv, gnmsv = (vec[:, 12 + 2 * i:14 + 2 * i] for i in range(6))

        def dst_columns(t):
            n = EREST if is_int(t) and t == ET - 1 else P
            return dst[bass.ds(t * P, n)].rearrange("(a n) -> a n", a=1).broadcast_to([P, n]), n

        loaded = sem("loaded")
        consts = sem("consts")
        pool_consts = sem("pool_consts")
        ident_zero = sem("ident_zero")
        ident_made = sem("ident_made")
        pads = sem("pads")
        ids_clear = sem("ids_clear")
        rows_float = sem("rows_float")
        turned = sem("turned")
        prev_made = sem("prev_made")
        idx_chain = sem("idx_chain")
        idx_loaded = sem("idx_loaded")
        split_done = sem("split_done")

        with nc.Block() as block:
            @block.sync
            def _(sp):
                sp.wait_ge(pads, 1)
                full = P * (ET - 1)
                for tile, table, shift in ((src_rows, src, 0), (dst_rows, dst, 0), (next_rows, dst, 1)):
                    sp.dma_start(tile[0:ET - 1, :],
                                 table[shift:shift + full].rearrange("(t p) -> t p", p=P)).then_inc(idx_loaded, 16)
                    sp.dma_start(tile[ET - 1:ET, 0:EREST - shift],
                                 table[full + shift:EDGES].rearrange("(a p) -> a p", a=1)).then_inc(idx_loaded, 16)
                sp.dma_start(id_table[0:P * TILES, :].rearrange("(p t) a -> p (t a)", t=TILES),
                             no_rows[:]).then_inc(ids_clear, 16)
                sp.dma_start(id_table[P * TILES:NODES, :], no_rows[0:REST, 0:1]).then_inc(ids_clear, 16)
                sp.wait_ge(ids_clear, 32)

            @block.scalar
            def _(act):
                row = 0
                for v, n in ((b1, 4), (bn_gamma, 4), (bn_beta, 4), (b2, 2), (ln_w, 2), (ln_b, 2),
                             (gn_w, 2), (gn_b, 2), (gn_ms, 2)):
                    act.dma_start(vec_rows[row:row + n, :], v.rearrange("(t p) -> t p", p=P)).then_inc(idx_loaded, 16)
                    row += n
                act.dma_start(W1s[:], W1.rearrange("(k p) n -> p k n", p=P)).then_inc(loaded, 16)
                act.dma_start(W2s[:], W2.rearrange("(k p) n -> p k n", p=P)).then_inc(loaded, 16)
                act.dma_start(Ws[:], W.rearrange("(k p) n -> p k n", p=P)).then_inc(loaded, 16)
                act.dma_start(Ms[:], M.rearrange("(k p) n -> p k n", p=P)).then_inc(loaded, 16)

            @block.gpsimd
            def _(pool):
                pool.memset(ident[:], 0.0).then_inc(ident_zero, 1)
                pool.wait_ge(ident_zero, 1)
                pool.affine_select(out=ident[:], in_=ident[:], compare_op=ALU.not_equal, fill=1.0, base=0,
                                   pattern=[[-1, P]], channel_multiplier=1).then_inc(ident_made, 1)
                pool.iota(edge_id[:], [[P, ET]], base=0, channel_multiplier=1).then_inc(pool_consts, 1)

            @block.vector
            def _(dve):
                dve.memset(src_rows[:], 0)
                dve.memset(dst_rows[:], NO_ROW)
                dve.memset(next_rows[:], NO_ROW + 1)
                dve.memset(no_rows[:], NO_ROW).then_inc(pads, 1)
                dve.memset(ones[:], 1.0)
                dve.memset(mean_of[:], 1.0 / CH)
                dve.memset(eps[:], EPS)
                dve.memset(zeros[:], 0.0).then_inc(consts, 1)
                dve.wait_ge(idx_loaded, 16 * 15)
                dve.tensor_copy(rows_f[:, 0, :], src_rows[:])
                dve.tensor_copy(rows_f[:, 1, :], dst_rows[:])
                dve.tensor_copy(rows_f[:, 2, :], next_rows[:]).then_inc(rows_float, 1)
                dve.wait_ge(turned, 1)
                dve.tensor_copy(src_f[:], bank[0][:, 0:ET])
                dve.tensor_copy(dst_f[:], bank[0][:, P:P + ET])
                dve.tensor_copy(next_f[:], bank[0][:, 2 * P:2 * P + ET])
                dve.tensor_copy(vec[:], bank[0][:, 3 * P:3 * P + 24])
                dve.memset(prev_last[:, 0:1], -1.0)
                dve.tensor_copy(prev_last[:, 1:ET], bank[1][:, 0:ET - 1]).then_inc(idx_chain, 1)
                dve.wait_ge(idx_chain, 1)
                dve.tensor_copy(index[:, :, 0], src_f[:])
                dve.tensor_copy(index[:, :, 1], dst_f[:])
                dve.tensor_tensor(last_of[:], dst_f[:], next_f[:], ALU.not_equal).then_inc(idx_chain, 1)
                dve.wait_ge(ident_made, 1)
                dve.memset(carry_key[:, 0:1], -1.0)
                dve.tensor_scalar(carry_key[:, 1:ET], dst_f[:, 0:ET - 1], 1.0, ident[:, P - 1:P],
                                  ALU.add, ALU.mult).then_inc(idx_chain, 1)
                dve.wait_ge(idx_chain, 3)
                dve.tensor_scalar(carry_key[:, 1:ET], carry_key[:, 1:ET], 1.0, None, ALU.subtract)
                dve.tensor_scalar(key_tmp[:], last_of[:], -float(NO_ROW), float(NO_ROW), ALU.mult,
                                  ALU.add).then_inc(idx_chain, 1)
                dve.wait_ge(idx_chain, 4)
                dve.tensor_tensor(key_tmp[:], key_tmp[:], dst_f[:], ALU.add).then_inc(idx_chain, 1)
                dve.wait_ge(idx_chain, 5)
                dve.tensor_copy(index[:, :, 2], key_tmp[:])
                dve.wait_ge(pool_consts, 1)
                dve.tensor_copy(index[:, :, 3], edge_id[:])
                dve.tensor_scalar(real_edge[:], dst_f[:], float(NODES), 2.0, ALU.is_lt, ALU.mult).then_inc(idx_chain, 1)
                dve.wait_ge(idx_chain, 6)
                dve.tensor_tensor(twice_last[:], last_of[:], real_edge[:], ALU.mult)
                dve.wait_ge(loaded, 16 * 4)
                dve.tensor_copy(W1h[:], W1s[:])
                dve.tensor_copy(W2h[:], W2s[:]).then_inc(split_done, 1)
                dve.wait_ge(split_done, 1)
                dve.tensor_tensor(W1l[:], W1s[:], W1h[:].bitcast(FP32), ALU.subtract)
                dve.tensor_tensor(W2l[:], W2s[:], W2h[:].bitcast(FP32), ALU.subtract)

            @block.tensor
            def _(pe):
                pe.wait_ge(ident_made, 1)
                pe.wait_ge(rows_float, 1)
                for j in range(3):
                    pe.transpose(bank[0][:, j * P:j * P + ET], rows_f[:, j, :], ident[0:ET, 0:ET])
                pe.transpose(bank[0][:, 3 * P:3 * P + 24], vec_rows[:], ident[0:24, 0:24])
                pe.matmul(bank[1][:, 0:ET], rows_f[:, 1, P - 1:P].broadcast_to([ET, P]), ident[0:ET, 0:ET],
                          start=True, stop=True).then_inc(turned, 1)

        next_phase()
        x_in = [sem(f"x_in{s}") for s in range(GU)]
        st_done = sem("st_done")
        var_done = sem("var_done")
        sd_done = sem("sd_done")
        rc_done = sem("rc_done")
        nb_done = sem("nb_done")
        h_done = sem("h_done")
        gram_done = sem("gram_done")
        s_in = [sem(f"s_in{s}") for s in range(EU)]
        d_in = [sem(f"d_in{s}") for s in range(EU)]
        ea_in = [sem(f"ea_in{s}") for s in range(EU)]
        bc_in = [sem(f"bc_in{s}") for s in range(EU)]
        id_out = [sem(f"id_out{s}") for s in range(EU)]
        sum_out = [sem(f"sum_out{s}") for s in range(EU)]
        got_index = sem("got_index")
        est_done = sem("est_done")
        evar_done = sem("evar_done")
        esd_done = sem("esd_done")
        erc_done = sem("erc_done")
        enb_done = sem("enb_done")
        ehn_done = sem("ehn_done")
        eadd_done = sem("eadd_done")
        esel_done = sem("esel_done")
        msg_done = sem("msg_done")
        tot_made = sem("tot_made")
        tot_kept = sem("tot_kept")
        q_done = sem("q_done")
        corr_done = sem("corr_done")
        ring_clear = sem("ring_clear")

        G, B = bank[0], bank[1]
        tot_ps = pair[0][:, 0, 0:CH]
        GH = 4

        with ExitStack() as scope, nc.Block() as block:
            xr = sb("xr", [P, GU, T, CH], scope=scope)
            hr = sb("hr", [P, GH, T, CH + 1], scope=scope)
            st6 = sb("st6", [P, GU, T, 6], scope=scope)
            mv = sb("mv", [P, GU, T, 2], scope=scope)
            sd = sb("sd", [P, GU, T], scope=scope)
            e_s = sb("e_s", [P, EU, CH], scope=scope)
            e_d = sb("e_d", [P, EU, CH], scope=scope)
            e_hs = sb("e_hs", [P, EU, CH], scope=scope)
            e_hd = sb("e_hd", [P, EU, CH], scope=scope)
            e_ea = sb("e_ea", [P, EU, CH], scope=scope)
            e_tot = sb("e_tot", [P, EU, CH], scope=scope)
            e_twice = sb("e_twice", [P, EU, CH], scope=scope)
            e_q = sb("e_q", [P, EU, CH], scope=scope)
            e_bc = sb("e_bc", [P, EU, P], I32, scope=scope)
            e_sel = sb("e_sel", [P, EU, P], scope=scope)
            e_car = sb("e_car", [P, EU, P], scope=scope)
            idx = sb("idx", [P, EU, 4], I32, scope=scope)
            est6 = sb("est6", [P, EU, 2, 6], scope=scope)
            emv = sb("emv", [P, EU, 2, 2], scope=scope)
            esd = sb("esd", [P, EU, 2], scope=scope)
            er = sb("er", [P, EU, 2], scope=scope)
            enb = sb("enb", [P, EU, 2], scope=scope)

            @block.sync
            def _(sp):
                sp.wait_ge(ring_clear, 1)

                def group(at):
                    if not inside(at, NG):
                        return
                    k = at[0]
                    s, _ = ring(at, GU)
                    p, n = group_shape(k)
                    after(sp, h_done, k - GU + 1)
                    sp.dma_start(xr[0:p, s, 0:n, :], group_rows(x, k)).then_inc(x_in[s], 16)

                def edge(at):
                    if inside(at, ET):
                        t = at[0]
                        s, _ = ring(at, EU)
                        after(sp, msg_done, t - EU + 1)
                        n = EREST if is_int(t) and t == ET - 1 else P
                        sp.dma_start(e_ea[0:n, s, :], edge_attr[bass.ds(t * P, n), :]).then_inc(ea_in[s], 16)
                        rows, n = dst_columns(t)
                        sp.dma_start(e_bc[:, s, 0:n], rows).then_inc(bc_in[s], 16)
                    at = back(at, 8)
                    if inside(at, ET):
                        t = at[0]
                        s, _ = ring(at, EU)
                        sp.wait_ge(tot_kept, t + 1)
                        sp.dma_start(sum_table[bass.ds(t * P, P), :], e_tot[:, s, :]).then_inc(sum_out[s], 16)

                mixed_rounds(sp, group, edge, 0, 8)
                for s in range(EU):
                    sp.wait_ge(sum_out[s], 16 * (-(-(ET - s) // EU)))

            @block.gpsimd
            def _(pool):
                pool.memset(hr[:, :, :, CH:CH + 1], 1.0)
                pool.memset(e_bc[:, :, :], 0)
                pool.memset(e_ea[:, :, :], 0.0).then_inc(ring_clear, 1)

                def edge(at):
                    t = at[0]
                    s, used = ring(at, EU)
                    after(pool, ehn_done, t - EU + 1)
                    after(pool, id_out[s], 16 * used)
                    pool.nop(nofuse=True)
                    pool.tensor_copy(idx[:, s, :], index[:, bass.ds(t, 1), :].rearrange("p a b -> p (a b)")
                                     ).then_inc(got_index, 1)
                    pool.wait_ge(got_index, t + 1)
                    pool.nop(nofuse=True)
                    pool.indirect_dma_start(e_s[:, s, :], None, x[:, :],
                                            bass.IndirectOffsetOnAxis(ap=idx[:, s, 0:1], axis=0),
                                            bounds_check=NODES - 1, oob_is_err=False).then_inc(s_in[s], 16)
                    pool.indirect_dma_start(e_d[:, s, :], None, x[:, :],
                                            bass.IndirectOffsetOnAxis(ap=idx[:, s, 1:2], axis=0),
                                            bounds_check=NODES - 1, oob_is_err=False).then_inc(d_in[s], 16)
                    pool.indirect_dma_start(id_table[:, :],
                                            bass.IndirectOffsetOnAxis(ap=idx[:, s, 2:3], axis=0),
                                            idx[:, s, 3:4], None,
                                            bounds_check=NODES - 1, oob_is_err=False).then_inc(id_out[s], 16)

                rounds(pool, edge, ET, EU, 2, 0)
                for s in range(EU):
                    pool.wait_ge(id_out[s], 16 * (-(-(ET - s) // EU)))

            @block.scalar
            def _(act):
                def group(at):
                    one = back(at, 1)
                    if inside(one, NG):
                        k = one[0]
                        s, _ = ring(one, GU)
                        p, n = group_shape(k)
                        act.wait_ge(var_done, k + 1)
                        after(act, rc_done, k - GU + 1)
                        act.activation(sd[0:p, s, 0:n], mv[0:p, s, 0:n, 1], ACT.Sqrt,
                                       bias=eps[0:p, :]).then_inc(sd_done, 1)
                    two = back(at, 2)
                    if inside(two, NG):
                        k = two[0]
                        s, _ = ring(two, GU)
                        h, _ = ring(two, GH)
                        p, n = group_shape(k)
                        act.wait_ge(nb_done, k + 1)
                        after(act, gram_done, k - GH + 1)
                        for j in range(n):
                            last = act.activation(hr[0:p, h, j, 0:CH], xr[0:p, s, j, :], ACT.Relu,
                                                  bias=nmr[0:p, bass.ds(k * T + j, 1)],
                                                  scale=rstd[0:p, bass.ds(k * T + j, 1)])
                        last.then_inc(h_done, 1)

                def edge(at):
                    five = back(at, 5)
                    if inside(five, ET):
                        t = five[0]
                        s, used = ring(five, EU)
                        act.wait_ge(tot_made, t + 1)
                        after(act, q_done, t - EU + 1)
                        after(act, corr_done, t - EU + 1)
                        after(act, sum_out[s], 16 * used)
                        act.activation(e_tot[:, s, :], tot_ps, ACT.Copy)
                        act.activation(e_twice[:, s, :], tot_ps, ACT.Copy,
                                       scale=twice_last[:, bass.ds(t, 1)]).then_inc(tot_kept, 1)
                    one = back(at, 1)
                    if inside(one, ET):
                        t = one[0]
                        s, _ = ring(one, EU)
                        act.wait_ge(evar_done, t + 1)
                        after(act, erc_done, t - EU + 1)
                        act.activation(esd[:, s, :], emv[:, s, :, 1], ACT.Sqrt,
                                       bias=eps[:]).then_inc(esd_done, 1)
                    two = back(at, 2)
                    if inside(two, ET):
                        t = two[0]
                        s, _ = ring(two, EU)
                        act.wait_ge(enb_done, t + 1)
                        after(act, tot_made, t - EU + 1)
                        after(act, q_done, t - EU + 1)
                        act.activation(e_hs[:, s, :], e_s[:, s, :], ACT.Relu,
                                       bias=enb[:, s, 0:1], scale=er[:, s, 0:1])
                        act.activation(e_hd[:, s, :], e_d[:, s, :], ACT.Relu,
                                       bias=enb[:, s, 1:2], scale=er[:, s, 1:2]).then_inc(ehn_done, 1)

                mixed_rounds(act, group, edge, 2, 5)

            @block.vector
            def _(dve):
                def group(at):
                    if inside(at, NG):
                        k = at[0]
                        s, used = ring(at, GU)
                        p, n = group_shape(k)
                        dve.wait_ge(x_in[s], 16 * (used + 1))
                        for j in range(n):
                            last = dve.bn_stats(st6[0:p, s, j, :], xr[0:p, s, j, :])
                        last.then_inc(st_done, 1)
                    two = back(at, 2)
                    if inside(two, NG):
                        k = two[0]
                        s, _ = ring(two, GU)
                        p, n = group_shape(k)
                        dve.wait_ge(sd_done, k + 1)
                        dve.reciprocal(rstd[0:p, bass.ds(k * T, n)], sd[0:p, s, 0:n]).then_inc(rc_done, 1)
                    one = back(at, 1)
                    if inside(one, NG):
                        k = one[0]
                        s, _ = ring(one, GU)
                        p, n = group_shape(k)
                        after(dve, sd_done, k - GU + 1)
                        dve.wait_ge(st_done, k + 1)
                        dve.nop(nofuse=True)
                        for j in range(n):
                            last = dve.bn_aggr(mv[0:p, s, j, :], st6[0:p, s, j, :])
                        last.then_inc(var_done, 1)
                    if inside(two, NG):
                        k = two[0]
                        s, _ = ring(two, GU)
                        p, n = group_shape(k)
                        dve.wait_ge(rc_done, k + 1)
                        dve.scalar_tensor_tensor(out=nmr[0:p, bass.ds(k * T, n)], in0=mv[0:p, s, 0:n, 0],
                                                 scalar=-1.0, in1=rstd[0:p, bass.ds(k * T, n)],
                                                 op0=ALU.mult, op1=ALU.mult).then_inc(nb_done, 1)

                def edge(at):
                    if inside(at, ET):
                        t = at[0]
                        s, used = ring(at, EU)
                        dve.wait_ge(s_in[s], 16 * (used + 1))
                        dve.wait_ge(d_in[s], 16 * (used + 1))
                        dve.bn_stats(est6[:, s, 0, :], e_s[:, s, :])
                        dve.bn_stats(est6[:, s, 1, :], e_d[:, s, :]).then_inc(est_done, 1)
                    two = back(at, 2)
                    if inside(two, ET):
                        t = two[0]
                        s, _ = ring(two, EU)
                        dve.wait_ge(esd_done, t + 1)
                        after(dve, ehn_done, t - EU + 1)
                        dve.reciprocal(er[:, s, :], esd[:, s, :]).then_inc(erc_done, 1)
                    one = back(at, 1)
                    if inside(one, ET):
                        t = one[0]
                        s, _ = ring(one, EU)
                        dve.wait_ge(est_done, t + 1)
                        dve.nop(nofuse=True)
                        dve.bn_aggr(emv[:, s, 0, :], est6[:, s, 0, :])
                        dve.bn_aggr(emv[:, s, 1, :], est6[:, s, 1, :]).then_inc(evar_done, 1)
                    three = back(at, 3)
                    if inside(three, ET):
                        t = three[0]
                        s, used = ring(three, EU)
                        dve.wait_ge(ehn_done, t + 1)
                        dve.wait_ge(ea_in[s], 16 * (used + 1))
                        dve.tensor_tensor(e_hs[:, s, :], e_hs[:, s, :], e_ea[:, s, :],
                                          ALU.add).then_inc(eadd_done, 1)
                    if inside(two, ET):
                        t = two[0]
                        s, _ = ring(two, EU)
                        dve.wait_ge(erc_done, t + 1)
                        dve.scalar_tensor_tensor(out=enb[:, s, :], in0=emv[:, s, :, 0], scalar=-1.0,
                                                 in1=er[:, s, :], op0=ALU.mult,
                                                 op1=ALU.mult).then_inc(enb_done, 1)
                    if inside(three, ET):
                        t = three[0]
                        s, used = ring(three, EU)
                        after(dve, tot_made, t - EU + 1)
                        dve.wait_ge(bc_in[s], 16 * (used + 1))
                        dve.tensor_scalar(e_sel[:, s, :], e_bc[:, s, :], dst_f[:, bass.ds(t, 1)], None, ALU.is_equal)
                        dve.tensor_scalar(e_car[:, s, :], e_bc[:, s, :], carry_key[:, bass.ds(t, 1)], None,
                                          ALU.is_equal)
                        dve.wait_ge(eadd_done, t + 1)
                        dve.tensor_scalar(e_hs[:, s, :], e_hs[:, s, :], 0.0, None,
                                          ALU.max).then_inc(msg_done, 1)
                    six = back(at, 6)
                    if inside(six, ET):
                        t = six[0]
                        s, _ = ring(six, EU)
                        dve.wait_ge(tot_kept, t + 1)
                        after(dve, corr_done, t - EU + 1)
                        dve.scalar_tensor_tensor(out=e_q[:, s, :], in0=e_twice[:, s, :], scalar=0.25,
                                                 in1=e_hd[:, s, :], op0=ALU.mult,
                                                 op1=ALU.add).then_inc(q_done, 1)

                mixed_rounds(dve, group, edge, 2, 6)

            @block.tensor
            def _(pe):
                pe.matmul(G[:, :], zeros[:, 0:P], zeros[:, 0:512], start=True, stop=False, skip_group_check=True)
                pe.matmul(B[:, :], zeros[:, 0:P], zeros[:, 0:512], start=True, stop=False, skip_group_check=True)
                pe.wait_ge(ring_clear, 1)

                def add(o, a, b):
                    return pe.matmul(o, a, b, start=False, stop=False, skip_group_check=True)

                def group(at):
                    at = back(at, 3)
                    if not inside(at, NG):
                        return
                    k = at[0]
                    s, _ = ring(at, GH)
                    p, n = group_shape(k)
                    pe.wait_ge(h_done, k + 1)
                    for j in range(n):
                        h = hr[0:p, s, j, :]
                        add(G[:, 0:CH + 1], h[:, 0:P], h)
                        last = add(G[:, CH + 1:CH + 2 + P], h[:, P:CH], h[:, P:CH + 1])
                    last.then_inc(gram_done, 1)

                def edge(at):
                    four = back(at, 4)
                    if inside(four, ET):
                        t = four[0]
                        s, _ = ring(four, EU)
                        pe.wait_ge(msg_done, t + 1)
                        first = is_int(t) and t == 0
                        after(pe, tot_kept, t)
                        last = pe.matmul(tot_ps, e_sel[:, s, :], e_hs[:, s, :], start=True, stop=first)
                        if not first:
                            last = pe.matmul(tot_ps, e_car[96:P, s, :], e_tot[96:P, (s - 1) % EU, :],
                                             start=False, stop=True)
                        last.then_inc(tot_made, 1)
                    seven = back(at, 7)
                    if inside(seven, ET):
                        t = seven[0]
                        s, _ = ring(seven, EU)
                        pe.wait_ge(q_done, t + 1)
                        a = e_twice[:, s, :]
                        add(B[:, 0:CH], e_q[:, s, 0:P], a)
                        add(B[:, CH:2 * CH], e_q[:, s, P:CH], a)
                        add(G[:, CH + 2 + P:CH + 3 + P], a[:, 0:P], ones[:])
                        add(G[:, CH + 3 + P:CH + 4 + P], a[:, P:CH], ones[:]).then_inc(corr_done, 1)

                mixed_rounds(pe, group, edge, 3, 7)
                pe.matmul(G[:, :], zeros[:, 0:P], zeros[:, 0:512], start=False, stop=True, skip_group_check=True)
                pe.matmul(B[:, :], zeros[:, 0:P], zeros[:, 0:512], start=False, stop=True, skip_group_check=True)

        next_phase()
        c0 = sem("c0")
        d_copied = sem("d_copied")
        d_made = sem("d_made")
        t_made = sem("t_made")
        wt_made = sem("wt_made")
        q_made = sem("q_made")
        var_made = sem("var_made")
        sdev_made = sem("sdev_made")
        N = float(NODES)
        with nc.Block() as block:
            @block.scalar
            def _(act):
                act.activation(Dm[:], B[:, :], ACT.Copy, scale=1.0 / N)
                act.activation(sums[:, 0:1], G[:, CH:CH + 1], ACT.Copy, scale=1.0 / N)
                act.activation(sums[:, 1:4], G[:, CH + 1 + P:CH + 4 + P], ACT.Copy,
                               scale=1.0 / N).then_inc(d_copied, 1)
                act.wait_ge(var_made, 1)
                act.activation(small[:, 4, :], small[:, 3, :], ACT.Sqrt, bias=eps[:]).then_inc(sdev_made, 1)

            @block.vector
            def _(dve):
                count = [0]

                def link(ins):
                    count[0] += 1
                    ins.then_inc(c0, 1)
                    dve.wait_ge(c0, count[0])

                dve.wait_ge(d_copied, 1)
                for o, g, f in ((0, 0, 1.0), (P, P, 2.0), (3 * P, CH + 1, 1.0)):
                    dve.scalar_tensor_tensor(out=Dm[:, o:o + P], in0=G[:, g:g + P], scalar=f / N,
                                             in1=Dm[:, o:o + P], op0=ALU.mult, op1=ALU.add)
                for j in range(2):
                    last = dve.scalar_tensor_tensor(out=mh[:, j:j + 1], in0=sums[:, 2 + j:3 + j], scalar=0.5,
                                                    in1=sums[:, j:j + 1], op0=ALU.mult, op1=ALU.add)
                last.then_inc(d_made, 1)
                dve.wait_ge(t_made, 1)
                for j in range(KC):
                    last = dve.tensor_tensor(WT[:, j, :], W1s[:, j, :], pair[0][:, j, :], ALU.mult)
                last.then_inc(wt_made, 1)
                dve.wait_ge(q_made, 1)
                link(dve.tensor_copy(small[:, 0:2, :], pair[1][:, 0, 0:8].rearrange("p (a b) -> p a b", a=2)))
                zq, zm = small[:, 0, :], small[:, 1, :]
                link(dve.tensor_tensor(small[:, 2, :], zm, zm, ALU.mult))
                link(dve.tensor_tensor(small[:, 2, :], zq, small[:, 2, :], ALU.subtract))
                dve.tensor_scalar(small[:, 3, :], small[:, 2, :], 0.0, None, ALU.max).then_inc(var_made, 1)
                link(dve.tensor_tensor(small[:, 5, :], zm, b1v, ALU.add))
                link(dve.tensor_tensor(small[:, 5, :], b1v, small[:, 5, :], ALU.subtract))
                dve.wait_ge(sdev_made, 1)
                link(dve.reciprocal(small[:, 6, :], small[:, 4, :]))
                link(dve.tensor_tensor(bnA[:], small[:, 6, :], gammav, ALU.mult))
                link(dve.tensor_tensor(small[:, 7, :], bnA[:], small[:, 5, :], ALU.mult))
                link(dve.tensor_tensor(bnC[:], small[:, 7, :], betav, ALU.add))

            @block.tensor
            def _(pe):
                pe.wait_ge(d_made, 1)
                for o in range(KC):
                    for l in range(KC):
                        last = pe.matmul(pair[0][:, o, :], Dm[:, l * CH + o * P:l * CH + o * P + P],
                                         W1s[:, l, :], start=l == 0, stop=l == KC - 1)
                last.then_inc(t_made, 1)
                pe.wait_ge(wt_made, 1)
                for m in range(HC):
                    for l in range(KC):
                        pe.matmul(pair[1][:, 0, m:m + 1], WT[:, l, m * P:m * P + P], ones[:],
                                  start=l == 0, stop=l == KC - 1)
                for m in range(HC):
                    for l in range(KC):
                        last = pe.matmul(pair[1][:, 0, 4 + m:5 + m], W1s[:, l, m * P:m * P + P], mh[:, l:l + 1],
                                         start=l == 0, stop=l == KC - 1)
                last.then_inc(q_made, 1)

        next_phase()
        NU = 4
        x2_in = [sem(f"x2_in{s}") for s in range(NU)]
        a2_in = [[sem(f"a2_in{s}_{j}") for j in range(T)] for s in range(NU)]
        y_out = [sem(f"y_out{s}") for s in range(NU)]
        xh_out = [sem(f"xh_out{s}") for s in range(NU)]
        ids_in = sem("ids_in")
        ids_got = sem("ids_got")
        a2_clear = sem("a2_clear")
        h2n_done = sem("h2n_done")
        xh2_done = sem("xh2_done")
        h2_done = sem("h2_done")
        t2_made = sem("t2_made")
        th_kept = sem("th_kept")
        tl_kept = sem("tl_kept")
        z_made = sem("z_made")
        r_kept = sem("r_kept")
        rh_kept = sem("rh_kept")
        rl_kept = sem("rl_kept")
        y_made = sem("y_made")
        y_kept = sem("y_kept")
        yst_done = sem("yst_done")
        hT_ps, z_ps, y_ps = pair[0], [pair[1][:, 0, :], pair[1][:, 1, :], pair[2][:, 0, :], pair[2][:, 1, :]], bank

        with ExitStack() as scope, nc.Block() as block:
            xr = sb("xr2", [P, NU, T, CH], scope=scope)
            ar = sb("ar2", [P, NU, T, CH], scope=scope)
            hr = sb("hr2", [P, NU, T, CH], scope=scope)
            tH = sb("tH", [P, 2, KC, GC], FP32R, scope=scope)
            tL = sb("tL", [P, 2, KC, GC], FP32R, scope=scope)
            r32 = sb("r32", [P, HC, GC], scope=scope)
            rH = sb("rH", [P, HC, GC], FP32R, scope=scope)
            rL = sb("rL", [P, HC, GC], FP32R, scope=scope)
            yr = sb("yr", [P, NU, KC, GC], scope=scope)
            ids = sb("ids", [P, TILES], I32, scope=scope)
            ids_rest = sb("ids_rest", [P, 1], I32, scope=scope)
            idx = sb("idx2", [P, NU, T], I32, scope=scope)

            @block.sync
            def _(sp):
                sp.dma_start(ids[:], id_table[0:P * TILES, :].rearrange("(p t) a -> p (t a)", t=TILES)
                             ).then_inc(ids_in, 16)
                sp.dma_start(ids_rest[0:REST, :], id_table[P * TILES:NODES, :]).then_inc(ids_in, 16)

                def step(at):
                    if inside(at, NG):
                        k = at[0]
                        s, used = ring(at, NU)
                        p, n = group_shape(k)
                        after(sp, xh_out[s], 16 * used)
                        sp.dma_start(xr[0:p, s, 0:n, :], group_rows(x, k)).then_inc(x2_in[s], 16)
                    three = back(at, 3)
                    if inside(three, NG):
                        k = three[0]
                        s, _ = ring(three, NU)
                        p, n = group_shape(k)
                        sp.wait_ge(xh2_done, k + 1)
                        sp.dma_start(group_rows(xh_table, k), xr[0:p, s, 0:n, :]).then_inc(xh_out[s], 16)
                    six = back(at, 6)
                    if inside(six, NG):
                        k = six[0]
                        s, _ = ring(six, NU)
                        n = columns(k)
                        sp.wait_ge(y_kept, k + 1)
                        sp.dma_start(group_block(yT_table, k)[:, :, 0:n], yr[:, s, :, 0:n]).then_inc(y_out[s], 16)

                rounds(sp, step, NG, NU, 2, 6)
                for s in range(NU):
                    sp.wait_ge(y_out[s], 16 * (-(-(NG - s) // NU)))
                    sp.wait_ge(xh_out[s], 16 * (-(-(NG - s) // NU)))

            @block.gpsimd
            def _(pool):
                pool.wait_ge(ids_in, 32)

                def step(at):
                    if inside(at, NG):
                        k = at[0]
                        s, _ = ring(at, NU)
                        p, n = group_shape(k)
                        after(pool, t2_made, k - NU + 1)
                        pool.nop(nofuse=True)
                        pool.memset(ar[0:p, s, 0:n, :], 0.0)
                        where = ids_rest[0:p, :] if is_int(k) and k == GROUPS else ids[:, bass.ds(k * T, T)]
                        pool.tensor_copy(idx[0:p, s, 0:n], where).then_inc(a2_clear, 1)
                        pool.wait_ge(a2_clear, k + 1)
                        pool.nop(nofuse=True)
                        for j in range(n):
                            pool.indirect_dma_start(ar[0:p, s, j, :], None, sum_table[:, :],
                                                    bass.IndirectOffsetOnAxis(ap=idx[0:p, s, j:j + 1], axis=0),
                                                    bounds_check=ET * P - 1, oob_is_err=False
                                                    ).then_inc(a2_in[s][j], 16)
                    two = back(at, 2)
                    if inside(two, NG):
                        k = two[0]
                        s, _ = ring(two, NU)
                        p, n = group_shape(k)
                        pool.wait_ge(h2n_done, k + 1)
                        pool.nop(nofuse=True)
                        pool.tensor_tensor(xr[0:p, s, 0:n, :], xr[0:p, s, 0:n, :], hr[0:p, s, 0:n, :],
                                           ALU.add).then_inc(xh2_done, 1)

                rounds(pool, step, NG, NU, 1, 2)

            @block.scalar
            def _(act):
                def norm(at):
                    if not inside(at, NG):
                        return []
                    k = at[0]
                    s, used = ring(at, NU)
                    p, n = group_shape(k)

                    def piece(j):
                        if j == 0:
                            act.wait_ge(x2_in[s], 16 * (used + 1))
                            after(act, h2_done, k - NU + 1)
                            after(act, xh2_done, k - NU + 1)
                        one = act.activation(hr[0:p, s, j, :], xr[0:p, s, j, :], ACT.Relu,
                                             bias=nmr[0:p, bass.ds(k * T + j, 1)],
                                             scale=rstd[0:p, bass.ds(k * T + j, 1)])
                        if j == n - 1:
                            one.then_inc(h2n_done, 1)

                    return [lambda j=j: piece(j) for j in range(n)]

                def hidden(at, m):
                    if not inside(at, NG):
                        return
                    k = at[0]
                    n = columns(k)
                    after(act, rl_kept, (k - 1) * HC + m + 1)
                    act.wait_ge(z_made, k * HC + m + 1)
                    act.activation(r32[:, m, 0:n], z_ps[m][:, 0:n], ACT.Relu, bias=bnC[:, m:m + 1],
                                   scale=bnA[:, m:m + 1]).then_inc(r_kept, 1)

                def keep_y(at):
                    if not inside(at, NG):
                        return
                    k = at[0]
                    s, used = ring(at, NU)
                    n = columns(k)
                    act.wait_ge(y_made, k + 1)
                    after(act, yst_done, k - NU + 1)
                    after(act, y_out[s], 16 * used)
                    for c in range(KC):
                        last = act.activation(yr[:, s, c, 0:n], y_ps[c][:, 0:n], ACT.Identity,
                                              bias=b2v[:, c:c + 1])
                    last.then_inc(y_kept, 1)

                def keep_high(at):
                    if not inside(at, NG):
                        return
                    k = at[0]
                    s, _ = ring(at, 2)
                    n = columns(k)
                    act.wait_ge(t2_made, k + 1)
                    after(act, z_made, (k - 1) * HC)
                    for c in range(KC):
                        last = act.activation(tH[:, s, c, 0:n], hT_ps[:, c, 0:n], ACT.Copy)
                    last.then_inc(th_kept, 1)

                def step(at):
                    keep_y(back(at, 1))
                    pieces = norm(back(at, -2))
                    for m in range(HC):
                        hidden(at, m)
                        for piece in pieces[m:m + 1]:
                            piece()
                    keep_high(back(at, -1))

                for k in range(2):
                    for piece in norm((k, k, 0, NU)):
                        piece()
                keep_high((0, 0, 0, NU))
                rounds(act, step, NG, NU, 1, 1)

            @block.vector
            def _(dve):
                def add(at):
                    if not inside(at, NG):
                        return
                    k = at[0]
                    s, used = ring(at, NU)
                    p, n = group_shape(k)
                    dve.wait_ge(h2n_done, k + 1)
                    for j in range(n):
                        dve.wait_ge(a2_in[s][j], 16 * (used + 1))
                    dve.tensor_tensor(ar[0:p, s, 0:n, :], ar[0:p, s, 0:n, :], hr[0:p, s, 0:n, :],
                                      ALU.add).then_inc(h2_done, 1)

                def keep_low(at):
                    if not inside(at, NG):
                        return
                    k = at[0]
                    s, _ = ring(at, 2)
                    n = columns(k)
                    dve.wait_ge(th_kept, k + 1)
                    for c in range(KC):
                        last = dve.tensor_tensor(tL[:, s, c, 0:n], hT_ps[:, c, 0:n],
                                                 tH[:, s, c, 0:n].bitcast(FP32), ALU.subtract)
                    last.then_inc(tl_kept, 1)

                def stats(at, c):
                    if not inside(at, NG):
                        return
                    k = at[0]
                    s, _ = ring(at, NU)
                    n = columns(k)
                    if c == 0:
                        dve.wait_ge(y_kept, k + 1)
                    one = dve.bn_stats(yst[:, c, bass.ds(k, 1), :].rearrange("p a b -> p (a b)"),
                                       yr[:, s, c, 0:n])
                    if c == KC - 1:
                        one.then_inc(yst_done, 1)

                def high(at, m):
                    if not inside(at, NG):
                        return
                    k = at[0]
                    n = columns(k)
                    dve.wait_ge(r_kept, k * HC + m + 1)
                    after(dve, y_made, k)
                    dve.tensor_copy(rH[:, m, 0:n], r32[:, m, 0:n]).then_inc(rh_kept, 1)

                def low(at, m):
                    if not inside(at, NG):
                        return
                    k = at[0]
                    n = columns(k)
                    dve.wait_ge(rh_kept, k * HC + m + 1)
                    dve.tensor_tensor(rL[:, m, 0:n], r32[:, m, 0:n], rH[:, m, 0:n].bitcast(FP32),
                                      ALU.subtract).then_inc(rl_kept, 1)

                def step(at):
                    high(at, 0)
                    stats(back(at, 1), 0)
                    low(at, 0)
                    high(at, 1)
                    stats(back(at, 1), 1)
                    low(at, 1)
                    high(at, 2)
                    add(back(at, -2))
                    low(at, 2)
                    high(at, 3)
                    low(at, 3)
                    keep_low(back(at, -1))

                add((0, 0, 0, NU))
                add((1, 1, 0, NU))
                keep_low((0, 0, 0, NU))
                rounds(dve, step, NG, NU, 1, 1)

            @block.tensor
            def _(pe):
                def turn(at):
                    if not inside(at, NG):
                        return
                    k = at[0]
                    s, _ = ring(at, NU)
                    p, n = group_shape(k)
                    pe.wait_ge(h2_done, k + 1)
                    after(pe, tl_kept, k)
                    for c in range(KC):
                        for j in range(n):
                            last = pe.transpose(hT_ps[:, c, j * P:j * P + p],
                                                ar[0:p, s, j, c * P:(c + 1) * P], ident[0:p, 0:p])
                    last.then_inc(t2_made, 1)

                def step(at):
                    if not inside(at, NG):
                        return
                    k = at[0]
                    s, _ = ring(at, 2)
                    n = columns(k)
                    pe.wait_ge(tl_kept, k + 1)
                    for m in range(HC):
                        after(pe, r_kept, (k - 1) * HC + m + 1)
                        parts = [(w, t, c) for w, t in ((W1h, tH), (W1l, tH), (W1h, tL)) for c in range(KC)]
                        for i, (w, t, c) in enumerate(parts):
                            last = pe.matmul(z_ps[m][:, 0:n], w[:, c, m * P:(m + 1) * P], t[:, s, c, 0:n],
                                             start=i == 0, stop=i == len(parts) - 1)
                        last.then_inc(z_made, 1)
                    turn(back(at, -1))
                    after(pe, y_kept, k)
                    for ms in ((0,), (1,), (2,), (3,)):
                        pe.wait_ge(rl_kept, k * HC + ms[-1] + 1)
                        for m in ms:
                            for c in range(KC):
                                for i, (w, t) in enumerate(((W2h, rH), (W2l, rH), (W2h, rL))):
                                    last = pe.matmul(y_ps[c][:, 0:n], w[:, m, c * P:(c + 1) * P], t[:, m, 0:n],
                                                     start=m == 0 and i == 0, stop=m == HC - 1 and i == 2)
                    last.then_inc(y_made, 1)

                turn((0, 0, 0, NU))
                rounds(pe, step, NG, NU, 1, 0)

        next_phase()
        c1 = sem("c1")
        mu_in = sem("mu_in")
        mu_made = sem("mu_made")
        vg_in = sem("vg_in")
        vg_made = sem("vg_made")
        v1_made = sem("v1_made")
        s1_made = sem("s1_made")
        v2_made = sem("v2_made")
        s2_made = sem("s2_made")
        with nc.Block() as block:
            mu, vg = pair[0][:, 0, 0:1], pair[0][:, 1, 0:1]
            row = [small[:, i, 0:2] for i in range(16)]

            @block.vector
            def _(dve):
                count = [0]

                def link(ins):
                    count[0] += 1
                    ins.then_inc(c1, 1)
                    dve.wait_ge(c1, count[0])

                for c in range(KC):
                    last = dve.bn_aggr(ymv[:, c, :], yst[:, c, :, :].rearrange("p a b -> p (a b)"))
                last.then_inc(mu_in, 1)
                dve.wait_ge(mu_in, 1)
                E, V = ymv[:, :, 0], ymv[:, :, 1]
                dve.wait_ge(mu_made, 1)
                link(dve.tensor_copy(row[15], mu.broadcast_to([P, 2])))
                link(dve.tensor_tensor(row[0], E, row[15], ALU.subtract))
                link(dve.tensor_tensor(row[1], row[0], row[0], ALU.mult))
                dve.tensor_tensor(row[2], row[1], V, ALU.add).then_inc(vg_in, 1)
                dve.wait_ge(vg_made, 1)
                dve.tensor_copy(row[3], vg.broadcast_to([P, 2])).then_inc(v1_made, 1)
                dve.wait_ge(s1_made, 1)
                link(dve.reciprocal(row[5], row[4]))
                link(dve.tensor_tensor(row[5], row[5], lnwv, ALU.mult))
                link(dve.tensor_tensor(row[6], row[0], row[5], ALU.mult))
                link(dve.tensor_tensor(row[6], row[6], lnbv, ALU.add))
                link(dve.tensor_tensor(row[7], row[6], gnmsv, ALU.mult))
                link(dve.tensor_tensor(row[8], row[6], row[7], ALU.subtract))
                link(dve.tensor_tensor(row[8], row[8], row[8], ALU.mult))
                link(dve.tensor_tensor(row[9], row[5], row[5], ALU.mult))
                link(dve.tensor_tensor(row[9], row[9], V, ALU.mult))
                dve.tensor_tensor(row[9], row[9], row[8], ALU.add).then_inc(v2_made, 1)
                link(dve.tensor_tensor(row[11], row[15], row[5], ALU.mult))
                link(dve.tensor_tensor(row[11], lnbv, row[11], ALU.subtract))
                link(dve.tensor_tensor(row[11], row[11], row[7], ALU.subtract))
                dve.wait_ge(s2_made, 1)
                link(dve.reciprocal(row[12], row[10]))
                link(dve.tensor_tensor(row[12], row[12], gnwv, ALU.mult))
                link(dve.tensor_tensor(gnP[:], row[5], row[12], ALU.mult))
                link(dve.tensor_tensor(row[11], row[11], row[12], ALU.mult))
                link(dve.tensor_tensor(gnQ[:], row[11], gnbv, ALU.add))

            @block.scalar
            def _(act):
                act.wait_ge(v1_made, 1)
                act.activation(row[4], row[3], ACT.Sqrt, bias=eps[:]).then_inc(s1_made, 1)
                act.wait_ge(v2_made, 1)
                act.activation(row[10], row[9], ACT.Sqrt, bias=eps[:]).then_inc(s2_made, 1)

            @block.tensor
            def _(pe):
                pe.wait_ge(mu_in, 1)
                for c in range(KC):
                    last = pe.matmul(mu, mean_of[:], ymv[:, c, 0:1], start=c == 0, stop=c == KC - 1)
                last.then_inc(mu_made, 1)
                pe.wait_ge(vg_in, 1)
                for c in range(KC):
                    last = pe.matmul(vg, mean_of[:], row[2][:, c:c + 1], start=c == 0, stop=c == KC - 1)
                last.then_inc(vg_made, 1)

        next_phase()
        RU = 8
        RL = 4
        xh_in = [sem(f"xh_in{s}") for s in range(RL)]
        y_in = [sem(f"y_in{s}") for s in range(RL)]
        x1_out = [sem(f"x1_out{s}") for s in range(RU)]
        o_out = [sem(f"o_out{s}") for s in range(RL)]
        g_done = sem("g_done")
        gt_made = sem("gt_made")
        x1_done = sem("x1_done")
        st3_done = sem("st3_done")
        var3_done = sem("var3_done")
        sd3_done = sem("sd3_done")
        rc3_done = sem("rc3_done")
        nb3_done = sem("nb3_done")
        h1_done = sem("h1_done")
        h1t_made = sem("h1t_made")
        h1t_kept = sem("h1t_kept")
        u_made = sem("u_made")
        o_done = sem("o_done")

        def tile_of(pr, j):
            return pr[:, j // 2, (j % 2) * CH:(j % 2 + 1) * CH]

        def flat(t, p, n):
            return t.rearrange("p a b -> p (a b)")[0:p, 0:n * CH]

        with ExitStack() as scope, nc.Block() as block:
            xhr = sb("xhr", [P, RL, T, CH], scope=scope)
            yr = sb("yr3", [P, RL, KC, GC], scope=scope)
            gr = sb("gr", [P, 2, KC, GC], scope=scope)
            x1r = sb("x1r", [P, RU, T, CH], scope=scope)
            h1r = sb("h1r", [P, 2, T, CH], scope=scope)
            h1T = sb("h1T", [P, 2, KC, GC], scope=scope)
            orr = sb("orr", [P, RL, T, CH], scope=scope)
            st6 = sb("st6_3", [P, RU, T, 6], scope=scope)
            mv = sb("mv_3", [P, RU, T, 2], scope=scope)
            sd = sb("sd_3", [P, RU, T], scope=scope)
            r3 = sb("r3", [P, RU, T], scope=scope)
            n3 = sb("n3", [P, RU, T], scope=scope)

            @block.sync
            def _(sp):
                def step(at):
                    if inside(at, NG):
                        k = at[0]
                        s, _ = ring(at, RL)
                        p, n = group_shape(k)
                        after(sp, x1_done, k - RL + 1)
                        sp.dma_start(xhr[0:p, s, 0:n, :], group_rows(xh_table, k)).then_inc(xh_in[s], 16)
                        c = columns(k)
                        after(sp, g_done, k - RL + 1)
                        sp.dma_start(yr[:, s, :, 0:c], group_block(yT_table, k)[:, :, 0:c]).then_inc(y_in[s], 16)
                    four = back(at, 4)
                    if inside(four, NG):
                        k = four[0]
                        s, _ = ring(four, RU)
                        p, n = group_shape(k)
                        sp.wait_ge(x1_done, k + 1)
                        sp.dma_start(group_rows(x1_table, k), x1r[0:p, s, 0:n, :]).then_inc(x1_out[s], 16)
                    late = back(at, 10)
                    if inside(late, NG):
                        k = late[0]
                        s, _ = ring(late, RL)
                        p, n = group_shape(k)
                        sp.wait_ge(o_done, k + 1)
                        sp.dma_start(group_rows(out, k), orr[0:p, s, 0:n, :]).then_inc(o_out[s], 16)

                rounds(sp, step, NG, RU, 2, 10)
                for s in range(RU):
                    sp.wait_ge(x1_out[s], 16 * (-(-(NG - s) // RU)))
                for s in range(RL):
                    sp.wait_ge(o_out[s], 16 * (-(-(NG - s) // RL)))

            @block.scalar
            def _(act):
                def step(at):
                    if inside(at, NG):
                        k = at[0]
                        s, used = ring(at, RL)
                        f, _ = ring(at, 2)
                        m = columns(k)
                        act.wait_ge(y_in[s], 16 * (used + 1))
                        after(act, gt_made, k - 1)
                        for c in range(KC):
                            last = act.activation(gr[:, f, c, 0:m], yr[:, s, c, 0:m], ACT.Relu,
                                                  bias=gnQ[:, c:c + 1], scale=gnP[:, c:c + 1])
                        last.then_inc(g_done, 1)
                    three = back(at, 3)
                    if inside(three, NG):
                        k = three[0]
                        s, _ = ring(three, RU)
                        p, n = group_shape(k)
                        act.wait_ge(var3_done, k + 1)
                        after(act, rc3_done, k - RU + 1)
                        act.activation(sd[0:p, s, 0:n], mv[0:p, s, 0:n, 1], ACT.Sqrt,
                                       bias=eps[0:p, :]).then_inc(sd3_done, 1)
                    six = back(at, 6)
                    if inside(six, NG):
                        k = six[0]
                        s, _ = ring(six, 2)
                        n = columns(k)
                        act.wait_ge(h1t_made, k + 1)
                        after(act, u_made, k - 1)
                        for c in range(KC):
                            last = act.activation(h1T[:, s, c, 0:n], pair[1][:, c, 0:n], ACT.Copy)
                        last.then_inc(h1t_kept, 1)
                    four = back(at, 4)
                    if inside(four, NG):
                        k = four[0]
                        s, _ = ring(four, RU)
                        f, _ = ring(four, 2)
                        p, n = group_shape(k)
                        act.wait_ge(nb3_done, k + 1)
                        after(act, h1t_made, k - 1)
                        for j in range(n):
                            last = act.activation(h1r[0:p, f, j, :], x1r[0:p, s, j, :], ACT.Relu,
                                                  bias=n3[0:p, s, j:j + 1], scale=r3[0:p, s, j:j + 1])
                        last.then_inc(h1_done, 1)

                rounds(act, step, NG, RU, 2, 6)

            @block.vector
            def _(dve):
                def step(at):
                    one = back(at, 1)
                    if inside(one, NG):
                        k = one[0]
                        s, used = ring(one, RL)
                        b, bused = ring(one, RU)
                        p, n = group_shape(k)
                        dve.wait_ge(xh_in[s], 16 * (used + 1))
                        dve.wait_ge(gt_made, k + 1)
                        after(dve, x1_out[b], 16 * bused)
                        after(dve, h1_done, k - RU + 1)
                        after(dve, o_done, k - RU + 1)
                        dve.tensor_tensor(flat(x1r[:, b, :, :], p, n), flat(xhr[:, s, :, :], p, n),
                                          flat(pair[0][:, :, :], p, n), ALU.add).then_inc(x1_done, 1)
                    four = back(at, 4)
                    if inside(four, NG):
                        k = four[0]
                        s, _ = ring(four, RU)
                        p, n = group_shape(k)
                        dve.wait_ge(sd3_done, k + 1)
                        after(dve, h1_done, k - RU + 1)
                        dve.reciprocal(r3[0:p, s, 0:n], sd[0:p, s, 0:n]).then_inc(rc3_done, 1)
                    two = back(at, 2)
                    if inside(two, NG):
                        k = two[0]
                        s, _ = ring(two, RU)
                        p, n = group_shape(k)
                        dve.wait_ge(x1_done, k + 1)
                        for j in range(n):
                            last = dve.bn_stats(st6[0:p, s, j, :], x1r[0:p, s, j, :])
                        last.then_inc(st3_done, 1)
                    if inside(four, NG):
                        k = four[0]
                        s, _ = ring(four, RU)
                        p, n = group_shape(k)
                        dve.wait_ge(rc3_done, k + 1)
                        dve.scalar_tensor_tensor(out=n3[0:p, s, 0:n], in0=mv[0:p, s, 0:n, 0], scalar=-1.0,
                                                 in1=r3[0:p, s, 0:n], op0=ALU.mult,
                                                 op1=ALU.mult).then_inc(nb3_done, 1)
                    three = back(at, 3)
                    if inside(three, NG):
                        k = three[0]
                        s, _ = ring(three, RU)
                        p, n = group_shape(k)
                        after(dve, sd3_done, k - RU + 1)
                        dve.wait_ge(st3_done, k + 1)
                        dve.nop(nofuse=True)
                        for j in range(n):
                            last = dve.bn_aggr(mv[0:p, s, j, :], st6[0:p, s, j, :])
                        last.then_inc(var3_done, 1)
                    seven = back(at, 7)
                    if inside(seven, NG):
                        k = seven[0]
                        s, used = ring(seven, RL)
                        b, _ = ring(seven, RU)
                        p, n = group_shape(k)
                        dve.wait_ge(u_made, k + 1)
                        after(dve, o_out[s], 16 * used)
                        dve.scalar_tensor_tensor(out=flat(orr[:, s, :, :], p, n), in0=flat(pair[2][:, :, :], p, n),
                                                 scalar=0.0, in1=flat(x1r[:, b, :, :], p, n),
                                                 op0=ALU.max, op1=ALU.add).then_inc(o_done, 1)

                rounds(dve, step, NG, RU, 2, 7)

            @block.tensor
            def _(pe):
                def step(at):
                    if inside(at, NG):
                        k = at[0]
                        s, _ = ring(at, 2)
                        p, n = group_shape(k)
                        pe.wait_ge(g_done, k + 1)
                        after(pe, x1_done, k)
                        for j in range(n):
                            for c in range(KC):
                                last = pe.transpose(tile_of(pair[0], j)[0:p, c * P:(c + 1) * P],
                                                    gr[:, s, c, j * P:j * P + p], ident[:])
                        last.then_inc(gt_made, 1)
                    five = back(at, 5)
                    if inside(five, NG):
                        k = five[0]
                        s, _ = ring(five, 2)
                        p, n = group_shape(k)
                        pe.wait_ge(h1_done, k + 1)
                        after(pe, h1t_kept, k)
                        for c in range(KC):
                            for j in range(n):
                                last = pe.transpose(pair[1][:, c, j * P:j * P + p],
                                                    h1r[0:p, s, j, c * P:(c + 1) * P], ident[0:p, 0:p])
                        last.then_inc(h1t_made, 1)
                    six = back(at, 6)
                    if inside(six, NG):
                        k = six[0]
                        s, _ = ring(six, 2)
                        p, n = group_shape(k)
                        pe.wait_ge(h1t_kept, k + 1)
                        after(pe, o_done, k)
                        for j in range(n):
                            for c in range(KC):
                                last = pe.matmul(tile_of(pair[2], j)[0:p, :], h1T[:, s, c, j * P:j * P + p],
                                                 Ws[:, c, :], start=c == 0, stop=c == KC - 1)
                        last.then_inc(u_made, 1)

                rounds(pe, step, NG, RU, 2, 6)

        next_phase()
        XU = 14
        XH = 7
        s4_in = [sem(f"s4_in{s}") for s in range(XU)]
        d4_in = [sem(f"d4_in{s}") for s in range(XU)]
        bc4_in = [sem(f"bc4_in{s}") for s in range(XH)]
        o4_out = [sem(f"o4_out{s}") for s in range(XU)]
        got4_index = sem("got4_index")
        put4_index = sem("put4_index")
        clear4 = sem("clear4")
        st4_done = sem("st4_done")
        var4_done = sem("var4_done")
        sd4_done = sem("sd4_done")
        rc4_done = sem("rc4_done")
        nb4_done = sem("nb4_done")
        hn4_done = sem("hn4_done")
        sel4_done = sem("sel4_done")
        sum4_made = sem("sum4_made")
        sum4_kept = sem("sum4_kept")
        hT4_made = sem("hT4_made")
        hT4_kept = sem("hT4_kept")
        u4_made = sem("u4_made")
        o4_done = sem("o4_done")
        with ExitStack() as scope, nc.Block() as block:
            e_s = sb("f_s", [P, XU, CH], scope=scope)
            e_d = sb("f_d", [P, XU, CH], scope=scope)
            e_o = sb("f_o", [P, XU, CH], scope=scope)
            e_hs = sb("f_hs", [P, XH, CH], scope=scope)
            e_hd = sb("f_hd", [P, XH, CH], scope=scope)
            e_hT = sb("f_hT", [P, XH, KC, P], scope=scope)
            e_sT = sb("f_sT", [P, XH, KC, P], scope=scope)
            e_bc = sb("f_bc", [P, XH, P], I32, scope=scope)
            e_sel = sb("f_sel", [P, XH, P], scope=scope)
            e_go = sb("f_go", [P, XH, P], scope=scope)
            idx = sb("f_idx", [P, XU, 2], I32, scope=scope)
            put = sb("f_put", [P, XU, 1], I32, scope=scope)
            est6 = sb("f_st6", [P, XU, 2, 6], scope=scope)
            emv = sb("f_mv", [P, XU, 2, 2], scope=scope)
            esd = sb("f_sd", [P, XU, 2], scope=scope)
            er = sb("f_r", [P, XU, 2], scope=scope)
            enb = sb("f_nb", [P, XU, 2], scope=scope)
            sT_ps = [bank[i][:, 0:CH] for i in range(2)]
            hT_ps4 = [pair[1][:, i, 0:CH] for i in range(2)]
            u_ps = [pair[0][:, i, 0:CH] for i in range(2)]

            @block.sync
            def _(sp):
                sp.wait_ge(clear4, 1)

                def step(at):
                    t = at[0]
                    s, _ = ring(at, XH)
                    after(sp, sel4_done, t - XH + 1)
                    rows, n = dst_columns(t)
                    sp.dma_start(e_bc[:, s, 0:n], rows).then_inc(bc4_in[s], 16)

                rounds(sp, step, ET - 1, XH, 2, 1)

            @block.gpsimd
            def _(pool):
                pool.memset(e_bc[:, :, :], 0)
                pool.memset(e_s[:, :, :], 0.0)
                pool.memset(e_d[:, :, :], 0.0).then_inc(clear4, 1)
                pool.wait_ge(clear4, 1)

                def step(at):
                    if inside(at, ET):
                        t = at[0]
                        s, _ = ring(at, XU)
                        after(pool, hn4_done, t - XU + 1)
                        after(pool, o4_done, t - XU + 1)
                        pool.nop(nofuse=True)
                        pool.tensor_copy(idx[:, s, :], index[:, bass.ds(t, 1), 0:2].rearrange("p a b -> p (a b)")
                                         ).then_inc(got4_index, 1)
                        pool.wait_ge(got4_index, t + 1)
                        pool.nop(nofuse=True)
                        for tile, j, done in ((e_s, 0, s4_in), (e_d, 1, d4_in)):
                            pool.indirect_dma_start(tile[:, s, :], None, x1_table[:, :],
                                                    bass.IndirectOffsetOnAxis(ap=idx[:, s, j:j + 1], axis=0),
                                                    bounds_check=NODES - 1, oob_is_err=False).then_inc(done[s], 16)
                    late = back(at, 9)
                    if inside(late, ET):
                        t = late[0]
                        s, used = ring(late, XU)
                        after(pool, o4_out[s], 16 * used)
                        pool.nop(nofuse=True)
                        pool.tensor_copy(put[:, s, :], index[:, bass.ds(t, 1), 2:3].rearrange("p a b -> p (a b)")
                                         ).then_inc(put4_index, 1)
                        pool.wait_ge(put4_index, t + 1)
                        pool.nop(nofuse=True)
                        pool.wait_ge(o4_done, t + 1)
                        pool.nop(nofuse=True)
                        pool.indirect_dma_start(out[:, :], bass.IndirectOffsetOnAxis(ap=put[:, s, :], axis=0),
                                                e_o[:, s, :], None, bounds_check=NODES - 1,
                                                oob_is_err=False).then_inc(o4_out[s], 16)

                rounds(pool, step, ET, XU, 2, 9)
                for s in range(XU):
                    pool.wait_ge(o4_out[s], 16 * (-(-(ET - s) // XU)))

            @block.scalar
            def _(act):
                def step(at):
                    one = back(at, 1)
                    if inside(one, ET):
                        t = one[0]
                        s, _ = ring(one, XU)
                        act.wait_ge(var4_done, t + 1)
                        after(act, rc4_done, t - XU + 1)
                        act.activation(esd[:, s, :], emv[:, s, :, 1], ACT.Sqrt, bias=eps[:]).then_inc(sd4_done, 1)
                    four = back(at, 4)
                    if inside(four, ET):
                        t = four[0]
                        s, _ = ring(four, XH)
                        act.wait_ge(hT4_made, t + 1)
                        after(act, u4_made, t - XH + 1)
                        act.activation(e_hT[:, s, :, :].rearrange("p a b -> p (a b)"), hT_ps4[ring(four, 2)[0]],
                                       ACT.Copy).then_inc(hT4_kept, 1)
                    two = back(at, 2)
                    if inside(two, ET):
                        t = two[0]
                        s, _ = ring(two, XU)
                        h, _ = ring(two, XH)
                        act.wait_ge(nb4_done, t + 1)
                        after(act, sum4_made, t - XH + 1)
                        after(act, hT4_made, t - XH + 1)
                        act.activation(e_hs[:, h, :], e_s[:, s, :], ACT.Relu,
                                       bias=enb[:, s, 0:1], scale=er[:, s, 0:1])
                        act.activation(e_hd[:, h, :], e_d[:, s, :], ACT.Relu,
                                       bias=enb[:, s, 1:2], scale=er[:, s, 1:2]).then_inc(hn4_done, 1)

                rounds(act, step, ET, XU, 2, 4)

            @block.vector
            def _(dve):
                def step(at):
                    if inside(at, ET):
                        t = at[0]
                        s, used = ring(at, XU)
                        dve.wait_ge(s4_in[s], 16 * (used + 1))
                        dve.wait_ge(d4_in[s], 16 * (used + 1))
                        dve.bn_stats(est6[:, s, 0, :], e_s[:, s, :])
                        dve.bn_stats(est6[:, s, 1, :], e_d[:, s, :]).then_inc(st4_done, 1)
                    two = back(at, 2)
                    if inside(two, ET):
                        t = two[0]
                        s, _ = ring(two, XU)
                        dve.wait_ge(sd4_done, t + 1)
                        after(dve, hn4_done, t - XU + 1)
                        dve.reciprocal(er[:, s, :], esd[:, s, :]).then_inc(rc4_done, 1)
                    one = back(at, 1)
                    if inside(one, ET):
                        t = one[0]
                        s, _ = ring(one, XU)
                        after(dve, sd4_done, t - XU + 1)
                        dve.wait_ge(st4_done, t + 1)
                        dve.nop(nofuse=True)
                        dve.bn_aggr(emv[:, s, 0, :], est6[:, s, 0, :])
                        dve.bn_aggr(emv[:, s, 1, :], est6[:, s, 1, :]).then_inc(var4_done, 1)
                    if inside(two, ET):
                        t = two[0]
                        s, _ = ring(two, XU)
                        h, hused = ring(two, XH)
                        dve.wait_ge(rc4_done, t + 1)
                        dve.scalar_tensor_tensor(out=enb[:, s, :], in0=emv[:, s, :, 0], scalar=-1.0,
                                                 in1=er[:, s, :], op0=ALU.mult,
                                                 op1=ALU.mult).then_inc(nb4_done, 1)
                        dve.wait_ge(bc4_in[h], 16 * (hused + 1))
                        after(dve, sum4_made, t - XH + 1)
                        after(dve, sum4_kept, t - XH + 1)
                        dve.tensor_scalar(e_sel[:, h, :], e_bc[:, h, :], dst_f[:, bass.ds(t, 1)], None, ALU.is_equal)
                        dve.tensor_scalar(e_go[:, h, :], e_bc[:, h, :], prev_last[:, bass.ds(t, 1)], None,
                                          ALU.is_equal).then_inc(sel4_done, 1)
                    four = back(at, 4)
                    if inside(four, ET):
                        t = four[0]
                        s, _ = ring(four, XH)
                        prev = (s - 1) % XH
                        dve.wait_ge(sum4_made, t + 1)
                        dve.wait_ge(sel4_done, t + 1)
                        after(dve, u4_made, t - XH + 1)
                        after(dve, sum4_kept, t)
                        for c in range(KC):
                            before = ones[:] if is_int(t) and t == 0 else e_sT[:, prev, c, P - 1:P]
                            last = dve.scalar_tensor_tensor(out=e_sT[:, s, c, :], in0=e_go[:, s, :], scalar=before,
                                                            in1=sT_ps[ring(four, 2)[0]][:, c * P:(c + 1) * P],
                                                            op0=ALU.mult, op1=ALU.add)
                        last.then_inc(sum4_kept, 1)
                    six = back(at, 6)
                    if inside(six, ET):
                        t = six[0]
                        s, used = ring(six, XU)
                        dve.wait_ge(u4_made, t + 1)
                        after(dve, o4_out[s], 16 * used)
                        dve.scalar_tensor_tensor(out=e_o[:, s, :], in0=u_ps[ring(six, 2)[0]], scalar=0.0, in1=e_d[:, s, :],
                                                 op0=ALU.max, op1=ALU.add).then_inc(o4_done, 1)

                rounds(dve, step, ET, XU, 2, 6)

            @block.tensor
            def _(pe):
                def step(at):
                    three = back(at, 3)
                    if inside(three, ET):
                        t = three[0]
                        s, _ = ring(three, XH)
                        pe.wait_ge(hn4_done, t + 1)
                        pe.wait_ge(sel4_done, t + 1)
                        after(pe, sum4_kept, t - 1)
                        for c in range(KC):
                            last = pe.matmul(sT_ps[ring(three, 2)[0]][:, c * P:(c + 1) * P], e_hs[:, s, c * P:(c + 1) * P],
                                             e_sel[:, s, :], start=True, stop=True)
                        last.then_inc(sum4_made, 1)
                        after(pe, hT4_kept, t - 1)
                        for c in range(KC):
                            last = pe.transpose(hT_ps4[ring(three, 2)[0]][:, c * P:(c + 1) * P],
                                                e_hd[:, s, c * P:(c + 1) * P], ident[:])
                        last.then_inc(hT4_made, 1)
                    five = back(at, 5)
                    if inside(five, ET):
                        t = five[0]
                        s, _ = ring(five, XH)
                        pe.wait_ge(hT4_kept, t + 1)
                        pe.wait_ge(sum4_kept, t + 1)
                        after(pe, o4_done, t - 1)
                        parts = [(e_hT, Ws, c) for c in range(KC)] + [(e_sT, Ms, c) for c in range(KC)]
                        for i, (a, w, c) in enumerate(parts):
                            last = pe.matmul(u_ps[ring(five, 2)[0]], a[:, s, c, :], w[:, c, :],
                                             start=i == 0, stop=i == len(parts) - 1)
                        last.then_inc(u4_made, 1)

                rounds(pe, step, ET, XU, 2, 5)


_INS = ['x', 'src', 'dst', 'edge_attr_256', 'L0_gnn_W1', 'L0_gnn_b1', 'L0_gnn_bn_gamma', 'L0_gnn_bn_beta',
        'L0_gnn_W2', 'L0_gnn_b2', 'L0_gnn_ln_w', 'L0_gnn_ln_b', 'L0_gnn_gn_w', 'L0_gnn_gn_b', 'L0_gnn_gn_ms',
        'L1_gnn_W', 'L1_gnn_M']


def kernel(**inputs):
    import numpy as _np
    import concourse.bacc as _bacc
    from concourse import mybir as _mybir
    from concourse.bass_utils import run_bass_kernel_spmd as _run

    nc = _bacc.Bacc("TRN2", target_bir_lowering=False, num_devices=1)
    arrays, args = {}, []
    for name in _INS:
        a = _np.ascontiguousarray(inputs[name])
        arrays[f"in_{name}"] = a
        args.append(nc.dram_tensor(f"in_{name}", a.shape, _mybir.dt.from_np(a.dtype), kind="ExternalInput").ap())
    out = nc.dram_tensor("out", (NODES, CH), _mybir.dt.float32, kind="ExternalOutput").ap()
    gnn_kernel(nc, *args, out)
    r = _run(nc, [arrays], core_ids=[0])
    return r.results[0]["out"]
```

```python
import concourse.bass as bass
from concourse import mybir
from contextlib import ExitStack

FP32 = mybir.dt.float32
FP32R = mybir.dt.float32r
I32 = mybir.dt.int32
ALU = mybir.AluOpType
ACT = mybir.ActivationFunctionType

NODES, CH, HID, EDGES = 50000, 256, 512, 12500
P = 128
T = 3
TILES = NODES // P
GROUPS = TILES // T
REST = NODES - P * TILES
NG = GROUPS + 1
GC = P * T
KC = CH // P
HC = HID // P
EP = P - 1
ET = -(-EDGES // EP)
EREST = EDGES - EP * (ET - 1)
ST = -(-EDGES // P)
SREST = EDGES - P * (ST - 1)
NO_ROW = 1 << 20
EPS = 1e-5



def back(at, lag):
    k, u, r, n = at
    return k - lag, (u - lag) % n, r + (u - lag) // n, n


def ring(at, size):
    k, u, r, n = at
    assert n % size == 0
    return u % size, r * (n // size) + u // size


def is_int(k):
    return isinstance(k, int)


def inside(at, n):
    return not is_int(at[0]) or 0 <= at[0] < n


def after(eng, sem, count):
    if not is_int(count) or count > 0:
        eng.wait_ge(sem, count)


def group_shape(k):
    return (REST, 1) if is_int(k) and k == GROUPS else (P, T)


def columns(k):
    p, n = group_shape(k)
    return p * n


def group_rows(table, k):
    if is_int(k) and k == GROUPS:
        return table[P * TILES:NODES, :].rearrange("(p t) c -> p t c", t=1)
    return table[0:P * TILES, :].rearrange("(p t) c -> p t c", t=TILES)[:, bass.ds(k * T, T), :]


def group_block(table, k):
    return table[k] if is_int(k) else table[bass.ds(k, 1)].rearrange("a p c n -> (a p) c n")


def rounds(eng, step, steps, unroll, peel, flush):
    def one_round(i):
        for u in range(unroll):
            step((i * unroll + u, u, i, unroll))

    full = steps // unroll
    for i in range(peel):
        one_round(i)
    with eng.Fori(peel, full) as i:
        one_round(i)
    for k in range(full * unroll, steps + flush):
        step((k, k % unroll, k // unroll, unroll))


GU, EU = 8, 6


AHEAD = 4


def mixed_rounds(eng, group, edge, group_flush, edge_flush):
    def one_round(i):
        for u in range(GU):
            group(back((i * GU + u, u, i, GU), -AHEAD))
            if u % 4 < 3:
                e = u // 4 * 3 + u % 4
                edge((i * EU + e, e, i, EU))

    full = NG // GU
    for i in range(2):
        one_round(i)
    with eng.Fori(2, full - 1) as i:
        one_round(i)
    one_round(full - 1)
    left = [("g", k) for k in range(full * GU + AHEAD, NG + group_flush)]
    tiles = [("e", t) for t in range(full * EU, ET + edge_flush)]
    for j in range(max(len(left), len(tiles))):
        for kind, k in left[j:j + 1] + tiles[j:j + 1]:
            if kind == "g":
                group((k, k % GU, k // GU, GU))
            else:
                edge((k, k % EU, k // EU, EU))




def gnn_kernel(nc, x, src, dst, edge_attr, W1, b1, bn_gamma, bn_beta, W2, b2, ln_w, ln_b,
               gn_w, gn_b, gn_ms, W, M, out):
    sum_table = nc.dram_tensor("sum_table", (ET * P, CH), FP32, kind="Internal").ap()
    index_table = nc.dram_tensor("index_table", (P, ET, 4), I32, kind="Internal").ap()
    id_table = nc.dram_tensor("id_table", (NODES, 1), I32, kind="Internal").ap()
    dst_table = nc.dram_tensor("dst_table", (ET * P,), I32, kind="Internal").ap()
    sorted_src = nc.dram_tensor("sorted_src", (ST * P, 1), I32, kind="Internal").ap()
    sorted_dst = nc.dram_tensor("sorted_dst", (ST * P, 1), I32, kind="Internal").ap()
    sorted_attr = nc.dram_tensor("sorted_attr", (ST * P, CH), FP32, kind="Internal").ap()
    xh_table = nc.dram_tensor("xh_table", (NODES, CH), FP32, kind="Internal").ap()
    x1_table = nc.dram_tensor("x1_table", (NODES, CH), FP32, kind="Internal").ap()
    yT_table = nc.dram_tensor("yT_table", (NG, P, KC, GC), FP32, kind="Internal").ap()

    with ExitStack() as ctx:
        def sb(name, shape, dt=FP32, scope=ctx):
            return scope.enter_context(nc.sbuf_tensor(name, shape, dt))

        phase = []

        def sem(name):
            phase.append(nc.alloc_semaphore(name))
            return phase[-1]

        def next_phase():
            nc.clear_and_free_semaphores(phase)
            nc.all_engine_barrier()
            phase.clear()

        bank = [ctx.enter_context(nc.psum_tensor(f"bank{i}", [P, 512], FP32)) for i in range(2)]
        pair = [ctx.enter_context(nc.psum_tensor(f"pair{i}", [P, 2, 512], FP32)) for i in range(3)]

        ident = sb("ident", [P, P])
        ones = sb("ones", [P, 1])
        but_first = sb("but_first", [P, 1])
        mean_of = sb("mean_of", [P, P])
        eps = sb("eps", [P, 1])
        W1s = sb("W1s", [P, KC, HID])
        W2s = sb("W2s", [P, HC, CH])
        W1h = sb("W1h", [P, KC, HID], FP32R)
        W1l = sb("W1l", [P, KC, HID], FP32R)
        W2h = sb("W2h", [P, HC, CH], FP32R)
        W2l = sb("W2l", [P, HC, CH], FP32R)
        Ws = sb("Ws", [P, KC, CH])
        Ms = sb("Ms", [P, KC, CH])
        vec_rows = sb("vec_rows", [24, P])
        vec = sb("vec", [P, 24])
        dst_f = sb("dst_f", [P, ET])
        last_of = sb("last_of", [P, ET])
        once_last = sb("once_last", [P, ET])
        carry_key = sb("carry_key", [P, ET])
        own_key = sb("own_key", [P, ET])
        prev_last = sb("prev_last", [P, ET])
        edge_id = sb("edge_id", [P, ET], I32)
        unsorted = sb("unsorted", [1, 1], I32)
        index = sb("index", [P, ET, 4], I32)
        rstd = sb("rstd", [P, NG * T])
        nmr = sb("nmr", [P, NG * T])
        sums = sb("sums", [P, 4])
        mh = sb("mh", [P, 2])
        small = sb("small", [P, 16, 4])
        bnA = sb("bnA", [P, HC])
        bnC = sb("bnC", [P, HC])
        yst = sb("yst", [P, KC, NG, 6])
        ymv = sb("ymv", [P, KC, 2])
        gnP = sb("gnP", [P, KC])
        gnQ = sb("gnQ", [P, KC])

        b1v, gammav, betav = vec[:, 0:4], vec[:, 4:8], vec[:, 8:12]
        b2v, lnwv, lnbv, gnwv, gnbv, gnmsv = (vec[:, 12 + 2 * i:14 + 2 * i] for i in range(6))

        def dst_columns(t):
            return dst_table[bass.ds(t * P, P)].rearrange("(a n) -> a n", a=1).broadcast_to([P, P])

        SC = 8
        CW = ST * P // SC
        loaded = sem("loaded")
        consts = sem("consts")
        pool_consts = sem("pool_consts")
        ident_zero = sem("ident_zero")
        ident_made = sem("ident_made")
        pads = sem("pads")
        ids_clear = sem("ids_clear")
        rows_float = sem("rows_float")
        ends_made = sem("ends_made")
        turned = sem("turned")
        idx_chain = sem("idx_chain")
        idx_loaded = sem("idx_loaded")
        vec_loaded = sem("vec_loaded")
        vec_turned = sem("vec_turned")
        falls_made = sem("falls_made")
        falls_turned = sem("falls_turned")
        flag_made = sem("flag_made")
        pairs_clear = sem("pairs_clear")
        keys_loaded = sem("keys_loaded")
        keys_made = sem("keys_made")
        chunk_loaded = sem("chunk_loaded")
        chunk_made = sem("chunk_made")
        steps_made = sem("steps_made")
        places_made = sem("places_made")
        pairs_out = sem("pairs_out")
        attr_in = sem("attr_in")
        tiles_set = sem("tiles_set")
        attr_out = sem("attr_out")
        rows_again = sem("rows_again")
        dst_out = sem("dst_out")

        x_in = [sem(f"x_in{s}") for s in range(GU)]
        st_done = sem("st_done")
        var_done = sem("var_done")
        sd_done = sem("sd_done")
        rc_done = sem("rc_done")
        nb_done = sem("nb_done")
        h_done = sem("h_done")
        gram_done = sem("gram_done")
        sd_in = [sem(f"sd_in{s}") for s in range(EU)]
        ea_in = [sem(f"ea_in{s}") for s in range(EU)]
        id_out = [sem(f"id_out{s}") for s in range(EU)]
        sum_out = [sem(f"sum_out{s}") for s in range(EU)]
        got_index = sem("got_index")
        index_out = sem("index_out")
        est_done = sem("est_done")
        evar_done = sem("evar_done")
        esd_done = sem("esd_done")
        erc_done = sem("erc_done")
        escaled = sem("escaled")
        enb_done = sem("enb_done")
        ehn_done = sem("ehn_done")
        eadd_done = sem("eadd_done")
        msg_done = sem("msg_done")
        tot_made = sem("tot_made")
        tot_kept = sem("tot_kept")
        carried = sem("carried")
        q_done = sem("q_done")
        corr_done = sem("corr_done")
        ones_made = sem("ones_made")
        index_made = sem("index_made")
        summed = sem("summed")
        split_loaded = sem("split_loaded")
        split_done = sem("split_done")

        G, B = bank[0], bank[1]
        tot_ps = pair[0][:, 0, 0:CH]
        GH = 4

        with ExitStack() as scope, nc.Block() as block:
            zeros = sb("zeros", [P, 512], scope=scope)
            no_rows = sb("no_rows", [P, TILES], I32, scope=scope)
            src_rows = sb("src_rows", [ET, P], I32, scope=scope)
            dst_rows = sb("dst_rows", [ET, P], I32, scope=scope)
            next_rows = sb("next_rows", [ET, P], I32, scope=scope)
            rows_f = sb("rows_f", [ET, 3, P], scope=scope)
            src_f = sb("src_f", [P, ET], scope=scope)
            next_f = sb("next_f", [P, ET], scope=scope)
            er_factor = sb("er_factor", [P, ET, 2], scope=scope)
            msg_sum = sb("msg_sum", [P, CH], scope=scope)
            key_tmp = sb("key_tmp", [P, ET], scope=scope)
            real_edge = sb("real_edge", [P, ET], scope=scope)
            falls = sb("falls", [ET, P + 1], scope=scope)
            any_fall = sb("any_fall", [1, 1], scope=scope)
            place = sb("place", [P, ST, 1], I32, scope=scope)
            edge_pairs = sb("edge_pairs", [P, ST, 2], I32, scope=scope)
            key = sb("key", [P, ST], scope=scope)
            edge_no = sb("edge_no", [P, SC, ST], scope=scope)
            counts = sb("counts", [P, SC, ST], scope=scope)
            chunk_i = sb("chunk_i", [P, CW], I32, scope=scope)
            keys = sb("keys", [P, CW], scope=scope)
            order_i = sb("order_i", [P, CW], I32, scope=scope)
            order_f = sb("order_f", [P, CW], scope=scope)
            apart = sb("apart", [P, CW], scope=scope)
            attr_tile = sb("attr_tile", [P, CH], scope=scope)
            place_tile = sb("place_tile", [P, 1], I32, scope=scope)
            pair_tile = sb("pair_tile", [P, 2], I32, scope=scope)

            xr = sb("xr", [P, GU, T, CH], scope=scope)
            hr = sb("hr", [P, GH, T, CH + 1], scope=scope)
            st6 = sb("st6", [P, GU, T, 6], scope=scope)
            mv = sb("mv", [P, GU, T, 2], scope=scope)
            sd = sb("sd", [P, GU, T], scope=scope)
            e_s = sb("e_s", [P, EU, CH], scope=scope)
            e_d = sb("e_d", [P, EU, CH], scope=scope)
            e_hs = sb("e_hs", [P, EU, CH], scope=scope)
            e_hd = sb("e_hd", [P, EU, CH], scope=scope)
            e_ea = sb("e_ea", [P, EU, CH], scope=scope)
            e_tot = sb("e_tot", [P, EU, CH], scope=scope)
            e_q = sb("e_q", [P, EU, CH], scope=scope)
            e_bc = sb("e_bc", [P, EU, P], I32, scope=scope)
            e_sel = sb("e_sel", [P, EU, P], scope=scope)
            idx = sb("idx", [P, EU, 4], I32, scope=scope)
            est6 = sb("est6", [P, EU, 2, 6], scope=scope)
            emv = sb("emv", [P, EU, 2, 2], scope=scope)
            esd = sb("esd", [P, EU, 2], scope=scope)
            esr = sb("esr", [P, EU, 2], scope=scope)
            er = sb("er", [P, EU, 2], scope=scope)
            enb = sb("enb", [P, EU, 2], scope=scope)

            @block.sync
            def _(sp):
                def group(at):
                    if not inside(at, NG):
                        return
                    k = at[0]
                    s, _ = ring(at, GU)
                    p, n = group_shape(k)
                    after(sp, h_done, k - GU + 1)
                    sp.dma_start(xr[0:p, s, 0:n, :], group_rows(x, k)).then_inc(x_in[s], 16)

                def edge(at):
                    if inside(at, ET):
                        t = at[0]
                        s, _ = ring(at, EU)
                        after(sp, msg_done, t - EU + 1)
                        n = EREST if is_int(t) and t == ET - 1 else EP
                        sp.dma_start(e_ea[1:1 + n, s, :], edge_attr[bass.ds(t * EP, n), :],
                                     cond=unsorted_sp < 1).then_inc(ea_in[s], 16)
                        sp.dma_start(e_ea[1:1 + n, s, :], sorted_attr[bass.ds(t * EP, n), :],
                                     cond=unsorted_sp > 0).then_inc(ea_in[s], 16)
                        sp.dma_start(e_bc[:, s, :], dst_columns(t)).then_inc(ea_in[s], 16)
                    at = back(at, 8)
                    if inside(at, ET):
                        t = at[0]
                        s, _ = ring(at, EU)
                        sp.wait_ge(tot_kept, t + 1)
                        sp.dma_start(sum_table[bass.ds(t * P, P), :], e_tot[:, s, :]).then_inc(sum_out[s], 16)

                group((0, 0, 0, GU))
                sp.wait_ge(pads, 1)
                full = EP * (ET - 1)
                for tile, table, shift in ((src_rows, src, 0), (dst_rows, dst, 0), (next_rows, dst, 1)):
                    sp.dma_start(tile[0:ET - 1, 1:P],
                                 table[shift:shift + full].rearrange("(t p) -> t p", p=EP)).then_inc(idx_loaded, 16)
                    sp.dma_start(tile[ET - 1:ET, 1:1 + EREST - shift],
                                 table[full + shift:EDGES].rearrange("(a p) -> a p", a=1)).then_inc(idx_loaded, 16)
                for k in range(1, AHEAD):
                    group((k, k, 0, GU))
                sp.dma_start(W1s[:], W1.rearrange("(k p) n -> p k n", p=P)).then_inc(split_loaded, 16)
                sp.dma_start(W2s[:], W2.rearrange("(k p) n -> p k n", p=P)).then_inc(split_loaded, 16)
                sp.dma_start(id_table[0:P * TILES, :].rearrange("(p t) a -> p (t a)", t=TILES),
                             no_rows[:]).then_inc(ids_clear, 16)
                sp.dma_start(id_table[P * TILES:NODES, :], no_rows[0:REST, 0:1]).then_inc(ids_clear, 16)
                sp.wait_ge(flag_made, 1)
                unsorted_sp = sp.value_load(unsorted[0:1, 0:1], min_val=0, max_val=1)
                with sp.If(unsorted_sp > 0):
                    sp.wait_ge(pairs_out, 32 * ST)
                    for tile, table, shift in ((src_rows, sorted_src, 0), (dst_rows, sorted_dst, 0),
                                               (next_rows, sorted_dst, 1)):
                        sp.dma_start(tile[0:ET - 1, 1:P], table[shift:shift + full, :].rearrange(
                            "(t p) a -> t (p a)", p=EP)).then_inc(rows_again, 16)
                        sp.dma_start(tile[ET - 1:ET, 1:1 + EREST - shift], table[full + shift:EDGES, :].rearrange(
                            "(a p) b -> a (p b)", a=1)).then_inc(rows_again, 16)
                    sp.wait_ge(rows_again, 96)
                sp.wait_ge(rows_float, 1)
                sp.dma_start(dst_table.rearrange("(t p) -> t p", p=P), dst_rows[:]).then_inc(dst_out, 16)
                sp.wait_ge(dst_out, 16)
                sp.wait_ge(index_made, 1)
                sp.dma_start(index_table[:, :, :], index[:]).then_inc(index_out, 16)
                mixed_rounds(sp, group, edge, 0, 8)
                sp.wait_ge(index_out, 16)
                sp.wait_ge(ids_clear, 32)
                for s in range(EU):
                    sp.wait_ge(sum_out[s], 16 * (-(-(ET - s) // EU)))

            @block.gpsimd
            def _(pool):
                pool.memset(hr[:, :, :, CH:CH + 1], 1.0)
                pool.memset(msg_sum[:], 0.0).then_inc(summed, 1)
                pool.memset(e_ea[0:1, :, :], 0.0)
                pool.memset(but_first[:], 1.0).then_inc(ones_made, 1)

                def gather(at):
                    if not inside(at, ET):
                        return
                    t = at[0]
                    s, used = ring(at, EU)
                    after(pool, ehn_done, t - EU + 1)
                    after(pool, id_out[s], 16 * used)
                    pool.nop(nofuse=True)
                    pool.tensor_copy(idx[:, s, :], index[:, bass.ds(t, 1), :].rearrange("p a b -> p (a b)")
                                     ).then_inc(got_index, 1)
                    pool.wait_ge(got_index, t + 1)
                    pool.nop(nofuse=True)
                    pool.indirect_dma_start(e_s[:, s, :], None, x[:, :],
                                            bass.IndirectOffsetOnAxis(ap=idx[:, s, 0:1], axis=0),
                                            bounds_check=NODES - 1, oob_is_err=False).then_inc(sd_in[s], 16)
                    pool.indirect_dma_start(e_d[:, s, :], None, x[:, :],
                                            bass.IndirectOffsetOnAxis(ap=idx[:, s, 1:2], axis=0),
                                            bounds_check=NODES - 1, oob_is_err=False).then_inc(sd_in[s], 16)
                    pool.indirect_dma_start(id_table[:, :],
                                            bass.IndirectOffsetOnAxis(ap=idx[:, s, 2:3], axis=0),
                                            idx[:, s, 3:4], None,
                                            bounds_check=NODES - 1, oob_is_err=False).then_inc(id_out[s], 16)

                def edge(at):
                    gather(at)
                    late = back(at, 8)
                    if inside(late, ET):
                        t = late[0]
                        s, _ = ring(late, EU)
                        n = 1 + EREST if is_int(t) and t == ET - 1 else P
                        pool.wait_ge(carried, t + 1)
                        pool.wait_ge(summed, t + 1)
                        pool.nop(nofuse=True)
                        pool.tensor_tensor(msg_sum[0:n, :], msg_sum[0:n, :], e_hs[0:n, s, :],
                                           ALU.add).then_inc(summed, 1)

                pool.memset(ident[:], 0.0).then_inc(ident_zero, 1)
                pool.wait_ge(ident_zero, 1)
                pool.affine_select(out=ident[:], in_=ident[:], compare_op=ALU.not_equal, fill=1.0, base=0,
                                   pattern=[[-1, P]], channel_multiplier=1).then_inc(ident_made, 1)
                pool.iota(edge_id[:], [[P, ET]], base=0, channel_multiplier=1).then_inc(pool_consts, 1)
                pool.wait_ge(flag_made, 1)
                with pool.If(pool.value_load(unsorted[0:1, 0:1], min_val=0, max_val=1) > 0):
                    pool.iota(order_i[:], [[1, CW]], base=0, channel_multiplier=0).then_inc(pool_consts, 1)
                    pool.memset(edge_pairs[:], NO_ROW).then_inc(pairs_clear, 1)
                    pool.wait_ge(pairs_clear, 1)
                    full = P * (ST - 1)
                    for j, table in enumerate((src, dst)):
                        pool.dma_start(edge_pairs[:, 0:ST - 1, j], table[0:full].rearrange("(t p) -> p t", p=P),
                                       allow_slow_non_contiguous=True).then_inc(keys_loaded, 16)
                        pool.dma_start(edge_pairs[0:SREST, ST - 1, j:j + 1],
                                       table[full:EDGES].rearrange("(p a) -> p a", a=1),
                                       allow_slow_non_contiguous=True).then_inc(keys_loaded, 16)
                    for c in range(SC):
                        if c > 0:
                            pool.wait_ge(chunk_made, c)
                        n = min(CW, EDGES - c * CW)
                        pool.dma_start(chunk_i[:, 0:n], dst[c * CW:c * CW + n].rearrange(
                            "(a n) -> a n", a=1).broadcast_to([P, n])).then_inc(chunk_loaded, 16)
                    pool.wait_ge(places_made, 1)

                    def move(t, n):
                        if not is_int(t) or t > 0:
                            pool.wait_ge(attr_out, 16 * t)
                            pool.wait_ge(pairs_out, 32 * t)
                        pool.dma_start(attr_tile[0:n, :], edge_attr[bass.ds(t * P, n), :]).then_inc(attr_in, 16)
                        pool.tensor_copy(place_tile[:], place[:, bass.ds(t, 1), 0]).then_inc(tiles_set, 1)
                        pool.tensor_copy(pair_tile[:], edge_pairs[:, bass.ds(t, 1), :].rearrange("p a b -> p (a b)")
                                         ).then_inc(tiles_set, 1)
                        pool.wait_ge(attr_in, 16 * t + 16)
                        pool.wait_ge(tiles_set, 2 * t + 2)
                        pool.nop(nofuse=True)
                        where = bass.IndirectOffsetOnAxis(ap=place_tile[:, 0:1], axis=0)
                        pool.indirect_dma_start(sorted_attr[:, :], where, attr_tile[:], None,
                                                bounds_check=ST * P - 1, oob_is_err=False).then_inc(attr_out, 16)
                        for j, table in enumerate((sorted_src, sorted_dst)):
                            pool.indirect_dma_start(table[:, :], where, pair_tile[:, j:j + 1], None,
                                                    bounds_check=ST * P - 1, oob_is_err=False
                                                    ).then_inc(pairs_out, 16)

                    move(0, P)
                    with pool.Fori(1, ST - 1) as t:
                        move(t, P)
                    move(ST - 1, SREST)
                    pool.wait_ge(attr_out, 16 * ST)
                    pool.wait_ge(pairs_out, 32 * ST)
                pool.wait_ge(index_made, 1)
                pool.wait_ge(ids_clear, 32)
                rounds(pool, edge, ET, EU, 2, 8)
                pool.wait_ge(loaded, 16 * 2)
                for s in range(EU):
                    pool.wait_ge(id_out[s], 16 * (-(-(ET - s) // EU)))

            @block.scalar
            def _(act):
                def group(at):
                    one = back(at, 1)
                    if inside(one, NG):
                        k = one[0]
                        s, _ = ring(one, GU)
                        p, n = group_shape(k)
                        act.wait_ge(var_done, k + 1)
                        after(act, rc_done, k - GU + 1)
                        act.activation(sd[0:p, s, 0:n], mv[0:p, s, 0:n, 1], ACT.Sqrt,
                                       bias=eps[0:p, :]).then_inc(sd_done, 1)
                    two = back(at, 2)
                    if inside(two, NG):
                        k = two[0]
                        s, _ = ring(two, GU)
                        h, _ = ring(two, GH)
                        p, n = group_shape(k)
                        act.wait_ge(nb_done, k + 1)
                        after(act, gram_done, k - GH + 1)
                        for j in range(n):
                            last = act.activation(hr[0:p, h, j, 0:CH], xr[0:p, s, j, :], ACT.Relu,
                                                  bias=nmr[0:p, bass.ds(k * T + j, 1)],
                                                  scale=rstd[0:p, bass.ds(k * T + j, 1)])
                        last.then_inc(h_done, 1)

                def carry(at, first):
                    if not inside(at, ET):
                        return
                    t = at[0]
                    s, _ = ring(at, EU)
                    act.wait_ge(msg_done, t + 1)
                    source = zeros[0:1, 0:CH] if first else tot_ps[0:1, :]
                    act.activation(e_hs[0:1, s, :], source, ACT.Copy).then_inc(carried, 1)

                def edge(at):
                    if is_int(at[0]) and at[0] == 4:
                        carry((0, 0, 0, EU), True)
                    five = back(at, 5)
                    if inside(five, ET):
                        t = five[0]
                        s, used = ring(five, EU)
                        act.wait_ge(tot_made, t + 1)
                        after(act, q_done, t - EU + 1)
                        after(act, corr_done, t - EU + 1)
                        after(act, sum_out[s], 16 * used)
                        act.activation(e_tot[:, s, :], tot_ps, ACT.Copy).then_inc(tot_kept, 1)
                        carry(back(five, -1), False)
                    one = back(at, 1)
                    if inside(one, ET):
                        t = one[0]
                        s, _ = ring(one, EU)
                        act.wait_ge(evar_done, t + 1)
                        after(act, erc_done, t - EU + 1)
                        act.activation(esd[:, s, :], emv[:, s, :, 1], ACT.Sqrt,
                                       bias=eps[:]).then_inc(esd_done, 1)
                    two = back(at, 2)
                    if inside(two, ET):
                        t = two[0]
                        s, _ = ring(two, EU)
                        act.wait_ge(enb_done, t + 1)
                        after(act, tot_made, t - EU + 1)
                        after(act, summed, t - EU + 2)
                        after(act, q_done, t - EU + 1)
                        act.activation(e_hs[:, s, :], e_s[:, s, :], ACT.Relu,
                                       bias=enb[:, s, 0:1], scale=er[:, s, 0:1])
                        act.activation(e_hd[:, s, :], e_d[:, s, :], ACT.Relu,
                                       bias=enb[:, s, 1:2], scale=er[:, s, 1:2]).then_inc(ehn_done, 1)

                act.wait_ge(consts, 1)
                for k in range(AHEAD):
                    group((k, k, 0, GU))
                row = 0
                for v, n in ((b1, 4), (bn_gamma, 4), (bn_beta, 4), (b2, 2), (ln_w, 2), (ln_b, 2),
                             (gn_w, 2), (gn_b, 2), (gn_ms, 2)):
                    act.dma_start(vec_rows[row:row + n, :], v.rearrange("(t p) -> t p", p=P)).then_inc(vec_loaded, 16)
                    row += n
                act.dma_start(Ws[:], W.rearrange("(k p) n -> p k n", p=P)).then_inc(loaded, 16)
                act.dma_start(Ms[:], M.rearrange("(k p) n -> p k n", p=P)).then_inc(loaded, 16)
                mixed_rounds(act, group, edge, 2, 5)

            @block.vector
            def _(dve):
                def group(at):
                    if inside(at, NG):
                        k = at[0]
                        s, used = ring(at, GU)
                        p, n = group_shape(k)
                        dve.wait_ge(x_in[s], 16 * (used + 1))
                        for j in range(n):
                            last = dve.bn_stats(st6[0:p, s, j, :], xr[0:p, s, j, :])
                        last.then_inc(st_done, 1)
                    two = back(at, 2)
                    if inside(two, NG):
                        k = two[0]
                        s, _ = ring(two, GU)
                        p, n = group_shape(k)
                        dve.wait_ge(sd_done, k + 1)
                        dve.reciprocal(rstd[0:p, bass.ds(k * T, n)], sd[0:p, s, 0:n]).then_inc(rc_done, 1)
                    one = back(at, 1)
                    if inside(one, NG):
                        k = one[0]
                        s, _ = ring(one, GU)
                        p, n = group_shape(k)
                        after(dve, sd_done, k - GU + 1)
                        dve.wait_ge(st_done, k + 1)
                        dve.nop(nofuse=True)
                        for j in range(n):
                            last = dve.bn_aggr(mv[0:p, s, j, :], st6[0:p, s, j, :])
                        last.then_inc(var_done, 1)
                    if inside(two, NG):
                        k = two[0]
                        s, _ = ring(two, GU)
                        p, n = group_shape(k)
                        dve.wait_ge(rc_done, k + 1)
                        dve.scalar_tensor_tensor(out=nmr[0:p, bass.ds(k * T, n)], in0=mv[0:p, s, 0:n, 0],
                                                 scalar=-1.0, in1=rstd[0:p, bass.ds(k * T, n)],
                                                 op0=ALU.mult, op1=ALU.mult).then_inc(nb_done, 1)

                def edge(at):
                    if inside(at, ET):
                        t = at[0]
                        s, used = ring(at, EU)
                        dve.wait_ge(sd_in[s], 32 * (used + 1))
                        dve.bn_stats(est6[:, s, 0, :], e_s[:, s, :])
                        dve.bn_stats(est6[:, s, 1, :], e_d[:, s, :]).then_inc(est_done, 1)
                    two = back(at, 2)
                    if inside(two, ET):
                        t = two[0]
                        s, _ = ring(two, EU)
                        dve.wait_ge(esd_done, t + 1)
                        after(dve, ehn_done, t - EU + 1)
                        dve.reciprocal(esr[:, s, :], esd[:, s, :]).then_inc(erc_done, 1)
                    one = back(at, 1)
                    if inside(one, ET):
                        t = one[0]
                        s, _ = ring(one, EU)
                        dve.wait_ge(est_done, t + 1)
                        dve.nop(nofuse=True)
                        dve.bn_aggr(emv[:, s, 0, :], est6[:, s, 0, :])
                        dve.bn_aggr(emv[:, s, 1, :], est6[:, s, 1, :]).then_inc(evar_done, 1)
                    if inside(two, ET):
                        t = two[0]
                        s, _ = ring(two, EU)
                        dve.wait_ge(erc_done, t + 1)
                        dve.tensor_tensor(er[:, s, :], esr[:, s, :],
                                          er_factor[:, bass.ds(t, 1), :].rearrange("p a b -> p (a b)"),
                                          ALU.mult).then_inc(escaled, 1)
                    three = back(at, 3)
                    if inside(three, ET):
                        t = three[0]
                        s, used = ring(three, EU)
                        dve.wait_ge(ehn_done, t + 1)
                        dve.wait_ge(ea_in[s], 48 * (used + 1))
                        dve.tensor_tensor(e_hs[:, s, :], e_hs[:, s, :], e_ea[:, s, :],
                                          ALU.add).then_inc(eadd_done, 1)
                    if inside(two, ET):
                        t = two[0]
                        s, _ = ring(two, EU)
                        dve.wait_ge(escaled, t + 1)
                        dve.scalar_tensor_tensor(out=enb[:, s, :], in0=emv[:, s, :, 0], scalar=-1.0,
                                                 in1=er[:, s, :], op0=ALU.mult,
                                                 op1=ALU.mult).then_inc(enb_done, 1)
                    if inside(three, ET):
                        t = three[0]
                        s, used = ring(three, EU)
                        after(dve, tot_made, t - EU + 1)
                        dve.tensor_scalar(e_sel[:, s, :], e_bc[:, s, :], carry_key[:, bass.ds(t, 1)], None,
                                          ALU.is_equal)
                        dve.wait_ge(eadd_done, t + 1)
                        dve.tensor_scalar(e_hs[:, s, :], e_hs[:, s, :], 0.0, None,
                                          ALU.max).then_inc(msg_done, 1)
                    six = back(at, 6)
                    if inside(six, ET):
                        t = six[0]
                        s, _ = ring(six, EU)
                        dve.wait_ge(tot_kept, t + 1)
                        after(dve, corr_done, t - EU + 1)
                        dve.scalar_tensor_tensor(out=e_q[:, s, :], in0=e_tot[:, s, :],
                                                 scalar=once_last[:, bass.ds(t, 1)], in1=e_hd[:, s, :], op0=ALU.mult,
                                                 op1=ALU.add).then_inc(q_done, 1)

                dve.memset(src_rows[:], 0)
                dve.memset(dst_rows[:], NO_ROW)
                dve.memset(next_rows[:], NO_ROW + 1)
                dve.memset(no_rows[:], NO_ROW).then_inc(pads, 1)
                dve.memset(ones[:], 1.0)
                dve.memset(mean_of[:], 1.0 / CH)
                dve.memset(eps[:], EPS)
                dve.memset(zeros[:], 0.0).then_inc(consts, 1)
                group((0, 0, 0, GU))
                dve.wait_ge(ones_made, 1)
                dve.memset(but_first[0:1, :], 0.0)
                dve.wait_ge(idx_loaded, 16 * 6)
                dve.tensor_tensor(falls[:, 1:P], dst_rows[:, 1:P], next_rows[:, 1:P],
                                  ALU.is_gt).then_inc(falls_made, 1)
                dve.wait_ge(falls_made, 1)
                dve.reduce_max(falls[:, P:P + 1], falls[:, 1:P], axis=mybir.AxisListType.X).then_inc(falls_made, 1)
                group((1, 1, 0, GU))
                dve.wait_ge(falls_turned, 1)
                dve.reduce_max(any_fall[:], pair[1][0:1, 1, 0:ET], axis=mybir.AxisListType.X).then_inc(falls_made, 1)
                dve.wait_ge(falls_made, 3)
                dve.tensor_copy(unsorted[:], any_fall[:]).then_inc(flag_made, 1)
                dve.wait_ge(flag_made, 1)
                with dve.If(dve.value_load(unsorted[0:1, 0:1], min_val=0, max_val=1) > 0):
                    dve.wait_ge(keys_loaded, 64)
                    dve.tensor_scalar(key[:], edge_pairs[:, :, 1], 16384.0, None, ALU.mult)
                    dve.wait_ge(pool_consts, 2)
                    for c in range(SC):
                        dve.tensor_scalar(edge_no[:, c, :], edge_id[:, 0:ST], float(c * CW), None, ALU.subtract)
                    dve.tensor_copy(order_f[:], order_i[:]).then_inc(keys_made, 1)
                    dve.wait_ge(keys_made, 1)
                    for c in range(SC):
                        n = min(CW, EDGES - c * CW)
                        if n < CW:
                            dve.memset(keys[:, n:CW], NO_ROW * 16384.0)
                        dve.wait_ge(chunk_loaded, 16 * (c + 1))
                        dve.tensor_scalar(keys[:, 0:n], chunk_i[:, 0:n], 16384.0, None, ALU.mult).then_inc(chunk_made, 1)
                        dve.wait_ge(chunk_made, c + 1)
                        with dve.Fori(0, ST) as t:
                            done = c * ST * 3 + t * 3
                            dve.scalar_tensor_tensor(out=apart[:], in0=keys[:], scalar=key[:, bass.ds(t, 1)],
                                                     in1=order_f[:], op0=ALU.subtract,
                                                     op1=ALU.add).then_inc(steps_made, 1)
                            dve.wait_ge(steps_made, done + 1)
                            dve.tensor_scalar(apart[:], apart[:], edge_no[:, c, bass.ds(t, 1)], None,
                                              ALU.is_lt).then_inc(steps_made, 1)
                            dve.wait_ge(steps_made, done + 2)
                            dve.reduce_sum(counts[:, c, bass.ds(t, 1)], apart[:],
                                           axis=mybir.AxisListType.X).then_inc(steps_made, 1)
                            dve.wait_ge(steps_made, done + 3)
                    for c in range(1, SC):
                        dve.tensor_tensor(counts[:, 0, :], counts[:, 0, :], counts[:, c, :],
                                          ALU.add).then_inc(steps_made, 1)
                        dve.wait_ge(steps_made, SC * ST * 3 + c)
                    dve.tensor_copy(place[:, :, 0], counts[:, 0, :]).then_inc(places_made, 1)
                    dve.wait_ge(rows_again, 96)
                dve.tensor_copy(dst_rows[:, 0:1], dst_rows[:, P - 1:P])
                dve.tensor_copy(next_rows[:, 0:1], dst_rows[:, P - 1:P]).then_inc(ends_made, 1)
                dve.wait_ge(ends_made, 1)
                dve.tensor_copy(rows_f[:, 0, :], src_rows[:])
                dve.tensor_copy(rows_f[:, 1, :], dst_rows[:])
                dve.tensor_copy(rows_f[:, 2, :], next_rows[:]).then_inc(rows_float, 1)
                group((2, 2, 0, GU))
                dve.wait_ge(turned, 1)
                dve.tensor_copy(src_f[:], pair[1][:, 0, 0:ET])
                dve.tensor_copy(dst_f[:], pair[1][:, 0, P:P + ET])
                dve.tensor_copy(next_f[:], pair[1][:, 0, 2 * P:2 * P + ET])
                dve.memset(prev_last[:, 0:1], -1.0)
                dve.tensor_copy(prev_last[:, 1:ET], pair[1][:, 1, 0:ET - 1]).then_inc(idx_chain, 1)
                dve.wait_ge(idx_chain, 1)
                dve.tensor_copy(index[:, :, 0], src_f[:])
                dve.tensor_copy(index[:, :, 1], dst_f[:])
                dve.tensor_tensor(last_of[:], dst_f[:], next_f[:], ALU.not_equal).then_inc(idx_chain, 1)
                dve.tensor_copy(carry_key[:], dst_f[:])
                dve.tensor_copy(own_key[:], dst_f[:]).then_inc(idx_chain, 1)
                dve.wait_ge(idx_chain, 3)
                dve.tensor_copy(carry_key[0:1, :], prev_last[0:1, :])
                dve.memset(own_key[0:1, :], -1.0)
                dve.tensor_scalar(key_tmp[:], last_of[:], -float(NO_ROW), float(NO_ROW), ALU.mult,
                                  ALU.add).then_inc(idx_chain, 1)
                dve.wait_ge(idx_chain, 4)
                dve.tensor_tensor(key_tmp[:], key_tmp[:], dst_f[:], ALU.add).then_inc(idx_chain, 1)
                dve.wait_ge(idx_chain, 5)
                dve.tensor_copy(index[:, :, 2], key_tmp[:])
                dve.wait_ge(pool_consts, 1)
                dve.tensor_copy(index[:, :, 3], edge_id[:])
                dve.tensor_scalar(real_edge[:], dst_f[:], float(NODES), 2.0, ALU.is_lt, ALU.mult).then_inc(idx_chain, 1)
                dve.wait_ge(idx_chain, 6)
                dve.memset(er_factor[:, :, 0], 1.0)
                dve.tensor_tensor(er_factor[:, :, 1], last_of[:], real_edge[:], ALU.mult)
                dve.scalar_tensor_tensor(out=once_last[:], in0=last_of[:], scalar=0.5, in1=real_edge[:],
                                         op0=ALU.mult, op1=ALU.mult).then_inc(index_made, 1)
                group((3, 3, 0, GU))
                dve.wait_ge(split_loaded, 32)
                dve.tensor_copy(W1h[:], W1s[:])
                dve.tensor_copy(W2h[:], W2s[:]).then_inc(split_done, 1)
                dve.wait_ge(split_done, 1)
                dve.tensor_tensor(W1l[:], W1s[:], W1h[:].bitcast(FP32), ALU.subtract)
                dve.tensor_tensor(W2l[:], W2s[:], W2h[:].bitcast(FP32), ALU.subtract)
                dve.wait_ge(index_made, 1)
                mixed_rounds(dve, group, edge, 2, 6)
                dve.wait_ge(vec_turned, 1)
                dve.tensor_copy(vec[:], pair[2][:, 0, 0:24])

            @block.tensor
            def _(pe):
                pe.wait_ge(consts, 1)
                pe.matmul(G[:, :], zeros[:, 0:P], zeros[:, 0:512], start=True, stop=False, skip_group_check=True)
                pe.matmul(B[:, :], zeros[:, 0:P], zeros[:, 0:512], start=True, stop=False, skip_group_check=True)
                pe.wait_ge(ones_made, 1)

                def add(o, a, b):
                    return pe.matmul(o, a, b, start=False, stop=False, skip_group_check=True)

                def group(at):
                    at = back(at, 3)
                    if not inside(at, NG):
                        return
                    k = at[0]
                    s, _ = ring(at, GH)
                    p, n = group_shape(k)
                    pe.wait_ge(h_done, k + 1)
                    for j in range(n):
                        h = hr[0:p, s, j, :]
                        add(G[:, 0:CH + 1], h[:, 0:P], h)
                        last = add(G[:, CH + 1:CH + 2 + P], h[:, P:CH], h[:, P:CH + 1])
                    last.then_inc(gram_done, 1)

                def edge(at):
                    seven = back(at, 7)
                    if inside(seven, ET):
                        t = seven[0]
                        s, _ = ring(seven, EU)
                        pe.wait_ge(q_done, t + 1)
                        a = e_tot[:, s, :]
                        add(B[:, 0:CH], e_q[:, s, 0:P], a)
                        add(B[:, CH:2 * CH], e_q[:, s, P:CH], a).then_inc(corr_done, 1)
                    four = back(at, 4)
                    if inside(four, ET):
                        t = four[0]
                        s, _ = ring(four, EU)
                        pe.wait_ge(carried, t + 1)
                        pe.matmul(tot_ps, e_sel[:, s, :], e_hs[:, s, :], start=True,
                                  stop=True).then_inc(tot_made, 1)

                pe.wait_ge(ident_made, 1)
                pe.wait_ge(falls_made, 2)
                pe.transpose(pair[1][0:1, 1, 0:ET], falls[:, P:P + 1], ident[0:ET, 0:ET]).then_inc(falls_turned, 1)
                pe.wait_ge(falls_made, 3)
                pe.wait_ge(rows_float, 1)
                for j in range(3):
                    pe.transpose(pair[1][:, 0, j * P:j * P + ET], rows_f[:, j, :], ident[0:ET, 0:ET])
                pe.matmul(pair[1][:, 1, 0:ET], rows_f[:, 1, P - 1:P].broadcast_to([ET, P]), ident[0:ET, 0:ET],
                          start=True, stop=True).then_inc(turned, 1)
                for k in range(AHEAD):
                    group((k, k, 0, GU))
                mixed_rounds(pe, group, edge, 3, 7)
                pe.wait_ge(vec_loaded, 16 * 9)
                pe.transpose(pair[2][:, 0, 0:24], vec_rows[:], ident[0:24, 0:24]).then_inc(vec_turned, 1)
                pe.wait_ge(summed, ET + 1)
                add(G[:, CH + 2 + P:CH + 3 + P], msg_sum[:, 0:P], but_first[:])
                add(G[:, CH + 3 + P:CH + 4 + P], msg_sum[:, P:CH], but_first[:])
                pe.matmul(G[:, :], zeros[:, 0:P], zeros[:, 0:512], start=False, stop=True, skip_group_check=True)
                pe.matmul(B[:, :], zeros[:, 0:P], zeros[:, 0:512], start=False, stop=True, skip_group_check=True)

        next_phase()
        c0 = sem("c0")
        d_copied = sem("d_copied")
        d_made = sem("d_made")
        t_made = sem("t_made")
        wt_made = sem("wt_made")
        q_made = sem("q_made")
        var_made = sem("var_made")
        sdev_made = sem("sdev_made")
        N = float(NODES)
        bn_ready = sem("bn_ready")
        NU = 4
        KEPT = 2 * NU
        NPEEL = KEPT // NU + 2
        kept = ctx.enter_context(ExitStack())
        xh_kept = sb("xh_kept", [P, KEPT, T, CH], scope=kept)
        y_stays = sb("y_stays", [P, KEPT, KC, GC], scope=kept)

        def stays(k):
            return is_int(k) and k < KEPT

        x2_in = [sem(f"x2_in{s}") for s in range(NU)]
        a2_in = [sem(f"a2_in{s}") for s in range(NU)]
        y_out = [sem(f"y_out{s}") for s in range(NU)]
        xh_out = [sem(f"xh_out{s}") for s in range(NU)]
        ids_in = sem("ids_in")
        a2_clear = sem("a2_clear")
        h2n_done = sem("h2n_done")
        xh2_done = sem("xh2_done")
        h2_done = sem("h2_done")
        t2_made = sem("t2_made")
        th_kept = sem("th_kept")
        tl_kept = sem("tl_kept")
        z_made = sem("z_made")
        r_kept = sem("r_kept")
        rh_kept = sem("rh_kept")
        rl_kept = sem("rl_kept")
        y_made = sem("y_made")
        y_kept = sem("y_kept")
        yst_done = sem("yst_done")
        hT_ps, z_ps, y_ps = pair[0], [pair[1][:, 0, :], pair[1][:, 1, :], pair[2][:, 0, :], pair[2][:, 1, :]], bank

        with ExitStack() as scope, nc.Block() as block:
            Dm = sb("Dm", [P, 512], scope=scope)
            WT = sb("WT", [P, KC, HID], scope=scope)
            xr = sb("xr2", [P, NU, T, CH], scope=scope)
            ar = sb("ar2", [P, NU, T, CH], scope=scope)
            hr = sb("hr2", [P, NU, T, CH], scope=scope)
            tH = sb("tH", [P, 2, KC, GC], FP32R, scope=scope)
            tL = sb("tL", [P, 2, KC, GC], FP32R, scope=scope)
            r32 = sb("r32", [P, HC, GC], scope=scope)
            rH = sb("rH", [P, HC, GC], FP32R, scope=scope)
            rL = sb("rL", [P, HC, GC], FP32R, scope=scope)
            yr = sb("yr", [P, NU, KC, GC], scope=scope)
            ids = sb("ids", [P, TILES], I32, scope=scope)
            ids_rest = sb("ids_rest", [P, 1], I32, scope=scope)
            idx = sb("idx2", [P, NU, T], I32, scope=scope)

            def xbuf(k, s):
                return xh_kept[:, k, :, :] if stays(k) else xr[:, s, :, :]

            def ybuf(k, s):
                return y_stays[:, k, :, :] if stays(k) else yr[:, s, :, :]

            @block.sync
            def _(sp):
                sp.dma_start(ids[:], id_table[0:P * TILES, :].rearrange("(p t) a -> p (t a)", t=TILES)
                             ).then_inc(ids_in, 16)
                sp.dma_start(ids_rest[0:REST, :], id_table[P * TILES:NODES, :]).then_inc(ids_in, 16)

                def step(at):
                    if inside(at, NG):
                        k = at[0]
                        s, used = ring(at, NU)
                        p, n = group_shape(k)
                        if is_int(k) and k < KEPT + NU:
                            after(sp, h2n_done, k - NU + 1)
                        else:
                            after(sp, xh_out[s], 16 * (used - KEPT // NU))
                        sp.dma_start(xbuf(k, s)[0:p, 0:n, :], group_rows(x, k)).then_inc(x2_in[s], 16)
                    three = back(at, 3)
                    if inside(three, NG) and not stays(three[0]):
                        k = three[0]
                        s, _ = ring(three, NU)
                        p, n = group_shape(k)
                        sp.wait_ge(xh2_done, k + 1)
                        sp.dma_start(group_rows(xh_table, k), xr[0:p, s, 0:n, :]).then_inc(xh_out[s], 16)
                    six = back(at, 6)
                    if inside(six, NG) and not stays(six[0]):
                        k = six[0]
                        s, _ = ring(six, NU)
                        n = columns(k)
                        sp.wait_ge(y_kept, k + 1)
                        sp.dma_start(group_block(yT_table, k)[:, :, 0:n], yr[:, s, :, 0:n]).then_inc(y_out[s], 16)

                rounds(sp, step, NG, NU, NPEEL, 6)
                for s in range(NU):
                    stored = -(-(NG - s) // NU) - KEPT // NU
                    sp.wait_ge(y_out[s], 16 * stored)
                    sp.wait_ge(xh_out[s], 16 * stored)

            @block.gpsimd
            def _(pool):
                pool.wait_ge(ids_in, 32)

                def step(at):
                    if inside(at, NG):
                        k = at[0]
                        s, _ = ring(at, NU)
                        p, n = group_shape(k)
                        after(pool, t2_made, k - NU + 1)
                        pool.nop(nofuse=True)
                        pool.memset(ar[0:p, s, 0:n, :], 0.0)
                        where = ids_rest[0:p, :] if is_int(k) and k == GROUPS else ids[:, bass.ds(k * T, T)]
                        pool.tensor_copy(idx[0:p, s, 0:n], where).then_inc(a2_clear, 1)
                        pool.wait_ge(a2_clear, k + 1)
                        pool.nop(nofuse=True)
                        for j in range(n):
                            pool.indirect_dma_start(ar[0:p, s, j, :], None, sum_table[:, :],
                                                    bass.IndirectOffsetOnAxis(ap=idx[0:p, s, j:j + 1], axis=0),
                                                    bounds_check=ET * P - 1, oob_is_err=False
                                                    ).then_inc(a2_in[s], 16)
                    two = back(at, 2)
                    if inside(two, NG):
                        k = two[0]
                        s, _ = ring(two, NU)
                        p, n = group_shape(k)
                        pool.wait_ge(h2n_done, k + 1)
                        pool.nop(nofuse=True)
                        pool.tensor_tensor(xbuf(k, s)[0:p, 0:n, :], xbuf(k, s)[0:p, 0:n, :], hr[0:p, s, 0:n, :],
                                           ALU.add).then_inc(xh2_done, 1)

                rounds(pool, step, NG, NU, NPEEL, 2)

            @block.scalar
            def _(act):
                def norm(at):
                    if not inside(at, NG):
                        return []
                    k = at[0]
                    s, used = ring(at, NU)
                    p, n = group_shape(k)

                    def piece(j):
                        if j == 0:
                            act.wait_ge(x2_in[s], 16 * (used + 1))
                            after(act, h2_done, k - NU + 1)
                            after(act, xh2_done, k - NU + 1)
                        one = act.activation(hr[0:p, s, j, :], xbuf(k, s)[0:p, j, :], ACT.Relu,
                                             bias=nmr[0:p, bass.ds(k * T + j, 1)],
                                             scale=rstd[0:p, bass.ds(k * T + j, 1)])
                        if j == n - 1:
                            one.then_inc(h2n_done, 1)

                    return [lambda j=j: piece(j) for j in range(n)]

                def hidden(at, m):
                    if not inside(at, NG):
                        return
                    k = at[0]
                    n = columns(k)
                    after(act, rl_kept, (k - 1) * HC + m + 1)
                    act.wait_ge(z_made, k * HC + m + 1)
                    act.activation(r32[:, m, 0:n], z_ps[m][:, 0:n], ACT.Relu, bias=bnC[:, m:m + 1],
                                   scale=bnA[:, m:m + 1]).then_inc(r_kept, 1)

                def keep_y(at):
                    if not inside(at, NG):
                        return
                    k = at[0]
                    s, used = ring(at, NU)
                    n = columns(k)
                    act.wait_ge(y_made, k + 1)
                    if not stays(k):
                        after(act, yst_done, k - NU + 1)
                        after(act, y_out[s], 16 * (used - KEPT // NU))
                    for c in range(KC):
                        last = act.activation(ybuf(k, s)[:, c, 0:n], y_ps[c][:, 0:n], ACT.Identity,
                                              bias=b2v[:, c:c + 1])
                    last.then_inc(y_kept, 1)

                def keep_high(at):
                    if not inside(at, NG):
                        return
                    k = at[0]
                    s, _ = ring(at, 2)
                    n = columns(k)
                    act.wait_ge(t2_made, k + 1)
                    after(act, z_made, (k - 1) * HC)
                    for c in range(KC):
                        last = act.activation(tH[:, s, c, 0:n], hT_ps[:, c, 0:n], ACT.Copy)
                    last.then_inc(th_kept, 1)

                def step(at):
                    keep_y(back(at, 1))
                    pieces = norm(back(at, -2))
                    for m in range(HC):
                        hidden(at, m)
                        for piece in pieces[m:m + 1]:
                            piece()
                    keep_high(back(at, -1))

                act.activation(Dm[:], B[:, :], ACT.Copy, scale=1.0 / N)
                act.activation(sums[:, 0:1], G[:, CH:CH + 1], ACT.Copy, scale=1.0 / N)
                act.activation(sums[:, 1:4], G[:, CH + 1 + P:CH + 4 + P], ACT.Copy,
                               scale=1.0 / N).then_inc(d_copied, 1)
                for k in range(2):
                    for piece in norm((k, k, 0, NU)):
                        piece()
                act.wait_ge(var_made, 1)
                act.activation(small[:, 4, :], small[:, 3, :], ACT.Sqrt, bias=eps[:]).then_inc(sdev_made, 1)
                keep_high((0, 0, 0, NU))
                act.wait_ge(bn_ready, 1)
                rounds(act, step, NG, NU, NPEEL, 1)

            @block.vector
            def _(dve):
                def add(at):
                    if not inside(at, NG):
                        return
                    k = at[0]
                    s, used = ring(at, NU)
                    p, n = group_shape(k)
                    dve.wait_ge(h2n_done, k + 1)
                    dve.wait_ge(a2_in[s], 16 * T * used + 16 * n)
                    dve.tensor_tensor(ar[0:p, s, 0:n, :], ar[0:p, s, 0:n, :], hr[0:p, s, 0:n, :],
                                      ALU.add).then_inc(h2_done, 1)

                def keep_low(at):
                    if not inside(at, NG):
                        return
                    k = at[0]
                    s, _ = ring(at, 2)
                    n = columns(k)
                    dve.wait_ge(th_kept, k + 1)
                    for c in range(KC):
                        last = dve.tensor_tensor(tL[:, s, c, 0:n], hT_ps[:, c, 0:n],
                                                 tH[:, s, c, 0:n].bitcast(FP32), ALU.subtract)
                    last.then_inc(tl_kept, 1)

                def stats(at, c):
                    if not inside(at, NG):
                        return
                    k = at[0]
                    s, _ = ring(at, NU)
                    n = columns(k)
                    if c == 0:
                        dve.wait_ge(y_kept, k + 1)
                    one = dve.bn_stats(yst[:, c, bass.ds(k, 1), :].rearrange("p a b -> p (a b)"),
                                       ybuf(k, s)[:, c, 0:n])
                    if c == KC - 1:
                        one.then_inc(yst_done, 1)

                def high(at, m):
                    if not inside(at, NG):
                        return
                    k = at[0]
                    n = columns(k)
                    dve.wait_ge(r_kept, k * HC + m + 1)
                    after(dve, y_made, k)
                    dve.tensor_copy(rH[:, m, 0:n], r32[:, m, 0:n]).then_inc(rh_kept, 1)

                def low(at, m):
                    if not inside(at, NG):
                        return
                    k = at[0]
                    n = columns(k)
                    dve.wait_ge(rh_kept, k * HC + m + 1)
                    dve.tensor_tensor(rL[:, m, 0:n], r32[:, m, 0:n], rH[:, m, 0:n].bitcast(FP32),
                                      ALU.subtract).then_inc(rl_kept, 1)

                def step(at):
                    high(at, 0)
                    stats(back(at, 1), 0)
                    low(at, 0)
                    high(at, 1)
                    stats(back(at, 1), 1)
                    low(at, 1)
                    high(at, 2)
                    add(back(at, -2))
                    low(at, 2)
                    high(at, 3)
                    low(at, 3)
                    keep_low(back(at, -1))

                count = [0]

                def link(ins):
                    count[0] += 1
                    ins.then_inc(c0, 1)
                    dve.wait_ge(c0, count[0])

                dve.wait_ge(d_copied, 1)
                for o, g, f in ((0, 0, 1.0), (P, P, 2.0), (3 * P, CH + 1, 1.0)):
                    dve.scalar_tensor_tensor(out=Dm[:, o:o + P], in0=G[:, g:g + P], scalar=f / N,
                                             in1=Dm[:, o:o + P], op0=ALU.mult, op1=ALU.add)
                for j in range(2):
                    last = dve.scalar_tensor_tensor(out=mh[:, j:j + 1], in0=sums[:, 2 + j:3 + j], scalar=1.0,
                                                    in1=sums[:, j:j + 1], op0=ALU.mult, op1=ALU.add)
                last.then_inc(d_made, 1)
                dve.wait_ge(t_made, 1)
                for j in range(KC):
                    last = dve.tensor_tensor(WT[:, j, :], W1s[:, j, :], pair[0][:, j, :], ALU.mult)
                last.then_inc(wt_made, 1)
                dve.wait_ge(q_made, 1)
                link(dve.tensor_copy(small[:, 0:2, :], pair[1][:, 0, 0:8].rearrange("p (a b) -> p a b", a=2)))
                zq, zm = small[:, 0, :], small[:, 1, :]
                link(dve.tensor_tensor(small[:, 2, :], zm, zm, ALU.mult))
                link(dve.tensor_tensor(small[:, 2, :], zq, small[:, 2, :], ALU.subtract))
                dve.tensor_scalar(small[:, 3, :], small[:, 2, :], 0.0, None, ALU.max).then_inc(var_made, 1)
                link(dve.tensor_tensor(small[:, 5, :], zm, b1v, ALU.add))
                link(dve.tensor_tensor(small[:, 5, :], b1v, small[:, 5, :], ALU.subtract))
                dve.wait_ge(sdev_made, 1)
                link(dve.reciprocal(small[:, 6, :], small[:, 4, :]))
                link(dve.tensor_tensor(bnA[:], small[:, 6, :], gammav, ALU.mult))
                link(dve.tensor_tensor(small[:, 7, :], bnA[:], small[:, 5, :], ALU.mult))
                dve.tensor_tensor(bnC[:], small[:, 7, :], betav, ALU.add).then_inc(bn_ready, 1)
                add((0, 0, 0, NU))
                add((1, 1, 0, NU))
                keep_low((0, 0, 0, NU))
                rounds(dve, step, NG, NU, NPEEL, 1)

            @block.tensor
            def _(pe):
                def turn(at):
                    if not inside(at, NG):
                        return
                    k = at[0]
                    s, _ = ring(at, NU)
                    p, n = group_shape(k)
                    pe.wait_ge(h2_done, k + 1)
                    after(pe, tl_kept, k)
                    for c in range(KC):
                        for j in range(n):
                            last = pe.transpose(hT_ps[:, c, j * P:j * P + p],
                                                ar[0:p, s, j, c * P:(c + 1) * P], ident[0:p, 0:p])
                    last.then_inc(t2_made, 1)

                def step(at):
                    if not inside(at, NG):
                        return
                    k = at[0]
                    s, _ = ring(at, 2)
                    n = columns(k)
                    pe.wait_ge(tl_kept, k + 1)
                    for m in range(HC):
                        after(pe, r_kept, (k - 1) * HC + m + 1)
                        parts = [(w, t, c) for w, t in ((W1h, tH), (W1l, tH), (W1h, tL)) for c in range(KC)]
                        for i, (w, t, c) in enumerate(parts):
                            last = pe.matmul(z_ps[m][:, 0:n], w[:, c, m * P:(m + 1) * P], t[:, s, c, 0:n],
                                             start=i == 0, stop=i == len(parts) - 1)
                        last.then_inc(z_made, 1)
                    turn(back(at, -1))
                    after(pe, y_kept, k)
                    for ms in ((0,), (1,), (2,), (3,)):
                        pe.wait_ge(rl_kept, k * HC + ms[-1] + 1)
                        for m in ms:
                            for c in range(KC):
                                for i, (w, t) in enumerate(((W2h, rH), (W2l, rH), (W2h, rL))):
                                    last = pe.matmul(y_ps[c][:, 0:n], w[:, m, c * P:(c + 1) * P], t[:, m, 0:n],
                                                     start=m == 0 and i == 0, stop=m == HC - 1 and i == 2)
                    last.then_inc(y_made, 1)

                pe.wait_ge(d_made, 1)
                for o in range(KC):
                    for l in range(KC):
                        last = pe.matmul(pair[0][:, o, :], Dm[:, l * CH + o * P:l * CH + o * P + P],
                                         W1s[:, l, :], start=l == 0, stop=l == KC - 1)
                last.then_inc(t_made, 1)
                pe.wait_ge(wt_made, 1)
                for m in range(HC):
                    for l in range(KC):
                        pe.matmul(pair[1][:, 0, m:m + 1], WT[:, l, m * P:m * P + P], ones[:],
                                  start=l == 0, stop=l == KC - 1)
                for m in range(HC):
                    for l in range(KC):
                        last = pe.matmul(pair[1][:, 0, 4 + m:5 + m], W1s[:, l, m * P:m * P + P], mh[:, l:l + 1],
                                         start=l == 0, stop=l == KC - 1)
                last.then_inc(q_made, 1)
                turn((0, 0, 0, NU))
                pe.wait_ge(var_made, 1)
                rounds(pe, step, NG, NU, 1, 0)

        next_phase()
        c1 = sem("c1")
        mu_in = sem("mu_in")
        mu_made = sem("mu_made")
        vg_in = sem("vg_in")
        vg_made = sem("vg_made")
        v1_made = sem("v1_made")
        s1_made = sem("s1_made")
        v2_made = sem("v2_made")
        s2_made = sem("s2_made")
        gn_ready = sem("gn_ready")
        mu, vg = pair[0][:, 0, 0:1], pair[0][:, 1, 0:1]
        row = [small[:, i, 0:2] for i in range(16)]
        RU = 8
        RL = 8
        OL = 4
        LEAD = 6

        def skipped(s):
            return -(-(KEPT - s) // RL)

        xh_in = [sem(f"xh_in{s}") for s in range(RL)]
        y_in = [sem(f"y_in{s}") for s in range(RL)]
        x1_out = [sem(f"x1_out{s}") for s in range(RU)]
        o_out = [sem(f"o_out{s}") for s in range(OL)]
        g_done = sem("g_done")
        gt_made = sem("gt_made")
        x1_done = sem("x1_done")
        st3_done = sem("st3_done")
        var3_done = sem("var3_done")
        sd3_done = sem("sd3_done")
        rc3_done = sem("rc3_done")
        nb3_done = sem("nb3_done")
        h1_done = sem("h1_done")
        h1t_made = sem("h1t_made")
        h1t_kept = sem("h1t_kept")
        u_made = sem("u_made")
        o_done = sem("o_done")

        def tile_of(pr, j):
            return pr[:, j // 2, (j % 2) * CH:(j % 2 + 1) * CH]

        def flat(t, p, n):
            return t.rearrange("p a b -> p (a b)")[0:p, 0:n * CH]

        with ExitStack() as scope, nc.Block() as block:
            xhr = sb("xhr", [P, RL, T, CH], scope=scope)
            yr = sb("yr3", [P, RL, KC, GC], scope=scope)
            gr = sb("gr", [P, 2, KC, GC], scope=scope)
            x1r = sb("x1r", [P, RU, T, CH], scope=scope)
            h1r = sb("h1r", [P, 2, T, CH], scope=scope)
            h1T = sb("h1T", [P, 2, KC, GC], scope=scope)
            orr = sb("orr", [P, OL, T, CH], scope=scope)
            st6 = sb("st6_3", [P, RU, T, 6], scope=scope)
            mv = sb("mv_3", [P, RU, T, 2], scope=scope)
            sd = sb("sd_3", [P, RU, T], scope=scope)
            r3 = sb("r3", [P, RU, T], scope=scope)
            n3 = sb("n3", [P, RU, T], scope=scope)

            @block.sync
            def _(sp):
                def load(at):
                    if not inside(at, NG):
                        return
                    k = at[0]
                    s, _ = ring(at, RL)
                    p, n = group_shape(k)
                    c = columns(k)
                    if not (is_int(k) and k < KEPT + RL):
                        sp.wait_ge(x1_done, k - RL + 1)
                        sp.wait_ge(g_done, k - RL + 1)
                    sp.dma_start(xhr[0:p, s, 0:n, :], group_rows(xh_table, k)).then_inc(xh_in[s], 16)
                    sp.dma_start(yr[:, s, :, 0:c], group_block(yT_table, k)[:, :, 0:c]).then_inc(y_in[s], 16)

                def step(at):
                    two = back(at, 2)
                    if inside(two, NG):
                        k = two[0]
                        s, _ = ring(two, RU)
                        p, n = group_shape(k)
                        sp.wait_ge(x1_done, k + 1)
                        sp.dma_start(group_rows(x1_table, k), x1r[0:p, s, 0:n, :]).then_inc(x1_out[s], 16)
                    ahead = back(at, -LEAD)
                    if not is_int(ahead[0]) or ahead[0] >= KEPT + RL:
                        load(ahead)
                    late = back(at, 8)
                    if inside(late, NG):
                        k = late[0]
                        s, _ = ring(late, OL)
                        p, n = group_shape(k)
                        sp.wait_ge(o_done, k + 1)
                        sp.dma_start(group_rows(out, k), orr[0:p, s, 0:n, :]).then_inc(o_out[s], 16)

                for k in range(KEPT, KEPT + RL):
                    load((k, k % RU, k // RU, RU))
                rounds(sp, step, NG - LEAD, RU, 2, LEAD + 8)
                for s in range(RU):
                    sp.wait_ge(x1_out[s], 16 * (-(-(NG - s) // RU)))
                for s in range(OL):
                    sp.wait_ge(o_out[s], 16 * (-(-(NG - s) // OL)))

            @block.scalar
            def _(act):
                def step(at):
                    if inside(at, NG):
                        k = at[0]
                        s, used = ring(at, RL)
                        f, _ = ring(at, 2)
                        m = columns(k)
                        if not stays(k):
                            act.wait_ge(y_in[s], 16 * (used + 1 - skipped(s)))
                        y = y_stays[:, k, :, :] if stays(k) else yr[:, s, :, :]
                        after(act, gt_made, k - 1)
                        for c in range(KC):
                            last = act.activation(gr[:, f, c, 0:m], y[:, c, 0:m], ACT.Relu,
                                                  bias=gnQ[:, c:c + 1], scale=gnP[:, c:c + 1])
                        last.then_inc(g_done, 1)
                    three = back(at, 3)
                    if inside(three, NG):
                        k = three[0]
                        s, _ = ring(three, RU)
                        p, n = group_shape(k)
                        act.wait_ge(var3_done, k + 1)
                        after(act, rc3_done, k - RU + 1)
                        act.activation(sd[0:p, s, 0:n], mv[0:p, s, 0:n, 1], ACT.Sqrt,
                                       bias=eps[0:p, :]).then_inc(sd3_done, 1)
                    six = back(at, 6)
                    if inside(six, NG):
                        k = six[0]
                        s, _ = ring(six, 2)
                        n = columns(k)
                        act.wait_ge(h1t_made, k + 1)
                        after(act, u_made, k - 1)
                        for c in range(KC):
                            last = act.activation(h1T[:, s, c, 0:n], pair[1][:, c, 0:n], ACT.Copy)
                        last.then_inc(h1t_kept, 1)
                    four = back(at, 4)
                    if inside(four, NG):
                        k = four[0]
                        s, _ = ring(four, RU)
                        f, _ = ring(four, 2)
                        p, n = group_shape(k)
                        act.wait_ge(nb3_done, k + 1)
                        after(act, h1t_made, k - 1)
                        for j in range(n):
                            last = act.activation(h1r[0:p, f, j, :], x1r[0:p, s, j, :], ACT.Relu,
                                                  bias=n3[0:p, s, j:j + 1], scale=r3[0:p, s, j:j + 1])
                        last.then_inc(h1_done, 1)

                act.wait_ge(v1_made, 1)
                act.activation(row[4], row[3], ACT.Sqrt, bias=eps[:]).then_inc(s1_made, 1)
                act.wait_ge(v2_made, 1)
                act.activation(row[10], row[9], ACT.Sqrt, bias=eps[:]).then_inc(s2_made, 1)
                act.wait_ge(gn_ready, 1)
                rounds(act, step, NG, RU, 2, 6)

            @block.vector
            def _(dve):
                def step(at):
                    one = back(at, 1)
                    if inside(one, NG):
                        k = one[0]
                        s, used = ring(one, RL)
                        b, bused = ring(one, RU)
                        p, n = group_shape(k)
                        if not stays(k):
                            dve.wait_ge(xh_in[s], 16 * (used + 1 - skipped(s)))
                        xh = xh_kept[:, k, :, :] if stays(k) else xhr[:, s, :, :]
                        dve.wait_ge(gt_made, k + 1)
                        after(dve, x1_out[b], 16 * bused)
                        after(dve, h1_done, k - RU + 1)
                        after(dve, o_done, k - RU + 1)
                        dve.tensor_tensor(flat(x1r[:, b, :, :], p, n), flat(xh, p, n),
                                          flat(pair[0][:, :, :], p, n), ALU.add).then_inc(x1_done, 1)
                    four = back(at, 4)
                    if inside(four, NG):
                        k = four[0]
                        s, _ = ring(four, RU)
                        p, n = group_shape(k)
                        dve.wait_ge(sd3_done, k + 1)
                        after(dve, h1_done, k - RU + 1)
                        dve.reciprocal(r3[0:p, s, 0:n], sd[0:p, s, 0:n]).then_inc(rc3_done, 1)
                    two = back(at, 2)
                    if inside(two, NG):
                        k = two[0]
                        s, _ = ring(two, RU)
                        p, n = group_shape(k)
                        dve.wait_ge(x1_done, k + 1)
                        for j in range(n):
                            last = dve.bn_stats(st6[0:p, s, j, :], x1r[0:p, s, j, :])
                        last.then_inc(st3_done, 1)
                    if inside(four, NG):
                        k = four[0]
                        s, _ = ring(four, RU)
                        p, n = group_shape(k)
                        dve.wait_ge(rc3_done, k + 1)
                        dve.scalar_tensor_tensor(out=n3[0:p, s, 0:n], in0=mv[0:p, s, 0:n, 0], scalar=-1.0,
                                                 in1=r3[0:p, s, 0:n], op0=ALU.mult,
                                                 op1=ALU.mult).then_inc(nb3_done, 1)
                    three = back(at, 3)
                    if inside(three, NG):
                        k = three[0]
                        s, _ = ring(three, RU)
                        p, n = group_shape(k)
                        after(dve, sd3_done, k - RU + 1)
                        dve.wait_ge(st3_done, k + 1)
                        dve.nop(nofuse=True)
                        for j in range(n):
                            last = dve.bn_aggr(mv[0:p, s, j, :], st6[0:p, s, j, :])
                        last.then_inc(var3_done, 1)
                    seven = back(at, 7)
                    if inside(seven, NG):
                        k = seven[0]
                        s, used = ring(seven, OL)
                        b, _ = ring(seven, RU)
                        p, n = group_shape(k)
                        dve.wait_ge(u_made, k + 1)
                        after(dve, o_out[s], 16 * used)
                        dve.scalar_tensor_tensor(out=flat(orr[:, s, :, :], p, n), in0=flat(pair[2][:, :, :], p, n),
                                                 scalar=0.0, in1=flat(x1r[:, b, :, :], p, n),
                                                 op0=ALU.max, op1=ALU.add).then_inc(o_done, 1)

                count = [0]

                def link(ins):
                    count[0] += 1
                    ins.then_inc(c1, 1)
                    dve.wait_ge(c1, count[0])

                for c in range(KC):
                    last = dve.bn_aggr(ymv[:, c, :], yst[:, c, :, :].rearrange("p a b -> p (a b)"))
                last.then_inc(mu_in, 1)
                dve.wait_ge(mu_in, 1)
                E, V = ymv[:, :, 0], ymv[:, :, 1]
                dve.wait_ge(mu_made, 1)
                link(dve.tensor_copy(row[15], mu.broadcast_to([P, 2])))
                link(dve.tensor_tensor(row[0], E, row[15], ALU.subtract))
                link(dve.tensor_tensor(row[1], row[0], row[0], ALU.mult))
                dve.tensor_tensor(row[2], row[1], V, ALU.add).then_inc(vg_in, 1)
                dve.wait_ge(vg_made, 1)
                dve.tensor_copy(row[3], vg.broadcast_to([P, 2])).then_inc(v1_made, 1)
                dve.wait_ge(s1_made, 1)
                link(dve.reciprocal(row[5], row[4]))
                link(dve.tensor_tensor(row[5], row[5], lnwv, ALU.mult))
                link(dve.tensor_tensor(row[6], row[0], row[5], ALU.mult))
                link(dve.tensor_tensor(row[6], row[6], lnbv, ALU.add))
                link(dve.tensor_tensor(row[7], row[6], gnmsv, ALU.mult))
                link(dve.tensor_tensor(row[8], row[6], row[7], ALU.subtract))
                link(dve.tensor_tensor(row[8], row[8], row[8], ALU.mult))
                link(dve.tensor_tensor(row[9], row[5], row[5], ALU.mult))
                link(dve.tensor_tensor(row[9], row[9], V, ALU.mult))
                dve.tensor_tensor(row[9], row[9], row[8], ALU.add).then_inc(v2_made, 1)
                link(dve.tensor_tensor(row[11], row[15], row[5], ALU.mult))
                link(dve.tensor_tensor(row[11], lnbv, row[11], ALU.subtract))
                link(dve.tensor_tensor(row[11], row[11], row[7], ALU.subtract))
                dve.wait_ge(s2_made, 1)
                link(dve.reciprocal(row[12], row[10]))
                link(dve.tensor_tensor(row[12], row[12], gnwv, ALU.mult))
                link(dve.tensor_tensor(gnP[:], row[5], row[12], ALU.mult))
                link(dve.tensor_tensor(row[11], row[11], row[12], ALU.mult))
                dve.tensor_tensor(gnQ[:], row[11], gnbv, ALU.add).then_inc(gn_ready, 1)
                rounds(dve, step, NG, RU, 2, 7)

            @block.tensor
            def _(pe):
                def step(at):
                    if inside(at, NG):
                        k = at[0]
                        s, _ = ring(at, 2)
                        p, n = group_shape(k)
                        pe.wait_ge(g_done, k + 1)
                        after(pe, x1_done, k)
                        for j in range(n):
                            for c in range(KC):
                                last = pe.transpose(tile_of(pair[0], j)[0:p, c * P:(c + 1) * P],
                                                    gr[:, s, c, j * P:j * P + p], ident[:])
                        last.then_inc(gt_made, 1)
                    five = back(at, 5)
                    if inside(five, NG):
                        k = five[0]
                        s, _ = ring(five, 2)
                        p, n = group_shape(k)
                        pe.wait_ge(h1_done, k + 1)
                        after(pe, h1t_kept, k)
                        for c in range(KC):
                            for j in range(n):
                                last = pe.transpose(pair[1][:, c, j * P:j * P + p],
                                                    h1r[0:p, s, j, c * P:(c + 1) * P], ident[0:p, 0:p])
                        last.then_inc(h1t_made, 1)
                    six = back(at, 6)
                    if inside(six, NG):
                        k = six[0]
                        s, _ = ring(six, 2)
                        p, n = group_shape(k)
                        pe.wait_ge(h1t_kept, k + 1)
                        after(pe, o_done, k)
                        for j in range(n):
                            for c in range(KC):
                                last = pe.matmul(tile_of(pair[2], j)[0:p, :], h1T[:, s, c, j * P:j * P + p],
                                                 Ws[:, c, :], start=c == 0, stop=c == KC - 1)
                        last.then_inc(u_made, 1)

                pe.wait_ge(mu_in, 1)
                for c in range(KC):
                    last = pe.matmul(mu, mean_of[:], ymv[:, c, 0:1], start=c == 0, stop=c == KC - 1)
                last.then_inc(mu_made, 1)
                pe.wait_ge(vg_in, 1)
                for c in range(KC):
                    last = pe.matmul(vg, mean_of[:], row[2][:, c:c + 1], start=c == 0, stop=c == KC - 1)
                last.then_inc(vg_made, 1)
                pe.wait_ge(v1_made, 1)
                rounds(pe, step, NG, RU, 2, 6)
        kept.close()

        next_phase()
        XU = 14
        XH = 7
        idx4_in = [sem(f"idx4_in{s}") for s in range(XU)]
        sd4_in = [sem(f"sd4_in{s}") for s in range(XU)]
        bc4_in = [sem(f"bc4_in{s}") for s in range(XH)]
        o4_out = [sem(f"o4_out{s}") for s in range(XU)]
        st4_done = sem("st4_done")
        var4_done = sem("var4_done")
        sd4_done = sem("sd4_done")
        rc4_done = sem("rc4_done")
        nb4_done = sem("nb4_done")
        hn4_done = sem("hn4_done")
        sel4_done = sem("sel4_done")
        sum4_made = sem("sum4_made")
        sum4_kept = sem("sum4_kept")
        hT4_made = sem("hT4_made")
        hT4_kept = sem("hT4_kept")
        u4_made = sem("u4_made")
        o4_done = sem("o4_done")
        with ExitStack() as scope, nc.Block() as block:
            e_s = sb("f_s", [P, XU, CH], scope=scope)
            e_d = sb("f_d", [P, XU, CH], scope=scope)
            e_o = sb("f_o", [P, XU, CH], scope=scope)
            e_hs = sb("f_hs", [P, XH, CH], scope=scope)
            e_hd = sb("f_hd", [P, XH, CH], scope=scope)
            e_hT = sb("f_hT", [P, XH, KC, P], scope=scope)
            e_sT = sb("f_sT", [P, XH, KC, P], scope=scope)
            e_bc = sb("f_bc", [P, XH, P], I32, scope=scope)
            e_sel = sb("f_sel", [P, XH, P], scope=scope)
            e_go = sb("f_go", [P, XH, P], scope=scope)
            idx = sb("f_idx", [P, XU, 4], I32, scope=scope)
            est6 = sb("f_st6", [P, XU, 2, 6], scope=scope)
            emv = sb("f_mv", [P, XU, 2, 2], scope=scope)
            esd = sb("f_sd", [P, XU, 2], scope=scope)
            er = sb("f_r", [P, XU, 2], scope=scope)
            enb = sb("f_nb", [P, XU, 2], scope=scope)
            sT_ps = [bank[i][:, 0:CH] for i in range(2)]
            hT_ps4 = [pair[1][:, i, 0:CH] for i in range(2)]
            u_ps = [pair[0][:, i, 0:CH] for i in range(2)]

            @block.sync
            def _(sp):
                def load_index(at):
                    if not inside(at, ET):
                        return
                    s, used = ring(at, XU)
                    after(sp, o4_out[s], 16 * used)
                    sp.dma_start(idx[:, s, :], index_table[:, bass.ds(at[0], 1), :].rearrange("p a b -> p (a b)")
                                 ).then_inc(idx4_in[s], 16)

                def step(at):
                    load_index(back(at, -2))
                    t = at[0]
                    s, _ = ring(at, XH)
                    after(sp, sel4_done, t - XH + 1)
                    sp.dma_start(e_bc[:, s, :], dst_columns(t)).then_inc(bc4_in[s], 16)

                load_index((0, 0, 0, XU))
                load_index((1, 1, 0, XU))
                rounds(sp, step, ET - 2, XU, 2, 2)

            @block.gpsimd
            def _(pool):
                def step(at):
                    if inside(at, ET):
                        t = at[0]
                        s, used = ring(at, XU)
                        after(pool, hn4_done, t - XU + 1)
                        after(pool, o4_done, t - XU + 1)
                        pool.wait_ge(idx4_in[s], 16 * (used + 1))
                        pool.nop(nofuse=True)
                        for tile, j in ((e_s, 0), (e_d, 1)):
                            pool.indirect_dma_start(tile[:, s, :], None, x1_table[:, :],
                                                    bass.IndirectOffsetOnAxis(ap=idx[:, s, j:j + 1], axis=0),
                                                    bounds_check=NODES - 1, oob_is_err=False
                                                    ).then_inc(sd4_in[s], 16)
                    late = back(at, 9)
                    if inside(late, ET):
                        t = late[0]
                        s, used = ring(late, XU)
                        pool.wait_ge(o4_done, t + 1)
                        pool.nop(nofuse=True)
                        pool.indirect_dma_start(out[:, :], bass.IndirectOffsetOnAxis(ap=idx[:, s, 2:3], axis=0),
                                                e_o[:, s, :], None, bounds_check=NODES - 1,
                                                oob_is_err=False).then_inc(o4_out[s], 16)

                rounds(pool, step, ET, XU, 2, 9)
                for s in range(XU):
                    pool.wait_ge(o4_out[s], 16 * (-(-(ET - s) // XU)))

            @block.scalar
            def _(act):
                def step(at):
                    one = back(at, 1)
                    if inside(one, ET):
                        t = one[0]
                        s, _ = ring(one, XU)
                        act.wait_ge(var4_done, t + 1)
                        after(act, rc4_done, t - XU + 1)
                        act.activation(esd[:, s, :], emv[:, s, :, 1], ACT.Sqrt, bias=eps[:]).then_inc(sd4_done, 1)
                    four = back(at, 4)
                    if inside(four, ET):
                        t = four[0]
                        s, _ = ring(four, XH)
                        act.wait_ge(hT4_made, t + 1)
                        after(act, u4_made, t - XH + 1)
                        act.activation(e_hT[:, s, :, :].rearrange("p a b -> p (a b)"), hT_ps4[ring(four, 2)[0]],
                                       ACT.Copy).then_inc(hT4_kept, 1)
                    two = back(at, 2)
                    if inside(two, ET):
                        t = two[0]
                        s, _ = ring(two, XU)
                        h, _ = ring(two, XH)
                        act.wait_ge(nb4_done, t + 1)
                        after(act, sum4_made, t - XH + 1)
                        after(act, hT4_made, t - XH + 1)
                        act.activation(e_hs[:, h, :], e_s[:, s, :], ACT.Relu,
                                       bias=enb[:, s, 0:1], scale=er[:, s, 0:1])
                        act.activation(e_hd[:, h, :], e_d[:, s, :], ACT.Relu,
                                       bias=enb[:, s, 1:2], scale=er[:, s, 1:2]).then_inc(hn4_done, 1)

                rounds(act, step, ET, XU, 2, 4)

            @block.vector
            def _(dve):
                def step(at):
                    if inside(at, ET):
                        t = at[0]
                        s, used = ring(at, XU)
                        dve.wait_ge(sd4_in[s], 32 * (used + 1))
                        dve.bn_stats(est6[:, s, 0, :], e_s[:, s, :])
                        dve.bn_stats(est6[:, s, 1, :], e_d[:, s, :]).then_inc(st4_done, 1)
                    two = back(at, 2)
                    if inside(two, ET):
                        t = two[0]
                        s, _ = ring(two, XU)
                        dve.wait_ge(sd4_done, t + 1)
                        after(dve, hn4_done, t - XU + 1)
                        dve.reciprocal(er[:, s, :], esd[:, s, :]).then_inc(rc4_done, 1)
                    one = back(at, 1)
                    if inside(one, ET):
                        t = one[0]
                        s, _ = ring(one, XU)
                        after(dve, sd4_done, t - XU + 1)
                        dve.wait_ge(st4_done, t + 1)
                        dve.nop(nofuse=True)
                        dve.bn_aggr(emv[:, s, 0, :], est6[:, s, 0, :])
                        dve.bn_aggr(emv[:, s, 1, :], est6[:, s, 1, :]).then_inc(var4_done, 1)
                    if inside(two, ET):
                        t = two[0]
                        s, _ = ring(two, XU)
                        h, hused = ring(two, XH)
                        dve.wait_ge(rc4_done, t + 1)
                        dve.scalar_tensor_tensor(out=enb[:, s, :], in0=emv[:, s, :, 0], scalar=-1.0,
                                                 in1=er[:, s, :], op0=ALU.mult,
                                                 op1=ALU.mult).then_inc(nb4_done, 1)
                        dve.wait_ge(bc4_in[h], 16 * (hused + 1))
                        after(dve, sum4_made, t - XH + 1)
                        after(dve, sum4_kept, t - XH + 1)
                        dve.tensor_scalar(e_sel[:, h, :], e_bc[:, h, :], own_key[:, bass.ds(t, 1)], None, ALU.is_equal)
                        dve.tensor_scalar(e_go[:, h, :], e_bc[:, h, :], prev_last[:, bass.ds(t, 1)], None,
                                          ALU.is_equal).then_inc(sel4_done, 1)
                    four = back(at, 4)
                    if inside(four, ET):
                        t = four[0]
                        s, _ = ring(four, XH)
                        prev = (s - 1) % XH
                        dve.wait_ge(sum4_made, t + 1)
                        dve.wait_ge(sel4_done, t + 1)
                        after(dve, u4_made, t - XH + 1)
                        after(dve, sum4_kept, t)
                        for c in range(KC):
                            before = ones[:] if is_int(t) and t == 0 else e_sT[:, prev, c, 0:1]
                            last = dve.scalar_tensor_tensor(out=e_sT[:, s, c, :], in0=e_go[:, s, :], scalar=before,
                                                            in1=sT_ps[ring(four, 2)[0]][:, c * P:(c + 1) * P],
                                                            op0=ALU.mult, op1=ALU.add)
                        last.then_inc(sum4_kept, 1)
                    six = back(at, 6)
                    if inside(six, ET):
                        t = six[0]
                        s, used = ring(six, XU)
                        dve.wait_ge(u4_made, t + 1)
                        after(dve, o4_out[s], 16 * used)
                        dve.scalar_tensor_tensor(out=e_o[:, s, :], in0=u_ps[ring(six, 2)[0]], scalar=0.0, in1=e_d[:, s, :],
                                                 op0=ALU.max, op1=ALU.add).then_inc(o4_done, 1)

                rounds(dve, step, ET, XU, 2, 6)

            @block.tensor
            def _(pe):
                def step(at):
                    three = back(at, 3)
                    if inside(three, ET):
                        t = three[0]
                        s, _ = ring(three, XH)
                        pe.wait_ge(hn4_done, t + 1)
                        pe.wait_ge(sel4_done, t + 1)
                        after(pe, sum4_kept, t - 1)
                        for c in range(KC):
                            last = pe.matmul(sT_ps[ring(three, 2)[0]][:, c * P:(c + 1) * P], e_hs[:, s, c * P:(c + 1) * P],
                                             e_sel[:, s, :], start=True, stop=True)
                        last.then_inc(sum4_made, 1)
                        after(pe, hT4_kept, t - 1)
                        for c in range(KC):
                            last = pe.transpose(hT_ps4[ring(three, 2)[0]][:, c * P:(c + 1) * P],
                                                e_hd[:, s, c * P:(c + 1) * P], ident[:])
                        last.then_inc(hT4_made, 1)
                    five = back(at, 5)
                    if inside(five, ET):
                        t = five[0]
                        s, _ = ring(five, XH)
                        pe.wait_ge(hT4_kept, t + 1)
                        pe.wait_ge(sum4_kept, t + 1)
                        after(pe, o4_done, t - 1)
                        parts = [(e_hT, Ws, c) for c in range(KC)] + [(e_sT, Ms, c) for c in range(KC)]
                        for i, (a, w, c) in enumerate(parts):
                            last = pe.matmul(u_ps[ring(five, 2)[0]], a[:, s, c, :], w[:, c, :],
                                             start=i == 0, stop=i == len(parts) - 1)
                        last.then_inc(u4_made, 1)

                rounds(pe, step, ET, XU, 2, 5)


_INS = ['x', 'src', 'dst', 'edge_attr_256', 'L0_gnn_W1', 'L0_gnn_b1', 'L0_gnn_bn_gamma', 'L0_gnn_bn_beta',
        'L0_gnn_W2', 'L0_gnn_b2', 'L0_gnn_ln_w', 'L0_gnn_ln_b', 'L0_gnn_gn_w', 'L0_gnn_gn_b', 'L0_gnn_gn_ms',
        'L1_gnn_W', 'L1_gnn_M']


def kernel(**inputs):
    import numpy as _np
    import concourse.bacc as _bacc
    from concourse import mybir as _mybir
    from concourse.bass_utils import run_bass_kernel_spmd as _run

    nc = _bacc.Bacc("TRN2", target_bir_lowering=False, num_devices=1)
    arrays, args = {}, []
    for name in _INS:
        a = _np.ascontiguousarray(inputs[name])
        arrays[f"in_{name}"] = a
        args.append(nc.dram_tensor(f"in_{name}", a.shape, _mybir.dt.from_np(a.dtype), kind="ExternalInput").ap())
    out = nc.dram_tensor("out", (NODES, CH), _mybir.dt.float32, kind="ExternalOutput").ap()
    gnn_kernel(nc, *args, out)
    r = _run(nc, [arrays], core_ids=[0])
    return r.results[0]["out"]
```
